# Optimizing a Trainium2 kernel written in Bass

```python
import numpy as np
import jax
import jax.numpy as jnp

def _softmax(x, axis=-1):
    return jax.nn.softmax(x, axis=axis)

def _gelu(x):
    return jax.nn.gelu(x, approximate=True)

def _silu(x):
    return jax.nn.silu(x)

def _sigmoid(x):
    return jax.nn.sigmoid(x)

def _layernorm(x, axis=-1, eps=1e-05):
    m = jnp.mean(x, axis=axis, keepdims=True)
    v = jnp.var(x, axis=axis, keepdims=True)
    return (x - m) / jnp.sqrt(v + eps)

def _scatter_add(tgt, idx, src, axis=0):
    return tgt.at[idx].add(src)

def _segment_sum(src, seg, n):
    return jax.ops.segment_sum(src, seg, n)
kernel_name = 'mk_decoder_postln_d2_seqx_r8_1349e8'

def setup_inputs(seed: int=0):
    np.random.seed(seed)
    _w = jnp.asarray

    def _rec_inputs():
        import jax
        import jax.numpy as jnp
        _rk = jax.random.key(seed)
        x = 4.136e-05 + 0.9999 * jax.random.normal(jax.random.fold_in(_rk, 1), (4, 256, 256), jnp.float32)
        _lenS = 256 - jax.random.randint(jax.random.fold_in(_rk, 7), (4,), 0, max(1, 256 // 4) + 1, jnp.int32)
        _lenS2 = 256 - jax.random.randint(jax.random.fold_in(_rk, 8), (4,), 0, max(1, 256 // 4) + 1, jnp.int32)
        _ctx_1024P = jax.random.normal(jax.random.fold_in(_rk, 11), (4, 16, 128), jnp.float32)
        _ctx_1024c = jax.random.dirichlet(jax.random.fold_in(_rk, 511), 0.3 * jnp.ones((16,), jnp.float32), (4, 256))
        _ctx_1024t = jnp.einsum('bsk,bkd->bsd', _ctx_1024c, _ctx_1024P)
        _ctx_1024t = _ctx_1024t * jax.lax.rsqrt(jnp.mean(jnp.square(_ctx_1024t)) + 1e-12) * 0.953939
        ctx_1024 = -0.000292821 + 1.00034 * (_ctx_1024t + 0.3 * jax.random.normal(jax.random.fold_in(_rk, 611), (4, 256, 128), jnp.float32))
        _validS = jnp.arange(256)[None, :] < _lenS[:, None]
        _validS2 = jnp.arange(256)[None, :] < _lenS2[:, None]
        _causal = jnp.tril(jnp.ones((256, 256), dtype=bool))
        mask_BxS2_bf1 = jnp.ones((4, 256), dtype=bool)
        return (x, ctx_1024, mask_BxS2_bf1)
    x, ctx_1024, mask_BxS2_bf1 = _rec_inputs()

    def _L0_attn_setup():
        import jax, jax.numpy as jnp
        import numpy as np
        L, N, E, H = (256, 2, 256, 16)
        DH = E // H
        SCALE = DH ** (-0.5)
        key = jax.random.key(seed)
        k1, k2, k3 = jax.random.split(key, 3)
        x = jax.random.normal(k1, (L, N, E), dtype=jnp.float32)
        weight_qkv = jax.random.normal(k2, (3 * E, E), dtype=jnp.float32) * 0.02
        weight_out = jax.random.normal(k3, (E, E), dtype=jnp.float32) * 0.02
        return {'x': x, 'weight_qkv': weight_qkv, 'weight_out': weight_out}
    _L0_attn_all = _L0_attn_setup()
    _L0_attn_in = {k: v for k, v in _L0_attn_all.items() if k in ('weight_qkv', 'weight_out')}
    del _L0_attn_all

    def _L0_xattn_setup():
        import jax, jax.numpy as jnp
        import numpy as np
        import math
        B, L, DM = (2, 256, 128)
        DS, DC, EXP = (16, 4, 2)
        DI = EXP * DM
        DR = math.ceil(DM / 16)
        DT_MIN, DT_MAX, DT_FLOOR = (0.001, 0.1, 0.0001)

        def _ssm_forward(hidden_states, z, in_proj_w, conv_w, conv_b, x_proj_w, dt_proj_w, dt_proj_b, A_log, D):
            b = hidden_states.shape[0]
            x = jnp.einsum('ed,bld->bel', in_proj_w, hidden_states)
            xp = jnp.pad(x, ((0, 0), (0, 0), (DC - 1, 0)))
            xc = jax.lax.conv_general_dilated(xp, conv_w[:, None, :], window_strides=(1,), padding='VALID', dimension_numbers=('NCH', 'OIH', 'NCH'), feature_group_count=DI)
            u = jax.nn.silu(xc + conv_b[None, :, None])
            x_dbl = jnp.einsum('ke,bel->bkl', x_proj_w, u)
            dt_lo = x_dbl[:, :DR]
            Bm = x_dbl[:, DR:DR + DS]
            Cm = x_dbl[:, DR + DS:]
            delta = jax.nn.softplus(jnp.einsum('er,brl->bel', dt_proj_w, dt_lo) + dt_proj_b[None, :, None])
            A = -jnp.exp(A_log)

            def step(state, xs):
                d_t, B_t, C_t, u_t = xs
                dA = jnp.exp(d_t[..., None] * A)
                state = state * dA + (d_t * u_t)[..., None] * B_t[:, None, :]
                y_t = jnp.einsum('ben,bn->be', state, C_t)
                return (state, y_t)
            xs = (jnp.moveaxis(delta, -1, 0), jnp.moveaxis(Bm, -1, 0), jnp.moveaxis(Cm, -1, 0), jnp.moveaxis(u, -1, 0))
            state0 = jnp.zeros((b, DI, DS), delta.dtype)
            _, ys = jax.lax.scan(step, state0, xs)
            y = jnp.moveaxis(ys, 0, -1)
            y = y + D[None, :, None] * u
            y = y * jax.nn.silu(z)
            return jnp.swapaxes(y, 1, 2)
        key = jax.random.key(seed)
        ks = jax.random.split(key, 8)
        hidden_states = jax.random.normal(ks[0], (B, L, DM), jnp.float32)
        z = jax.random.normal(ks[1], (B, DI, L), jnp.float32)
        in_proj_w = jax.random.normal(ks[2], (DI, DM), jnp.float32) * DM ** (-0.5)
        conv_w = jax.random.normal(ks[3], (DI, DC), jnp.float32) * DC ** (-0.5)
        conv_b = jnp.zeros((DI,), jnp.float32)
        x_proj_w = jax.random.normal(ks[4], (DR + 2 * DS, DI), jnp.float32) * DI ** (-0.5)
        dt_std = DR ** (-0.5)
        dt_proj_w = jax.random.uniform(ks[5], (DI, DR), jnp.float32, -dt_std, dt_std)
        dt = jnp.exp(jax.random.uniform(ks[6], (DI,), jnp.float32) * (math.log(DT_MAX) - math.log(DT_MIN)) + math.log(DT_MIN))
        dt = jnp.clip(dt, DT_FLOOR)
        dt_proj_b = dt + jnp.log(-jnp.expm1(-dt))
        A_log = jnp.log(jnp.broadcast_to(jnp.arange(1, DS + 1, dtype=jnp.float32), (DI, DS)))
        D = jnp.ones((DI,), jnp.float32)
        return dict(hidden_states=hidden_states, z=z, in_proj_w=in_proj_w, conv_w=conv_w, conv_b=conv_b, x_proj_w=x_proj_w, dt_proj_w=dt_proj_w, dt_proj_b=dt_proj_b, A_log=A_log, D=D)
    _L0_xattn_all = _L0_xattn_setup()
    _L0_xattn_in = {k: v for k, v in _L0_xattn_all.items() if k in ('in_proj_w', 'conv_w', 'conv_b', 'x_proj_w', 'dt_proj_w', 'dt_proj_b', 'A_log', 'D')}
    del _L0_xattn_all

    def _L0_ffn_setup():
        import jax, jax.numpy as jnp
        import numpy as np
        D = 256
        E = 8
        R = 16
        K = 2
        INIT_BONUS = 3.0
        ANNEAL_STEPS = 625
        CURRENT_STEP = 1
        key = jax.random.key(seed)
        ks = jax.random.split(key, 7)
        s_in = 1.0 / np.sqrt(D)
        s_r = 1.0 / np.sqrt(R)
        return {'x': jax.random.normal(ks[0], (2, 512, D), dtype=jnp.float32), 'Wr': jax.random.normal(ks[1], (D, E), dtype=jnp.float32) * s_in, 'br': jax.random.normal(ks[2], (E,), dtype=jnp.float32) * 0.01, 'Wd': jax.random.normal(ks[3], (E, D, R), dtype=jnp.float32) * s_in, 'bd': jnp.zeros((E, R), dtype=jnp.float32), 'Wu': jax.random.normal(ks[4], (E, R, D), dtype=jnp.float32) * s_r, 'bu': jnp.zeros((E, D), dtype=jnp.float32)}
    _L0_ffn_all = _L0_ffn_setup()
    _L0_ffn_in = {k: v for k, v in _L0_ffn_all.items() if k in ('Wr', 'br', 'Wd', 'bd', 'Wu', 'bu')}
    del _L0_ffn_all

    def _L1_attn_setup():
        import jax, jax.numpy as jnp
        import numpy as np
        D_MODEL = 256
        N_HEADS = 16
        HEAD_DIM = D_MODEL // N_HEADS
        ROPE_THETA = 10000.0
        BATCH = 2
        SEQ_LEN = 256

        def _apply_rope(x):
            S = x.shape[2]
            inv_freq = 1.0 / ROPE_THETA ** (jnp.arange(0, HEAD_DIM, 2, dtype=jnp.float32) / HEAD_DIM)
            t = jnp.arange(S, dtype=jnp.float32)
            freqs = jnp.outer(t, inv_freq)
            cos = jnp.cos(freqs)
            sin = jnp.sin(freqs)
            x1 = x[..., 0::2]
            x2 = x[..., 1::2]
            rot = jnp.stack([x1 * cos - x2 * sin, x1 * sin + x2 * cos], axis=-1)
            return rot.reshape(x.shape)
        key = jax.random.key(seed)
        ks = jax.random.split(key, 5)
        scale = 1.0 / np.sqrt(D_MODEL)
        x = jax.random.normal(ks[0], (BATCH, SEQ_LEN, D_MODEL), dtype=jnp.float32)
        Wq = jax.random.normal(ks[1], (D_MODEL, D_MODEL), dtype=jnp.float32) * scale
        Wk = jax.random.normal(ks[2], (D_MODEL, D_MODEL), dtype=jnp.float32) * scale
        Wv = jax.random.normal(ks[3], (D_MODEL, D_MODEL), dtype=jnp.float32) * scale
        Wo = jax.random.normal(ks[4], (D_MODEL, D_MODEL), dtype=jnp.float32) * scale
        return {'x': x, 'Wq': Wq, 'Wk': Wk, 'Wv': Wv, 'Wo': Wo}
    _L1_attn_all = _L1_attn_setup()
    _L1_attn_in = {k: v for k, v in _L1_attn_all.items() if k in ('Wq', 'Wk', 'Wv', 'Wo')}
    del _L1_attn_all

    def _L1_xattn_setup():
        import jax, jax.numpy as jnp
        import numpy as np
        N_HEADS = 16
        N_KV_HEADS = 8
        HEAD_DIM = 128
        D_TEXT = 256
        D_VISION = 128
        GROUPS = N_HEADS // N_KV_HEADS
        key = jax.random.key(seed)
        ks = jax.random.split(key, 6)
        B, T_text, T_vis = (4, 256, 72)
        text_hidden = jax.random.normal(ks[0], (B, T_text, D_TEXT), dtype=jnp.float32)
        vision_tokens = jax.random.normal(ks[1], (B, T_vis, D_VISION), dtype=jnp.float32)
        vision_mask = jnp.ones((B, T_vis), dtype=bool)
        s = 0.02
        Wq = jax.random.normal(ks[2], (D_TEXT, N_HEADS * HEAD_DIM), dtype=jnp.float32) * s
        Wk = jax.random.normal(ks[3], (D_VISION, N_KV_HEADS * HEAD_DIM), dtype=jnp.float32) * s
        Wv = jax.random.normal(ks[4], (D_VISION, N_KV_HEADS * HEAD_DIM), dtype=jnp.float32) * s
        Wo = jax.random.normal(ks[5], (N_HEADS * HEAD_DIM, D_TEXT), dtype=jnp.float32) * s
        return {'text_hidden': text_hidden, 'vision_tokens': vision_tokens, 'vision_mask': vision_mask, 'Wq': Wq, 'Wk': Wk, 'Wv': Wv, 'Wo': Wo}
    _L1_xattn_all = _L1_xattn_setup()
    _L1_xattn_in = {k: v for k, v in _L1_xattn_all.items() if k in ('Wq', 'Wk', 'Wv', 'Wo')}
    del _L1_xattn_all

    def _L1_ffn_setup():
        import jax, jax.numpy as jnp
        import numpy as np
        B, S, D = (4, 256, 256)
        E = 8
        H = 352
        CAP_F = 1.0

        def _moe(x, Wg, W1, W3, W2, sw1, sw3, sw2):
            b, sl, d = x.shape
            T = b * sl
            C = int(CAP_F * T / E)
            xt = x.reshape(T, d)
            probs = jax.nn.softmax(xt @ Wg, axis=-1)
            eidx = jnp.argmax(probs, axis=-1)
            gate = jnp.take_along_axis(probs, eidx[:, None], 1)[:, 0]
            oh = jax.nn.one_hot(eidx, E, dtype=jnp.int32)
            pos = (jnp.cumsum(oh, axis=0) * oh).sum(-1) - 1
            keep = pos < C
            flat = jnp.where(keep, eidx * C + pos, E * C)
            xd = jnp.zeros((E * C, d), x.dtype).at[flat].set(xt, mode='drop')
            xd = xd.reshape(E, C, d)
            h = jax.nn.silu(jnp.einsum('ecd,edh->ech', xd, W1)) * jnp.einsum('ecd,edh->ech', xd, W3)
            oe = jnp.einsum('ech,ehd->ecd', h, W2).reshape(E * C, d)
            out = jnp.take(oe, jnp.minimum(flat, E * C - 1), axis=0)
            out = out * (gate * keep.astype(x.dtype))[:, None]
            shared = jax.nn.silu(xt @ sw1) * (xt @ sw3) @ sw2
            return (out + shared).reshape(b, sl, d)
        key = jax.random.key(seed)
        ks = jax.random.split(key, 8)
        s = lambda fan: 1.0 / np.sqrt(fan)
        return {'x': jax.random.normal(ks[0], (B, S, D), jnp.float32), 'Wg': jax.random.normal(ks[1], (D, E), jnp.float32) * s(D), 'W1': jax.random.normal(ks[2], (E, D, H), jnp.float32) * s(D), 'W3': jax.random.normal(ks[3], (E, D, H), jnp.float32) * s(D), 'W2': jax.random.normal(ks[4], (E, H, D), jnp.float32) * s(H), 'sw1': jax.random.normal(ks[5], (D, H), jnp.float32) * s(D), 'sw3': jax.random.normal(ks[6], (D, H), jnp.float32) * s(D), 'sw2': jax.random.normal(ks[7], (H, D), jnp.float32) * s(H)}
    _L1_ffn_all = _L1_ffn_setup()
    _L1_ffn_in = {k: v for k, v in _L1_ffn_all.items() if k in ('Wg', 'W1', 'W3', 'W2', 'sw1', 'sw3', 'sw2')}
    del _L1_ffn_all
    return {'x': x, 'ctx_1024': ctx_1024, 'mask_BxS2_bf1': mask_BxS2_bf1, 'L0_attn_weight_qkv': _L0_attn_in['weight_qkv'], 'L0_attn_weight_out': _L0_attn_in['weight_out'], 'L0_xattn_in_proj_w': _L0_xattn_in['in_proj_w'], 'L0_xattn_conv_w': _L0_xattn_in['conv_w'], 'L0_xattn_conv_b': _L0_xattn_in['conv_b'], 'L0_xattn_x_proj_w': _L0_xattn_in['x_proj_w'], 'L0_xattn_dt_proj_w': _L0_xattn_in['dt_proj_w'], 'L0_xattn_dt_proj_b': _L0_xattn_in['dt_proj_b'], 'L0_xattn_A_log': _L0_xattn_in['A_log'], 'L0_xattn_D': _L0_xattn_in['D'], 'L0_ffn_Wr': _L0_ffn_in['Wr'], 'L0_ffn_br': _L0_ffn_in['br'], 'L0_ffn_Wd': _L0_ffn_in['Wd'], 'L0_ffn_bd': _L0_ffn_in['bd'], 'L0_ffn_Wu': _L0_ffn_in['Wu'], 'L0_ffn_bu': _L0_ffn_in['bu'], 'L1_attn_Wq': _L1_attn_in['Wq'], 'L1_attn_Wk': _L1_attn_in['Wk'], 'L1_attn_Wv': _L1_attn_in['Wv'], 'L1_attn_Wo': _L1_attn_in['Wo'], 'L1_xattn_Wq': _L1_xattn_in['Wq'], 'L1_xattn_Wk': _L1_xattn_in['Wk'], 'L1_xattn_Wv': _L1_xattn_in['Wv'], 'L1_xattn_Wo': _L1_xattn_in['Wo'], 'L1_ffn_Wg': _L1_ffn_in['Wg'], 'L1_ffn_W1': _L1_ffn_in['W1'], 'L1_ffn_W3': _L1_ffn_in['W3'], 'L1_ffn_W2': _L1_ffn_in['W2'], 'L1_ffn_sw1': _L1_ffn_in['sw1'], 'L1_ffn_sw3': _L1_ffn_in['sw3'], 'L1_ffn_sw2': _L1_ffn_in['sw2']}

def reference(x, ctx_1024, mask_BxS2_bf1, L0_attn_weight_qkv, L0_attn_weight_out, L0_xattn_in_proj_w, L0_xattn_conv_w, L0_xattn_conv_b, L0_xattn_x_proj_w, L0_xattn_dt_proj_w, L0_xattn_dt_proj_b, L0_xattn_A_log, L0_xattn_D, L0_ffn_Wr, L0_ffn_br, L0_ffn_Wd, L0_ffn_bd, L0_ffn_Wu, L0_ffn_bu, L1_attn_Wq, L1_attn_Wk, L1_attn_Wv, L1_attn_Wo, L1_xattn_Wq, L1_xattn_Wk, L1_xattn_Wv, L1_xattn_Wo, L1_ffn_Wg, L1_ffn_W1, L1_ffn_W3, L1_ffn_W2, L1_ffn_sw1, L1_ffn_sw3, L1_ffn_sw2):
    import jax
    import jax.numpy as jnp

    def _L0_attn_ref(x, weight_qkv, weight_out):
        import jax, jax.numpy as jnp
        import numpy as np
        L, N, E, H = (256, 2, 256, 16)
        DH = E // H
        SCALE = DH ** (-0.5)
        l, n, e = x.shape
        h, dh = (H, DH)
        qkv = jnp.einsum('lne,fe->lnf', x, weight_qkv)
        q, k, v = jnp.split(qkv, 3, axis=-1)
        q = q.reshape(l, n, h, dh) * jnp.asarray(SCALE, x.dtype)
        k = k.reshape(l, n, h, dh)
        v = v.reshape(l, n, h, dh)
        attn = jnp.einsum('lnhd,mnhd->nhlm', q, k)
        causal = jnp.tril(jnp.ones((l, l), dtype=bool))
        attn = jnp.where(causal, attn, jnp.asarray(-jnp.inf, attn.dtype))
        attn = jax.nn.softmax(attn, axis=-1)
        out = jnp.einsum('nhlm,mnhd->lnhd', attn, v).reshape(l, n, e)
        return jnp.einsum('lne,fe->lnf', out, weight_out)

    def _L0_xattn_ref(hidden_states, z, in_proj_w, conv_w, conv_b, x_proj_w, dt_proj_w, dt_proj_b, A_log, D):
        import jax, jax.numpy as jnp
        import numpy as np
        import math
        B, L, DM = (2, 256, 128)
        DS, DC, EXP = (16, 4, 2)
        DI = EXP * DM
        DR = math.ceil(DM / 16)
        DT_MIN, DT_MAX, DT_FLOOR = (0.001, 0.1, 0.0001)

        def _ssm_forward(hidden_states, z, in_proj_w, conv_w, conv_b, x_proj_w, dt_proj_w, dt_proj_b, A_log, D):
            b = hidden_states.shape[0]
            x = jnp.einsum('ed,bld->bel', in_proj_w, hidden_states)
            xp = jnp.pad(x, ((0, 0), (0, 0), (DC - 1, 0)))
            xc = jax.lax.conv_general_dilated(xp, conv_w[:, None, :], window_strides=(1,), padding='VALID', dimension_numbers=('NCH', 'OIH', 'NCH'), feature_group_count=DI)
            u = jax.nn.silu(xc + conv_b[None, :, None])
            x_dbl = jnp.einsum('ke,bel->bkl', x_proj_w, u)
            dt_lo = x_dbl[:, :DR]
            Bm = x_dbl[:, DR:DR + DS]
            Cm = x_dbl[:, DR + DS:]
            delta = jax.nn.softplus(jnp.einsum('er,brl->bel', dt_proj_w, dt_lo) + dt_proj_b[None, :, None])
            A = -jnp.exp(A_log)

            def step(state, xs):
                d_t, B_t, C_t, u_t = xs
                dA = jnp.exp(d_t[..., None] * A)
                state = state * dA + (d_t * u_t)[..., None] * B_t[:, None, :]
                y_t = jnp.einsum('ben,bn->be', state, C_t)
                return (state, y_t)
            xs = (jnp.moveaxis(delta, -1, 0), jnp.moveaxis(Bm, -1, 0), jnp.moveaxis(Cm, -1, 0), jnp.moveaxis(u, -1, 0))
            state0 = jnp.zeros((b, DI, DS), delta.dtype)
            _, ys = jax.lax.scan(step, state0, xs)
            y = jnp.moveaxis(ys, 0, -1)
            y = y + D[None, :, None] * u
            y = y * jax.nn.silu(z)
            return jnp.swapaxes(y, 1, 2)
        return _ssm_forward(hidden_states, z, in_proj_w, conv_w, conv_b, x_proj_w, dt_proj_w, dt_proj_b, A_log, D)

    def _L0_ffn_ref(x, Wr, br, Wd, bd, Wu, bu):
        import jax, jax.numpy as jnp
        import numpy as np
        D = 256
        E = 8
        R = 16
        K = 2
        INIT_BONUS = 3.0
        ANNEAL_STEPS = 625
        CURRENT_STEP = 1
        logits = jnp.einsum('btd,de->bte', x, Wr) + br
        progress = min(CURRENT_STEP / ANNEAL_STEPS, 1.0)
        bonus = INIT_BONUS * (1.0 - progress)
        logits = logits + bonus
        gates = jax.nn.softmax(logits, axis=-1)
        topk_vals, topk_idx = jax.lax.top_k(gates, K)
        topk_vals = topk_vals / topk_vals.sum(axis=-1, keepdims=True)
        w = (jax.nn.one_hot(topk_idx, E, dtype=x.dtype) * topk_vals[..., None]).sum(axis=-2)
        h = jax.nn.relu(jnp.einsum('btd,edr->betr', x, Wd) + bd[None, :, None, :])
        eo = jnp.einsum('betr,erd->betd', h, Wu) + bu[None, :, None, :]
        out = jnp.einsum('bte,betd->btd', w, eo)
        return out

    def _L1_attn_ref(x, Wq, Wk, Wv, Wo):
        import jax, jax.numpy as jnp
        import numpy as np
        D_MODEL = 256
        N_HEADS = 16
        HEAD_DIM = D_MODEL // N_HEADS
        ROPE_THETA = 10000.0
        BATCH = 2
        SEQ_LEN = 256

        def _apply_rope(x):
            S = x.shape[2]
            inv_freq = 1.0 / ROPE_THETA ** (jnp.arange(0, HEAD_DIM, 2, dtype=jnp.float32) / HEAD_DIM)
            t = jnp.arange(S, dtype=jnp.float32)
            freqs = jnp.outer(t, inv_freq)
            cos = jnp.cos(freqs)
            sin = jnp.sin(freqs)
            x1 = x[..., 0::2]
            x2 = x[..., 1::2]
            rot = jnp.stack([x1 * cos - x2 * sin, x1 * sin + x2 * cos], axis=-1)
            return rot.reshape(x.shape)
        B, S, _ = x.shape
        q = (x @ Wq.T).reshape(B, S, N_HEADS, HEAD_DIM).transpose(0, 2, 1, 3)
        k = (x @ Wk.T).reshape(B, S, N_HEADS, HEAD_DIM).transpose(0, 2, 1, 3)
        v = (x @ Wv.T).reshape(B, S, N_HEADS, HEAD_DIM).transpose(0, 2, 1, 3)
        q = _apply_rope(q)
        k = _apply_rope(k)
        scores = jnp.einsum('bhqd,bhkd->bhqk', q, k) / np.sqrt(HEAD_DIM).astype(np.float32)
        causal = jnp.tril(jnp.ones((S, S), dtype=bool))
        scores = jnp.where(causal, scores, -jnp.inf)
        attn = jax.nn.softmax(scores, axis=-1)
        out = jnp.einsum('bhqk,bhkd->bhqd', attn, v)
        out = out.transpose(0, 2, 1, 3).reshape(B, S, N_HEADS * HEAD_DIM)
        return out @ Wo.T

    def _L1_xattn_ref(text_hidden, vision_tokens, vision_mask, Wq, Wk, Wv, Wo):
        import jax, jax.numpy as jnp
        import numpy as np
        N_HEADS = 16
        N_KV_HEADS = 8
        HEAD_DIM = 128
        D_TEXT = 256
        D_VISION = 128
        GROUPS = N_HEADS // N_KV_HEADS
        B, T_text, _ = text_hidden.shape
        T_vis = vision_tokens.shape[1]
        scale = jnp.float32(np.sqrt(HEAD_DIM))
        q = (text_hidden @ Wq).reshape(B, T_text, N_HEADS, HEAD_DIM).transpose(0, 2, 1, 3)
        k = (vision_tokens @ Wk).reshape(B, T_vis, N_KV_HEADS, HEAD_DIM).transpose(0, 2, 1, 3)
        v = (vision_tokens @ Wv).reshape(B, T_vis, N_KV_HEADS, HEAD_DIM).transpose(0, 2, 1, 3)
        k = jnp.repeat(k, GROUPS, axis=1)
        v = jnp.repeat(v, GROUPS, axis=1)
        scores = jnp.einsum('bhtd,bhsd->bhts', q, k) / scale
        mask = vision_mask[:, None, None, :]
        scores = jnp.where(mask, scores, -jnp.inf)
        attn = jax.nn.softmax(scores, axis=-1)
        attn = jnp.nan_to_num(attn, nan=0.0)
        out = jnp.einsum('bhts,bhsd->bhtd', attn, v)
        out = out.transpose(0, 2, 1, 3).reshape(B, T_text, N_HEADS * HEAD_DIM)
        return out @ Wo

    def _L1_ffn_ref(x, Wg, W1, W3, W2, sw1, sw3, sw2):
        import jax, jax.numpy as jnp
        import numpy as np
        B, S, D = (4, 256, 256)
        E = 8
        H = 352
        CAP_F = 1.0

        def _moe(x, Wg, W1, W3, W2, sw1, sw3, sw2):
            b, sl, d = x.shape
            T = b * sl
            C = int(CAP_F * T / E)
            xt = x.reshape(T, d)
            probs = jax.nn.softmax(xt @ Wg, axis=-1)
            eidx = jnp.argmax(probs, axis=-1)
            gate = jnp.take_along_axis(probs, eidx[:, None], 1)[:, 0]
            oh = jax.nn.one_hot(eidx, E, dtype=jnp.int32)
            pos = (jnp.cumsum(oh, axis=0) * oh).sum(-1) - 1
            keep = pos < C
            flat = jnp.where(keep, eidx * C + pos, E * C)
            xd = jnp.zeros((E * C, d), x.dtype).at[flat].set(xt, mode='drop')
            xd = xd.reshape(E, C, d)
            h = jax.nn.silu(jnp.einsum('ecd,edh->ech', xd, W1)) * jnp.einsum('ecd,edh->ech', xd, W3)
            oe = jnp.einsum('ech,ehd->ecd', h, W2).reshape(E * C, d)
            out = jnp.take(oe, jnp.minimum(flat, E * C - 1), axis=0)
            out = out * (gate * keep.astype(x.dtype))[:, None]
            shared = jax.nn.silu(xt @ sw1) * (xt @ sw3) @ sw2
            return (out + shared).reshape(b, sl, d)
        return _moe(x, Wg, W1, W3, W2, sw1, sw3, sw2)
    x = _layernorm(x + _L0_attn_ref(x, L0_attn_weight_qkv, L0_attn_weight_out), axis=-1)
    x = _layernorm(x + _L0_xattn_ref(ctx_1024, x, L0_xattn_in_proj_w, L0_xattn_conv_w, L0_xattn_conv_b, L0_xattn_x_proj_w, L0_xattn_dt_proj_w, L0_xattn_dt_proj_b, L0_xattn_A_log, L0_xattn_D), axis=-1)
    x = _layernorm(x + _L0_ffn_ref(x, L0_ffn_Wr, L0_ffn_br, L0_ffn_Wd, L0_ffn_bd, L0_ffn_Wu, L0_ffn_bu), axis=-1)
    x = _layernorm(x + _L1_attn_ref(x, L1_attn_Wq, L1_attn_Wk, L1_attn_Wv, L1_attn_Wo), axis=-1)
    x = _layernorm(x + _L1_xattn_ref(x, ctx_1024, mask_BxS2_bf1, L1_xattn_Wq, L1_xattn_Wk, L1_xattn_Wv, L1_xattn_Wo), axis=-1)
    x = _layernorm(x + _L1_ffn_ref(x, L1_ffn_Wg, L1_ffn_W1, L1_ffn_W3, L1_ffn_W2, L1_ffn_sw1, L1_ffn_sw3, L1_ffn_sw2), axis=-1)
    return x

_drawn_inputs = setup_inputs


def setup_inputs(seed=0):
    import zlib

    import numpy as np

    out = dict(_drawn_inputs(seed))
    spreads = {'L0_xattn_conv_b': (0.0, 0.1),
     'L0_xattn_D': (1.0, 0.2),
     'L0_ffn_bd': (0.0, 0.1),
     'L0_ffn_bu': (0.0, 0.1)}
    factors = {'L1_xattn_Wq': 5.788, 'L1_xattn_Wk': 5.095}
    for name, (base, spread) in spreads.items():
        noise = np.random.default_rng([zlib.crc32(name.encode()), seed]).standard_normal(out[name].shape)
        drawn = base * np.exp(spread * noise) if base else spread * noise
        out[name] = jnp.asarray(drawn.astype(out[name].dtype))
    for name, factor in factors.items():
        out[name] = (out[name] * factor).astype(out[name].dtype)
    return out
```

```python
from contextlib import ExitStack

import numpy as np

import concourse.bass as bass
from concourse import mybir

F32 = mybir.dt.float32
BF16 = mybir.dt.bfloat16
U32 = mybir.dt.uint32
U8 = mybir.dt.uint8
ALU = mybir.AluOpType
ACT = mybir.ActivationFunctionType
AX = mybir.AxisListType

P = 128
B, S, D = 4, 256, 256
T = B * S
NT = T // P
KD = D // P
HEADS, DH = 16, 16
CTX = 128
DI, DS, DC, DR = 256, 16, 4, 8
E, R = 8, 16
XH, XKV, XD = 16, 8, 128
HID = 352
HC = [(0, 128), (128, 128), (256, 96)]
CAP = T // E
EPS = 1e-5
BONUS = 3.0 * (1.0 - min(1 / 625, 1.0))
NEG = -1e30
XSCALE = 1.0 / float(np.float32(np.sqrt(XD)))


_LAST = []


def last():
    return _LAST[-1]


class Signal:

    def __init__(self, ctx, nc, name):
        self.sem, self.n = ctx.enter_context(nc.semaphore(name)), 0

    def inc(self, step=1):
        self.n += step
        _LAST[:] = [(self.sem, self.n)]
        return self.sem, step

    def nth(self, i, step=1):
        return self.sem, (i + 1) * step


class Drained:

    def __init__(self, sem, value):
        self.sem, self.value = sem, value

    def inc(self):
        _LAST[:] = [(self.sem, self.value)]
        return self.sem, 1


class Banks:

    def __init__(self, ctx, nc, name, n):
        self.banks = [ctx.enter_context(nc.psum_tensor(f"{name}{i}", [P, 512], F32)) for i in range(n)]
        self.filled = Signal(ctx, nc, f"{name}_filled")
        self.drained = [Signal(ctx, nc, f"{name}{i}_drained") for i in range(n)]
        self.table, self.used = {}, 0

    def take(self, pe, *use):
        i, k = self.used % len(self.banks), self.used // len(self.banks)
        assert use not in self.table
        self.table[use] = (i, k, self.used)
        self.used += 1
        if k:
            pe.wait_ge(self.drained[i].sem, k)
        return self.banks[i]

    def get(self, eng, *use):
        i, _, n = self.table[use]
        eng.wait_ge(*self.filled.nth(n))
        return self.banks[i]

    def full(self, *use):
        return self.filled.nth(self.table[use][2])

    def drain(self, *use):
        i, k, _ = self.table[use]
        return Drained(self.drained[i].sem, k + 1)

    def empty(self, *use):
        i, k, _ = self.table[use]
        return self.drained[i].sem, k + 1


class Engine:

    def __init__(self, eng):
        self.eng, self.passed = eng, {}

    def wait_ge(self, sem, value):
        if self.passed.get(id(sem), 0) < value:
            self.eng.wait_ge(sem, value)
            self.passed[id(sem)] = value


def decoder(nc, a, out):
    ctx = ExitStack()
    with ctx:
        def sb(name, shape, dt=F32):
            return ctx.enter_context(nc.sbuf_tensor(name, shape, dt))

        def signal(name):
            return Signal(ctx, nc, name)

        x_tok = sb("x_tok", [P, NT, D])
        ctx_t = sb("ctx_t", [CTX, T])
        ident = sb("ident", [P, P])
        ident_bf = sb("ident_bf", [P, P], BF16)
        row_pick = sb("row_pick", [96, 32, P], BF16)
        mask_qk = sb("mask_qk", [P, P], BF16)
        mask_kq = sb("mask_kq", [P, P], BF16)
        head_of = sb("head_of", [P, 8])
        small = sb("small", [P, 64])
        eid_rev = sb("eid_rev", [P, E])
        delta = sb("delta", [P, 2, B, S])
        u = sb("u", [P, 2, B, S])
        du = sb("du", [P, 2, B, S])
        bc_parts = sb("bc_parts", [96, B, S], BF16)
        silu_z = sb("silu_z", [P, NT, D])
        a_neg = sb("a_neg", [P, 2, DS])
        ln_r = sb("ln_r", [P, 2, D])
        ln_st = sb("ln_st", [P, 2, 6])
        ln_mv = sb("ln_mv", [P, 2, 2])
        ln_var = sb("ln_var", [P, 2, 2])
        ln_rs = sb("ln_rs", [P, 2, 2])
        half_neg = sb("half_neg", [P, 2])
        x_feat = sb("x_feat", [P, KD, S])
        ssm_p = sb("ssm_p", [P, 2, 4 + 1 + 1 + 1 + DS])
        w_r = sb("w_r", [P, KD, E])
        b_r = sb("b_r", [P, E])
        w_d = sb("w_d", [P, KD, P])
        b_d = sb("b_d", [P, 1])
        w_u = sb("w_u", [P, D])
        b_u = sb("b_u", [E, D])
        spread = sb("spread", [E, P])
        rope = sb("rope", [P, 2, 3, 8])
        y_gate = sb("y_gate", [P, 2, S])
        g8 = sb("g8", [P, 10, 2, E])
        w_e_t = sb("w_e_t", [E, S])
        h_relu, h_w = y_gate[:, 0, :], y_gate[:, 1, :]

        def arena(name, words):
            t = sb(name, [P, words])
            at = [0]

            def reset():
                at[0] = 0

            def view(shape, dt=F32):
                n = int(np.prod(shape))
                w = n if dt != BF16 else n // 2
                v = t[:, at[0]:at[0] + w]
                at[0] += w
                assert at[0] <= words, (name, at[0])
                if dt != F32:
                    v = v.bitcast(dt)
                if len(shape) > 1:
                    names = "abcd"[:len(shape)]
                    v = v.rearrange(f"p ({' '.join(names)}) -> p {' '.join(names)}",
                                    **{c: n for c, n in zip(names, shape)})
                return v
            return view, reset

        one, one_again = arena("arena_one", 16300)
        x0_feat = one([KD, T])
        in_pt = one([DI])
        x_pt = one([2, 104])
        dt_pt = one([DI])[0:DR, :]
        w_qkv = one([KD, 3 * D])
        w_o0 = one([KD, D])
        qkv = one([NT, 3 * D])
        x_pad = one([2, 2, S + DC - 1])
        tmp_a = one([2, 2 * S])
        tmp_b = one([2, 2 * S])
        dt_low = one([T])
        bf_tmp = one([2 * S], BF16)
        s0 = one([2, 4, HEADS, 4])
        prod0 = silu_z[:, 0:4, :]
        s0_stat = one([P])
        o0_feat = x0_feat
        o0 = qkv[:, :, 0:D]
        one_again()
        w_qk1 = one([KD, 2 * D])
        w_v1 = one([KD, D])
        w_o1 = one([KD, D])
        qk_rot = one([2, 2 * D])
        rot_b = one([2 * D])
        q_feat = one([KD, S])
        k_feat = one([KD, S])
        k_head = one([HEADS, S])
        NB = 2
        decay, drive, state, seen_c = (
            k_head[:, 4 * i:4 * i + 4, :].rearrange("p (n e) s -> p n e s", n=NB) for i in range(4))
        p_t0 = one([HEADS, S])
        p_t1 = one([HEADS, P])
        v_aug = one([2, HEADS, 32])
        o_heads, o_norm, o_feat = qk_rot.rearrange("p a (b s) -> p (a b) s", b=2), k_feat, q_feat
        neg_max = one([2, HEADS])
        nm_res = one([2, HEADS])
        nm_parts = one([2, 96], BF16)
        nm_feat = one([S], BF16)
        o_den = one([2, HEADS])
        one_again()
        w_1 = one([E, KD, HID])
        w_3 = one([E, KD, HID])
        e_gate = one([3 * P])
        e_hid = one([2, 3 * P])

        two, two_again = arena("arena_two", 18900)
        wx_q = two([KD, XH * XD])
        wx_k = two([XKV * XD])
        wx_v = two([XKV * XD])
        wx_o = two([XH, D])
        kx_feat = two([XKV, S])
        vx_tok = two([2, XKV * XD])
        NX = 3
        qx_feat = two([2, S])
        px = two([NX, 2, S])
        px_t = two([2, 2, S])
        ox_feat = two([2, S])
        x_max = two([NX, 2])
        x_nmax = two([NX, 2])
        x_sum = two([NX, 2])
        x_inv = two([NX, 2])
        mask_add = two([B, S], BF16)
        mask_raw = two([T // 4]).bitcast(U8)
        mask_any = two([B])
        two_again()
        w_2 = two([E, 3, D])
        ws_1 = two([KD, HID])
        ws_3 = two([KD, HID])
        ws_2 = two([3, D])
        w_g = two([KD, E])
        hs = two([3, 512])
        x5_feat = two([KD, T])
        r8 = two([8, NT, E])
        oh_bf = two([NT, E], BF16)
        tri = two([P], BF16)
        ones = two([P], BF16)
        r1 = two([8, NT])
        dump = two([NT])
        ebase = two([E])
        slot_u = two([2, NT]).bitcast(U32)
        xd_tok, xd_feat, oe = delta, du, u
        xd_tok = xd_tok[:, :, :, :].rearrange("p a b c -> p (a b c)").rearrange("p (e d) -> p e d", e=E)
        xd_feat = xd_feat[:, :, :, :].rearrange("p a b c -> p (a b c)").rearrange("p (k t) -> p k t", k=KD)
        oe = oe[:, :, :, :].rearrange("p a b c -> p (a b c)").rearrange("p (e d) -> p e d", e=E)
        og = silu_z

        xd_dram = nc.dram_tensor("xd_dram", (2 * T, D), F32).ap()
        oe_dram = nc.dram_tensor("oe_dram", (T, D), F32).ap()

        psum = Banks(ctx, nc, "psum", 5)
        y_psum = Banks(ctx, nc, "y_psum", 1)
        o_psum = Banks(ctx, nc, "o_psum", 2)

        names = """ld_attn0 ld_ssm ld_const ld_moe0 ld_x ld_rope ld_attn1 ld_xattn ld_w13 ld_w2 ld_shared ld_moe1
            zeroed xd_scattered xd_loaded oe_stored oe_gathered out_stored pe_step act_step dve_step
            pool_step pads_clear final_ready u_ready conv_ready expo_arg softplus_t softplus_w softplus_ln
            delta_ready a_ready a_exp s0_arg s0_exp o0_ready decay_ready decay_used seen_used silu_z_ready
            y_ready x1_ready x2_ready x3_ready x4_ready x5_ready var_ready rstd_ready gate_arg gate_exp
            w_ready qk_ready khead_ready nm_ready ones_ready decay_clear smax_ready sexp_ready pn_ready
            ox_used route_exp oh_ready slots_ready""".split()
        sg = {n: signal(n) for n in names}

        block = ctx.enter_context(nc.Block())

        loads = dict(ld_ssm=5, ld_attn0=3, ld_const=6, ld_x=1, ld_moe0=7, ld_xattn=5, ld_rope=2, ld_attn1=3,
                     ld_w13=2, ld_w2=1, ld_shared=4, ld_moe1=4)

        def loaded(name):
            return sg[name].sem, 16 * loads[name]

        def T2(t, b):
            return t[:, 2 * b:2 * b + 2, :]

        @block.tensor
        def _(eng):
            pe = Engine(eng)
            mm, tr = nc.tensor.matmul, nc.tensor.transpose

            def turn(name, b, tiles):
                ps = psum.take(pe, name, b)
                for k in range(KD):
                    for h in range(2):
                        ins = tr(ps[:, k * S + h * P:k * S + h * P + P], tiles(h, k), ident[:, :])
                ins.then_inc(*psum.filled.inc())

            def project(name, b, feat, w):
                ps = psum.take(pe, name, b)
                for h in range(2):
                    for k in range(KD):
                        ins = mm(ps[:, h * D:(h + 1) * D], feat(h, k), w[:, k, :], start=(k == 0), stop=(k == KD - 1))
                ins.then_inc(*psum.filled.inc())

            pe.wait_ge(*loaded("ld_ssm"))
            for hf in range(2):
                for et in range(2):
                    ps = psum.take(pe, "xin", hf, et)
                    mm(ps[:, :], in_pt[:, et * P:(et + 1) * P], ctx_t[:, hf * 512:(hf + 1) * 512],
                                 start=True, stop=True).then_inc(*psum.filled.inc())
            pe.wait_ge(*loaded("ld_attn0"))

            def qkv0(t):
                for name, c0, c1 in (("qk0", 0, 512), ("v0", 512, 768)):
                    ps = psum.take(pe, name, t)
                    for k in range(KD):
                        ins = mm(ps[:, 0:c1 - c0], x0_feat[:, k, t * P:(t + 1) * P], w_qkv[:, k, c0:c1],
                                 start=(k == 0), stop=(k == KD - 1))
                    ins.then_inc(*psum.filled.inc())

            for t in range(NT // 2):
                qkv0(t)
            for hf in range(2):
                cols = slice(hf * 512, (hf + 1) * 512)
                pe.wait_ge(*sg["u_ready"].nth(2 * hf + 1))
                uf = u[:, :, :, :].rearrange("p e b s -> p e (b s)")
                ps = psum.take(pe, "bc", hf)
                for et in range(2):
                    ins = mm(ps[0:96, :], x_pt[:, et, 0:96], uf[:, et, cols], start=(et == 0), stop=(et == 1))
                ins.then_inc(*psum.filled.inc())
                ps = psum.take(pe, "dt", hf)
                for et in range(2):
                    ins = mm(ps[0:DR, :], x_pt[:, et, 96:104], uf[:, et, cols], start=(et == 0), stop=(et == 1))
                ins.then_inc(*psum.filled.inc())
                pe.wait_ge(*psum.empty("dt", hf))
                for et in range(2):
                    ps = psum.take(pe, "dp", hf, et)
                    mm(ps[:, :], dt_pt[:, et * P:(et + 1) * P], dt_low[0:DR, cols], start=True, stop=True).then_inc(*psum.filled.inc())
                for t in range(4 + 2 * hf, 6 + 2 * hf):
                    qkv0(t)
            pe.wait_ge(*sg["o0_ready"].nth(1))
            pe.wait_ge(*loaded("ld_const"))
            for t in range(0, NT, 2):
                turn("o0t", t, lambda h, k: o0[:, t + h, k * P:(k + 1) * P])
            for t in range(0, NT, 2):
                pe.wait_ge(*psum.empty("o0t", t))
                project("proj0", t // 2, lambda h, k: o0_feat[:, k, (t + h) * P:(t + h + 1) * P], w_o0)

            def ssm_core(b):
                for n in range(DS + 3):
                    if n < DS:
                        pe.wait_ge(*sg["delta_ready"].nth(b // 2))
                        ps = psum.take(pe, "bcn", b, n)
                        for j in range(2):
                            ins = mm(ps[:, j * S:(j + 1) * S], row_pick[:, j * DS + n, :], bc_parts[:, b, :],
                                     start=True, stop=True)
                        ins.then_inc(*psum.filled.inc())
                    if n >= 3:
                        m = n - 3
                        if m == 0:
                            y_acc = y_psum.take(pe, "y", b)
                        pe.wait_ge(*psum.empty("bcn", b, m))
                        ins = mm(y_acc[:, :], ident[:, :], seen_c[:, m % NB, :, :].rearrange("p e s -> p (e s)"),
                                 start=(m == 0), stop=(m == DS - 1))
                        if m == DS - 1:
                            ins.then_inc(*y_psum.filled.inc())
                        else:
                            ins.then_inc(*sg["seen_used"].inc())

            def ssm_tail(b):
                pe.wait_ge(*sg["y_ready"].nth(b))
                ps = psum.take(pe, "yt", b)
                for lt in range(2):
                    for et in range(2):
                        ins = tr(ps[:, lt * DI + et * P:lt * DI + (et + 1) * P], y_gate[:, et, lt * P:(lt + 1) * P],
                                 ident[:, :])
                ins.then_inc(*psum.filled.inc())

            def moe0(b):
                pe.wait_ge(*sg["x2_ready"].nth(2 * b + 1))
                pe.wait_ge(*loaded("ld_moe0"))
                turn("x2t", b, lambda h, k: x_tok[:, 2 * b + h, k * P:(k + 1) * P])
                pe.wait_ge(*psum.empty("x2t", b))
                ps = psum.take(pe, "gate0", b)
                for h in range(2):
                    for k in range(KD):
                        ins = mm(ps[:, h * E:(h + 1) * E], x_feat[:, k, h * P:(h + 1) * P], w_r[:, k, :],
                                 start=(k == 0), stop=(k == KD - 1))
                ins.then_inc(*psum.filled.inc())
                ps = psum.take(pe, "hid0", b)
                for k in range(KD):
                    ins = mm(ps[:, 0:S], w_d[:, k, :], x_feat[:, k, :], start=(k == 0), stop=(k == KD - 1))
                ins.then_inc(*psum.filled.inc())
                pe.wait_ge(*sg["w_ready"].nth(b))
                ps = psum.take(pe, "wt0", b)
                for h in range(2):
                    ins = tr(ps[0:E, h * P:(h + 1) * P], g8[:, 9, h, :], ident[:, :])
                ins.then_inc(*psum.filled.inc())
                pe.wait_ge(*psum.empty("wt0", b))
                ps = psum.take(pe, "spread0", b)
                mm(ps[:, 0:S], spread[:, :], w_e_t[:, :], start=True, stop=True).then_inc(*psum.filled.inc())
                pe.wait_ge(*psum.empty("spread0", b))
                ps = psum.take(pe, "out0", b)
                for h in range(2):
                    mm(ps[:, h * D:(h + 1) * D], h_w[:, h * P:(h + 1) * P], w_u[:, :], start=True, stop=False)
                    ins = mm(ps[:, h * D:(h + 1) * D], w_e_t[:, h * P:(h + 1) * P], b_u[:, :], start=False, stop=True)
                ins.then_inc(*psum.filled.inc())

            def attn1(b):
                pe.wait_ge(*sg["x3_ready"].nth(2 * b + 1))
                pe.wait_ge(*loaded("ld_attn1"))
                turn("x3t", b, lambda h, k: x_tok[:, 2 * b + h, k * P:(k + 1) * P])
                pe.wait_ge(*psum.empty("x3t", b))
                for h in range(2):
                    ps = psum.take(pe, "qk1", b, h)
                    for k in range(KD):
                        ins = mm(ps[:, :], x_feat[:, k, h * P:(h + 1) * P], w_qk1[:, k, :],
                                 start=(k == 0), stop=(k == KD - 1))
                    ins.then_inc(*psum.filled.inc())
                project("v1", b, lambda h, k: x_feat[:, k, h * P:(h + 1) * P], w_v1)
                pe.wait_ge(*sg["qk_ready"].nth(2 * b + 1))
                for name, c0 in (("q1t", 0), ("k1t", D)):
                    ps = psum.take(pe, name, b)
                    for k in range(KD):
                        for h in range(2):
                            ins = tr(ps[:, k * S + h * P:k * S + (h + 1) * P],
                                     qk_rot[:, h, c0 + k * P:c0 + (k + 1) * P], ident[:, :])
                    ins.then_inc(*psum.filled.inc())
                pe.wait_ge(*psum.empty("q1t", b))
                for g in range(4):
                    pe.wait_ge(*sg["khead_ready"].nth(b * HEADS + 4 * g + 3))
                    ps = psum.take(pe, "s1a", b, g)
                    mm(ps[:, :], q_feat[:, g // 2, 0:P], k_head[:, 4 * g:4 * g + 4, 0:P], start=True, stop=False)
                    mm(ps[:, :], ident_bf[:, :], mask_qk[:, :].unsqueeze(1).broadcast_to([P, 4, P]),
                                 start=False, stop=True).then_inc(*psum.filled.inc())
                for g in range(8):
                    ps = psum.take(pe, "s1b", b, g)
                    mm(ps[:, :], q_feat[:, g // 4, P:S], k_head[:, 2 * g:2 * g + 2, :], start=True, stop=False)
                    mm(ps[:, :].rearrange("p (h k) -> p h k", h=2)[:, :, P:S], ident_bf[:, :],
                                 mask_qk[:, :].unsqueeze(1).broadcast_to([P, 2, P]), start=False, stop=True).then_inc(*psum.filled.inc())
                pe.wait_ge(*sg["nm_ready"].nth(b))
                ps = psum.take(pe, "nm1", b)
                psb = ps[:, :].bitcast(BF16)
                for h in range(2):
                    ins = tr(psb[0:96, h * P:(h + 1) * P], nm_parts[:, h, :], ident_bf[:, :])
                ins.then_inc(*psum.filled.inc())
                pe.wait_ge(*psum.empty("nm1", b))

                def scores_t(name, g, heads, kt):
                    q0 = kt * P
                    w = S - q0
                    ps = psum.take(pe, name, b, g)
                    for i, h in enumerate(heads):
                        o = ps[:, i * w:(i + 1) * w]
                        mm(o, k_head[:, h, kt * P:(kt + 1) * P], q_feat[:, h // 8, q0:S], start=True, stop=False)
                        mm(o, row_pick[:, h, :], nm_feat[0:96, q0:S], start=False, stop=False)
                        ins = mm(o[:, 0:P], ident_bf[:, :], mask_kq[:, :], start=False, stop=True)
                    ins.then_inc(*psum.filled.inc())

                def values(h):
                    g, j = h // 4, h % 4
                    if h % 8 == 0:
                        values.ps = psum.take(pe, "ov1", b, h // 8)
                    pe.wait_ge(*psum.empty("st0", b, 2 * g))
                    pe.wait_ge(*psum.empty("st0", b, 2 * g + 1))
                    pe.wait_ge(*psum.empty("st1", b, g))
                    o = values.ps[32 * j:32 * j + 32, (g % 2) * S:(g % 2 + 1) * S]
                    mm(o, v_aug[:, 0, h, :], p_t0[:, h, :], start=True, stop=False)
                    ins = mm(o[:, P:S], v_aug[:, 1, h, :], p_t1[:, h, :], start=False, stop=True)
                    if h % 8 == 7:
                        ins.then_inc(*psum.filled.inc())

                pe.wait_ge(*psum.empty("v1", b))
                pe.wait_ge(*sg["ones_ready"].nth(0))
                for g in range(4):
                    scores_t("st0", 2 * g, (4 * g, 4 * g + 1), 0)
                    scores_t("st0", 2 * g + 1, (4 * g + 2, 4 * g + 3), 0)
                    scores_t("st1", g, range(4 * g, 4 * g + 4), 1)
                    if g:
                        for h in range(4 * g - 4, 4 * g):
                            values(h)
                for h in range(12, 16):
                    values(h)
                for h in range(2):
                    pe.wait_ge(*psum.empty("ov1", b, 0))
                    pe.wait_ge(*psum.empty("ov1", b, 1))
                    ps = psum.take(pe, "on1", b, h)
                    for g in range(4):
                        ins = tr(ps[:, g * P:(g + 1) * P], o_heads[:, g, h * P:(h + 1) * P], ident[:, :])
                    ins.then_inc(*psum.filled.inc())
                pe.wait_ge(*psum.empty("on1", b, 0))
                pe.wait_ge(*psum.empty("on1", b, 1))
                turn("o1t", b, lambda h, k: o_norm[:, h, k * P:(k + 1) * P])
                pe.wait_ge(*psum.empty("o1t", b))
                project("proj1", b, lambda h, k: o_feat[:, k, h * P:(h + 1) * P], w_o1)

            def xattn(b):
                pe.wait_ge(*loaded("ld_xattn"))
                for g in range(0, XKV, 2):
                    ps = psum.take(pe, "kx", b, g)
                    for i in range(2):
                        ins = mm(ps[:, i * S:(i + 1) * S], wx_k[:, (g + i) * XD:(g + i + 1) * XD],
                                 ctx_t[:, b * S:(b + 1) * S], start=True, stop=True)
                    ins.then_inc(*psum.filled.inc())
                for kt in range(2):
                    for i in range(2):
                        ps = psum.take(pe, "vx", b, kt, i)
                        mm(ps[:, :], ctx_t[:, b * S + kt * P:b * S + (kt + 1) * P],
                                     wx_v[:, i * 512:(i + 1) * 512], start=True, stop=True).then_inc(*psum.filled.inc())
                pe.wait_ge(*sg["x4_ready"].nth(2 * b + 1))
                turn("x4t", b, lambda h, k: x_tok[:, 2 * b + h, k * P:(k + 1) * P])
                pe.wait_ge(*psum.empty("x4t", b))
                pe.wait_ge(*psum.empty("vx", b, 1, 1))
                acc = [o_psum.take(pe, "ox", b, h) for h in range(2)]
                for i in range(XH + 4):
                    if 3 <= i < XH + 3:
                        h = i - 3
                        pe.wait_ge(*sg["pn_ready"].nth(2 * (b * XH + h) + 1))
                        ps = psum.take(pe, "pxt", b, h)
                        for kt in range(2):
                            for qt in range(2):
                                ins = tr(ps[:, kt * S + qt * P:kt * S + (qt + 1) * P],
                                         px[:, h % NX, qt, kt * P:(kt + 1) * P], ident[:, :])
                        ins.then_inc(*psum.filled.inc())
                    if i < XH:
                        ps = psum.take(pe, "qx", b, i)
                        for k in range(KD):
                            ins = mm(ps[:, 0:S], wx_q[:, k, i * XD:(i + 1) * XD], x_feat[:, k, :],
                                     start=(k == 0), stop=(k == KD - 1))
                        ins.then_inc(*psum.filled.inc())
                    if 1 <= i < XH + 1:
                        h = i - 1
                        pe.wait_ge(*psum.empty("qx", b, h))
                        ps = psum.take(pe, "sx", b, h)
                        for qt in range(2):
                            ins = mm(ps[:, qt * S:(qt + 1) * S], qx_feat[:, h % 2, qt * P:(qt + 1) * P],
                                     kx_feat[:, h // 2, :], start=True, stop=True)
                        ins.then_inc(*psum.filled.inc())
                    if 3 <= i < XH + 3:
                        h = i - 3
                        pe.wait_ge(*psum.empty("pxt", b, h))
                        ps = psum.take(pe, "pvx", b, h)
                        for kt in range(2):
                            ins = mm(ps[:, 0:S], vx_tok[:, kt, h // 2 * XD:(h // 2 + 1) * XD], px_t[:, h % 2, kt, :],
                                     start=(kt == 0), stop=(kt == 1))
                        ins.then_inc(*psum.filled.inc())
                    if i >= 4:
                        h = i - 4
                        pe.wait_ge(*psum.empty("pvx", b, h))
                        for qt in range(2):
                            ins = mm(acc[qt][:, 0:D], ox_feat[:, h % 2, qt * P:(qt + 1) * P], wx_o[:, h, :],
                                     start=(h == 0), stop=(h == XH - 1))
                            if h == XH - 1:
                                ins.then_inc(*o_psum.filled.inc())
                        if h < XH - 1:
                            ins.then_inc(*sg["ox_used"].inc())

            for b in range(B):
                ssm_core(b)
                ssm_tail(b)
                moe0(b)
                attn1(b)
                xattn(b)

            for t in range(0, NT, 2):
                pe.wait_ge(*sg["x5_ready"].nth(t + 1))
                turn("x5t", t, lambda h, k: x_tok[:, t + h, k * P:(k + 1) * P])
            for t in range(0, NT, 2):
                pe.wait_ge(*psum.empty("x5t", t))
            pe.wait_ge(*loaded("ld_shared"))
            ps = psum.take(pe, "route")
            for t in range(NT):
                for k in range(KD):
                    ins = mm(ps[:, t * E:(t + 1) * E], x5_feat[:, k, t * P:(t + 1) * P], w_g[:, k, :],
                             start=(k == 0), stop=(k == KD - 1))
            ins.then_inc(*psum.filled.inc())

            def shared_hidden(hf, chunks):
                for c in chunks:
                    c0, m = HC[c]
                    for name, w in (("sh1", ws_1), ("sh3", ws_3)):
                        ps = psum.take(pe, name, hf, c)
                        for k in range(KD):
                            ins = mm(ps[0:m, :], w[:, k, c0:c0 + m], x5_feat[:, k, hf * 512:(hf + 1) * 512],
                                     start=(k == 0), stop=(k == KD - 1))
                        ins.then_inc(*psum.filled.inc())

            def shared_out(hf):
                for c in range(3):
                    pe.wait_ge(*psum.empty("sh3", hf, c))
                for t in range(0, 4, 2):
                    ps = psum.take(pe, "sh2", hf, t)
                    for i in range(2):
                        for c, (c0, m) in enumerate(HC):
                            ins = mm(ps[:, i * D:(i + 1) * D], hs[0:m, c, (t + i) * P:(t + i + 1) * P], ws_2[0:m, c, :],
                                     start=(c == 0), stop=(c == 2))
                    ins.then_inc(*psum.filled.inc())

            shared_hidden(0, (0, 1))
            pe.wait_ge(*sg["oh_ready"].nth(0))
            pe.wait_ge(*loaded("ld_moe1"))
            ps = psum.take(pe, "pos")
            for t in range(NT):
                for j in range(t):
                    mm(ps[:, t * E:(t + 1) * E], ones, oh_bf[:, j, :], start=(j == 0), stop=False)
                ins = mm(ps[:, t * E:(t + 1) * E], tri, oh_bf[:, t, :], start=(t == 0), stop=True)
            ins.then_inc(*psum.filled.inc())
            shared_hidden(0, (2,))
            shared_out(0)
            shared_hidden(1, (0, 1, 2))
            shared_out(1)
            pe.wait_ge(*sg["xd_loaded"].nth(0, 16))
            for e in range(0, E, 2):
                turn("xdt", e, lambda h, k: xd_tok[:, e + h, k * P:(k + 1) * P])
            pe.wait_ge(*loaded("ld_w13"))
            pe.wait_ge(*loaded("ld_w2"))
            for e in range(E + 1):
                if e < E:
                    pe.wait_ge(*psum.empty("xdt", e // 2 * 2))
                    for name, w in (("e1", w_1), ("e3", w_3)):
                        ps = psum.take(pe, name, e)
                        for c, (c0, m) in enumerate(HC):
                            for k in range(KD):
                                ins = mm(ps[0:m, c * P:(c + 1) * P], w[:, e, k, c0:c0 + m],
                                         xd_feat[:, k, e * P:(e + 1) * P], start=(k == 0), stop=(k == KD - 1))
                        ins.then_inc(*psum.filled.inc())
                if e:
                    pe.wait_ge(*psum.empty("e3", e - 1))
                    ps = psum.take(pe, "e2", e - 1)
                    for c, (c0, m) in enumerate(HC):
                        ins = mm(ps[:, 0:D], e_hid[0:m, (e - 1) % 2, c * P:(c + 1) * P], w_2[0:m, e - 1, c, :],
                                 start=(c == 0), stop=(c == 2))
                    ins.then_inc(*psum.filled.inc())

        @block.vector
        def _(eng):
            v = Engine(eng)
            V = nc.vector

            def lk(ins, signal=None):
                ins.then_inc(*(signal or sg["dve_step"]).inc())
                v.wait_ge(*last())

            norms = [0]

            def norm(b, get, done, out_tile=None):
                get()
                i = norms[0]
                norms[0] += 1
                v.wait_ge(*last())
                for h in range(2):
                    V.bn_stats(ln_st[:, h, :], ln_r[:, h, :]).then_inc(*sg["dve_step"].inc())
                v.wait_ge(*last())
                for h in range(2):
                    V.bn_aggr(ln_mv[:, h, :], ln_st[:, h, :]).then_inc(*sg["dve_step"].inc())
                v.wait_ge(*last())
                V.tensor_scalar(ln_var[:, i % 2, :], ln_mv[:, :, 1], EPS, None, ALU.add).then_inc(*sg["var_ready"].inc())
                v.wait_ge(*sg["rstd_ready"].nth(i))
                for h in range(2):
                    dst = x_tok[:, 2 * b + h, :] if out_tile is None else out_tile(h)
                    V.tensor_scalar(dst, ln_r[:, h, :], ln_mv[:, h, 0:1], ln_rs[:, i % 2, h:h + 1],
                                         ALU.subtract, ALU.mult).then_inc(*done.inc())
                v.wait_ge(*last())

            def add_branch(b, name, *use):
                def get():
                    ps = psum.get(v, name, *use)
                    V.tensor_tensor(ln_r[:, :, :].rearrange("p a b -> p (a b)"), ps[:, :],
                                         T2(x_tok, b).rearrange("p a b -> p (a b)"), ALU.add).then_inc(*psum.drain(name, *use).inc())
                return get

            v.wait_ge(*loaded("ld_ssm"))
            v.wait_ge(*sg["a_exp"].nth(0))
            V.tensor_scalar(a_neg[:, :, :], ssm_p[:, :, 7:23], -1.0, None, ALU.mult).then_inc(*sg["a_ready"].inc())
            ssm_flat = {n: t[:, :, :, :].rearrange("p e b s -> p e (b s)") for n, t in (("u", u), ("delta", delta), ("du", du))}
            bcf = tmp_b[0:96, :, :].rearrange("p e s -> p (e s)")[:, 0:2 * S]
            for hf in range(2):
                cols = slice(hf * 512, (hf + 1) * 512)
                v.wait_ge(*psum.empty("xin", hf, 0))
                v.wait_ge(*psum.empty("xin", hf, 1))
                v.wait_ge(*sg["pads_clear"].nth(0))
                if hf:
                    v.wait_ge(*sg["u_ready"].nth(2 * hf - 1))
                for j in range(DC):
                    for et in range(2):
                        o = tmp_a[:, et, :].rearrange("p (b s) -> p b s", b=2)
                        src = x_pad[:, et, :, j:j + S]
                        if j == 0:
                            V.tensor_scalar(o, src, ssm_p[:, et, 0:1], ssm_p[:, et, 4:5], ALU.mult, ALU.add).then_inc(*sg["dve_step"].inc())
                        else:
                            V.scalar_tensor_tensor(o, src, ssm_p[:, et, j:j + 1], o, ALU.mult, ALU.add).then_inc(*(sg["conv_ready"] if j == DC - 1 else sg["dve_step"]).inc())
                    v.wait_ge(*last())
                ps = psum.get(v, "bc", hf)
                parts = bc_parts[:, :, :].rearrange("p b s -> p (b s)")[:, cols]
                lk(V.tensor_copy(bcf, ps[0:96, :]), psum.drain("bc", hf))
                lk(V.tensor_copy(parts, bcf))
                lk(V.tensor_tensor(bcf, bcf, parts, ALU.subtract))
                lk(V.tensor_copy(bf_tmp[0:96, :], bcf))
                lk(V.tensor_tensor(bcf, bcf, bf_tmp[0:96, :], ALU.subtract))
                lk(V.tensor_copy(parts[32:64, :], bf_tmp[32:64, :]))
                lk(V.tensor_copy(parts[64:96, :], bcf[64:96, :]))
                ps = psum.get(v, "dt", hf)
                lk(V.tensor_copy(dt_low[0:DR, cols], ps[0:DR, :]), psum.drain("dt", hf))
                xb = ssm_flat["delta"][:, :, cols]
                for et in range(2):
                    ps = psum.get(v, "dp", hf, et)
                    V.tensor_scalar(xb[:, et, :], ps[:, :], ssm_p[:, et, 5:6], None, ALU.add).then_inc(*psum.drain("dp", hf, et).inc())
                v.wait_ge(*last())
                lk(V.scalar_tensor_tensor(tmp_a[:, :, :], xb, -1.0, xb, ALU.mult, ALU.min), sg["expo_arg"])
                v.wait_ge(*sg["softplus_t"].nth(hf))
                lk(V.tensor_scalar(tmp_a[:, :, :], tmp_b[:, :, :], 1.0, None, ALU.add), sg["softplus_w"])
                v.wait_ge(*sg["softplus_ln"].nth(hf))
                lk(V.scalar_tensor_tensor(tmp_a[:, :, :], tmp_a[:, :, :], -1.0, tmp_b[:, :, :], ALU.add, ALU.subtract))
                lk(V.tensor_tensor(tmp_a[:, :, :], ssm_flat["du"][:, :, cols], tmp_a[:, :, :], ALU.subtract))
                lk(V.scalar_tensor_tensor(xb, xb, 0.0, tmp_a[:, :, :], ALU.max, ALU.add))
                lk(V.tensor_tensor(ssm_flat["du"][:, :, cols], xb, ssm_flat["u"][:, :, cols], ALU.mult), sg["delta_ready"])

            V.memset(s0[:, :, :, :, :], NEG).then_inc(*sg["dve_step"].inc())
            for t in range(NT):
                v.wait_ge(*psum.empty("qk0", t))
                v.wait_ge(*psum.empty("v0", t))
            kv = qkv.rearrange("p (m n) c -> p n m c", n=2)
            v.wait_ge(*last())
            for n in range(2):
                for l in range(4):
                    q = kv[:, n, l, 0:D].unsqueeze(1).broadcast_to([P, l + 1, D])
                    lk(V.tensor_tensor(prod0[:, 0:l + 1, :], q, kv[:, n, 0:l + 1, D:2 * D], ALU.mult))
                    lk(V.tensor_reduce(s0[:, n, l, :, 0:l + 1].rearrange("p h m -> p m h"),
                                       prod0[:, 0:l + 1, :].rearrange("p m (h d) -> p m h d", h=HEADS), AX.X, ALU.add))
            s0f = s0.rearrange("p n l h m -> p (n l h) m") if len(s0.shape) == 5 else s0
            lk(V.tensor_reduce(s0_stat, s0f, AX.X, ALU.max))
            lk(V.tensor_tensor(s0f, s0f, s0_stat.unsqueeze(2).broadcast_to([P, P, 4]), ALU.subtract), sg["s0_arg"])
            v.wait_ge(*sg["s0_exp"].nth(0))
            lk(V.tensor_reduce(s0_stat, s0f, AX.X, ALU.add))
            lk(V.reciprocal(s0_stat, s0_stat))
            lk(V.tensor_tensor(s0f, s0f, s0_stat.unsqueeze(2).broadcast_to([P, P, 4]), ALU.mult))
            for n in range(2):
                for l in range(4):
                    m = l + 1
                    o = prod0.rearrange("p a b -> p (a b)")[:, 0:D * m].rearrange("p (h d m) -> p h d m", h=HEADS, m=m)
                    pr = s0[:, n, l, :, 0:m].unsqueeze(2).broadcast_to([P, HEADS, DH, m])
                    vv = kv[:, n, 0:m, 2 * D:3 * D].rearrange("p m (h d) -> p h d m", h=HEADS)
                    lk(V.tensor_tensor(o, pr, vv, ALU.mult))
                    lk(V.tensor_reduce(kv[:, n, l, 0:D].rearrange("p (h d) -> p h d", h=HEADS), o, AX.X, ALU.add),
                       sg["o0_ready"] if l == 3 else None)
            v.wait_ge(*loaded("ld_x"))
            for b in range(B):
                norm(b, add_branch(b, "proj0", b), sg["x1_ready"])

            def ssm_core(b):
                v.wait_ge(*sg["delta_ready"].nth(b // 2))
                v.wait_ge(*sg["decay_clear"].nth(b))
                marks = {}
                for i in range(DS + 2):
                    if i < DS:
                        ps = psum.get(v, "bcn", b, i)
                        if i >= NB:
                            v.wait_ge(*marks["scan", i - NB])
                        V.tensor_tensor(
                            drive[:, i % NB, :, :], du[:, :, b, :], ps[:, 0:S].unsqueeze(1).broadcast_to([P, 2, S]),
                            ALU.mult).then_inc(*sg["dve_step"].inc())
                        marks["drive", i] = last()
                    if 1 <= i <= DS:
                        n = i - 1
                        v.wait_ge(*sg["decay_ready"].nth(2 * (b * DS + n) + 1))
                        v.wait_ge(*marks["drive", n])
                        if n >= NB:
                            v.wait_ge(*marks["seen", n - NB])
                        V.tensor_tensor_scan(
                            state[:, n % NB, :, :].rearrange("p e s -> p (e s)"),
                            decay[:, n % NB, :, :].rearrange("p e s -> p (e s)"),
                            drive[:, n % NB, :, :].rearrange("p e s -> p (e s)"), 0.0, ALU.mult, ALU.add).then_inc(*sg["decay_used"].inc())
                        marks["scan", n] = last()
                    if i >= 2:
                        n = i - 2
                        ps = psum.get(v, "bcn", b, n)
                        v.wait_ge(*marks["scan", n])
                        k = b * DS + n
                        if n >= NB:
                            v.wait_ge(*sg["seen_used"].nth(b * (DS - 1) + n - NB))
                        elif b:
                            v.wait_ge(*y_psum.full("y", b - 1))
                        V.tensor_tensor(
                            seen_c[:, n % NB, :, :], state[:, n % NB, :, :],
                            ps[:, S:2 * S].unsqueeze(1).broadcast_to([P, 2, S]), ALU.mult).then_inc(*psum.drain("bcn", b, n).inc())
                        marks["seen", n] = last()

            def ssm_tail(b):
                ps = y_psum.get(v, "y", b)
                if b:
                    v.wait_ge(*psum.full("yt", b - 1))
                for et in range(2):
                    V.scalar_tensor_tensor(y_gate[:, et, :], u[:, et, b, :], ssm_p[:, et, 6:7],
                                                ps[:, et * S:(et + 1) * S], ALU.mult, ALU.add).then_inc(*(y_psum.drain("y", b) if et else sg["dve_step"]).inc())
                v.wait_ge(*last())
                v.wait_ge(*sg["silu_z_ready"].nth(0))
                lk(V.tensor_tensor(y_gate[:, :, :], y_gate[:, :, :], T2(silu_z, b), ALU.mult), sg["y_ready"])
                norm(b, add_branch(b, "yt", b), sg["x2_ready"])

            def first_of_max(g, score, hit, stat, rev, n, signal=None):
                shape = list(g.shape)
                lk(V.tensor_reduce(stat, g, AX.X, ALU.max))
                lk(V.tensor_tensor(hit, g, stat.unsqueeze(2).broadcast_to(shape), ALU.is_equal))
                lk(V.tensor_tensor(score, hit, rev.unsqueeze(1).broadcast_to(shape), ALU.mult))
                lk(V.tensor_reduce(stat, score, AX.X, ALU.max))
                lk(V.tensor_tensor(hit, score, stat.unsqueeze(2).broadcast_to(shape), ALU.is_equal), signal)

            def moe0(b):
                v.wait_ge(*loaded("ld_moe0"))
                v.wait_ge(*loaded("ld_const"))
                G = [g8[:, i, :, :] for i in range(10)]
                stat = small[:, 8:10]
                if b:
                    v.wait_ge(*psum.full("wt0", b - 1))
                ps = psum.get(v, "gate0", b)
                lk(V.scalar_tensor_tensor(G[0], ps[:, 0:2 * E].rearrange("p (h e) -> p h e", h=2), float(BONUS),
                                          b_r[:, :].unsqueeze(1).broadcast_to([P, 2, E]), ALU.add, ALU.add),
                   psum.drain("gate0", b))
                lk(V.tensor_reduce(stat, G[0], AX.X, ALU.max))
                lk(V.tensor_tensor(G[0], G[0], stat.unsqueeze(2).broadcast_to([P, 2, E]), ALU.subtract), sg["gate_arg"])
                v.wait_ge(*sg["gate_exp"].nth(b))
                first_of_max(G[1], G[2], G[3], stat, eid_rev[:, :], 2)
                lk(V.scalar_tensor_tensor(G[4], G[3], -4.0, G[1], ALU.mult, ALU.add))
                first_of_max(G[4], G[5], G[6], stat, eid_rev[:, :], 2)
                lk(V.tensor_tensor(G[7], G[3], G[6], ALU.add))
                lk(V.tensor_tensor(G[8], G[7], G[1], ALU.mult))
                lk(V.tensor_reduce(stat, G[8], AX.X, ALU.add))
                lk(V.reciprocal(stat, stat))
                lk(V.tensor_tensor(G[9], G[8], stat.unsqueeze(2).broadcast_to([P, 2, E]), ALU.mult), sg["w_ready"])
                ps = psum.get(v, "wt0", b)
                V.tensor_copy(w_e_t[:, :], ps[0:E, 0:S]).then_inc(*psum.drain("wt0", b).inc())
                v.wait_ge(*psum.empty("hid0", b))
                ps = psum.get(v, "spread0", b)
                lk(V.tensor_tensor(h_w[:, :], h_relu[:, :], ps[:, 0:S], ALU.mult), psum.drain("spread0", b))
                norm(b, add_branch(b, "out0", b), sg["x3_ready"])

            def attn1(b):
                v.wait_ge(*loaded("ld_rope"))
                for h in range(2):
                    ps = psum.get(v, "qk1", b, h)[:, :].rearrange("p (g i c) -> p g i c", i=8, c=2)
                    dst = qk_rot[:, h, :].rearrange("p (g i c) -> p g i c", i=8, c=2)
                    tb = rot_b.rearrange("p (g i c) -> p g i c", i=8, c=2)
                    cos, nsin, sin = (rope[:, h, i, :].unsqueeze(1).broadcast_to([P, 32, 8]) for i in range(3))
                    if b and not h:
                        v.wait_ge(*psum.full("k1t", b - 1))
                    V.tensor_tensor(dst[:, :, :, 0], ps[:, :, :, 0], cos, ALU.mult).then_inc(*sg["dve_step"].inc())
                    V.tensor_tensor(dst[:, :, :, 1], ps[:, :, :, 1], cos, ALU.mult).then_inc(*sg["dve_step"].inc())
                    V.tensor_tensor(tb[:, :, :, 0], ps[:, :, :, 1], nsin, ALU.mult).then_inc(*sg["dve_step"].inc())
                    lk(V.tensor_tensor(tb[:, :, :, 1], ps[:, :, :, 0], sin, ALU.mult), psum.drain("qk1", b, h))
                    lk(V.tensor_tensor(qk_rot[:, h, :], qk_rot[:, h, :], rot_b, ALU.add), sg["qk_ready"])
                v.wait_ge(*psum.empty("k1t", b))
                for h in range(HEADS):
                    if b:
                        v.wait_ge(*psum.full("st1", b - 1, 3))
                    V.tensor_scalar(k_head[:, h, :], k_feat[:, h // 8, :], head_of[:, h % 8:h % 8 + 1], None,
                                         ALU.mult).then_inc(*sg["khead_ready"].inc())
                if not b:
                    V.memset(nm_parts[:, :, :], 0.0).then_inc(*sg["dve_step"].inc())
                for g in range(4):
                    ps = psum.get(v, "s1a", b, g)
                    V.tensor_reduce(neg_max[:, 0, 4 * g:4 * g + 4], ps[:, :].rearrange("p (h k) -> p h k", h=4),
                                         AX.X, ALU.max, negate=True).then_inc(*psum.drain("s1a", b, g).inc())
                for g in range(8):
                    ps = psum.get(v, "s1b", b, g)
                    V.tensor_reduce(neg_max[:, 1, 2 * g:2 * g + 2], ps[:, :].rearrange("p (h k) -> p h k", h=2),
                                         AX.X, ALU.max, negate=True).then_inc(*psum.drain("s1b", b, g).inc())
                v.wait_ge(*last())
                if b:
                    v.wait_ge(*psum.full("nm1", b - 1))
                src = neg_max
                for i in range(3):
                    part = nm_parts[:, :, 32 * i:32 * i + HEADS]
                    lk(V.tensor_copy(part, src), sg["nm_ready"] if i == 2 else None)
                    if i < 2:
                        lk(V.tensor_tensor(nm_res, src, part, ALU.subtract))
                        src = nm_res
                for h in range(2):
                    ps = psum.get(v, "on1", b, h)[:, :].rearrange("p (h c) -> p h c", h=HEADS)
                    if b and not h:
                        v.wait_ge(*psum.full("o1t", b - 1))
                    lk(V.reciprocal(o_den[:, h, :], ps[:, :, DH]))
                    lk(V.tensor_tensor(o_norm[:, h, :].rearrange("p (h d) -> p h d", h=HEADS), ps[:, :, 0:DH],
                                       o_den[:, h, :].unsqueeze(2).broadcast_to([P, HEADS, DH]), ALU.mult),
                       psum.drain("on1", b, h))
                norm(b, add_branch(b, "proj1", b), sg["x4_ready"])

            def xattn(b):
                if not b:
                    v.wait_ge(*loaded("ld_xattn"))
                    lk(V.tensor_scalar(mask_add.rearrange("p b s -> p (b s)"), mask_raw, -NEG, NEG, ALU.mult, ALU.add))
                    lk(V.tensor_reduce(mask_any, mask_raw.rearrange("p (b s) -> p b s", b=B), AX.X, ALU.max))
                marks = {}
                for i in range(XH + 2):
                    if i < XH:
                        ps = psum.get(v, "sx", b, i)
                        j = i % NX
                        if i >= NX:
                            v.wait_ge(*psum.full("pxt", b, i - NX))
                        for qt in range(2):
                            V.tensor_tensor_reduce(px[:, j, qt, :], ps[:, qt * S:(qt + 1) * S], mask_add[:, b, :],
                                                        XSCALE, -3e38, ALU.add, ALU.max, x_max[:, j, qt:qt + 1]).then_inc(*(psum.drain("sx", b, i) if qt else sg["dve_step"]).inc())
                        v.wait_ge(*last())
                        V.tensor_scalar(x_nmax[:, j, :], x_max[:, j, :], -1.0, None, ALU.mult).then_inc(*sg["smax_ready"].inc())
                    if 1 <= i < XH + 1:
                        h = i - 1
                        j = h % NX
                        v.wait_ge(*sg["sexp_ready"].nth(2 * (b * XH + h) + 1))
                        lk(V.reciprocal(x_inv[:, j, :], x_sum[:, j, :]))
                        for qt in range(2):
                            V.tensor_scalar(px[:, j, qt, :], px[:, j, qt, :], x_inv[:, j, qt:qt + 1],
                                                 mask_any[:, b:b + 1], ALU.mult, ALU.mult).then_inc(*sg["pn_ready"].inc())
                    if i >= 2:
                        h = i - 2
                        ps = psum.get(v, "pxt", b, h)
                        if h >= 2:
                            v.wait_ge(*psum.full("pvx", b, h - 2))
                        V.tensor_copy(px_t[:, h % 2, :, :].rearrange("p a b -> p (a b)"), ps[:, :]).then_inc(*psum.drain("pxt", b, h).inc())

                def get():
                    for h in range(2):
                        ps = o_psum.get(v, "ox", b, h)
                        V.tensor_tensor(ln_r[:, h, :], ps[:, 0:D], x_tok[:, 2 * b + h, :], ALU.add).then_inc(*o_psum.drain("ox", b, h).inc())
                norm(b, get, sg["x5_ready"])

            for b in range(B):
                ssm_core(b)
                ssm_tail(b)
                moe0(b)
                attn1(b)
                xattn(b)

            RR = [r8[:, i, :, :] for i in range(8)]
            Q1 = [r1[:, i, :] for i in range(8)]
            v.wait_ge(*loaded("ld_moe1"))
            v.wait_ge(*o_psum.empty("ox", B - 1, 1))
            ps = psum.get(v, "route")
            lg = ps[:, 0:NT * E].rearrange("p (t e) -> p t e", t=NT)
            lk(V.tensor_reduce(Q1[0], lg, AX.X, ALU.max))
            lk(V.tensor_tensor(RR[0], lg, Q1[0].unsqueeze(2).broadcast_to([P, NT, E]), ALU.subtract), psum.drain("route"))
            v.wait_ge(*sg["route_exp"].nth(0))
            lk(V.tensor_reduce(Q1[1], RR[1], AX.X, ALU.add))
            lk(V.reciprocal(Q1[1], Q1[1]))
            lk(V.tensor_tensor(RR[1], RR[1], Q1[1].unsqueeze(2).broadcast_to([P, NT, E]), ALU.mult))
            first_of_max(RR[1], RR[2], RR[3], Q1[2], eid_rev[:, :], NT)
            lk(V.tensor_copy(oh_bf[:, :, :], RR[3]), sg["oh_ready"])
            lk(V.tensor_tensor(RR[4], RR[3], RR[1], ALU.mult))
            lk(V.tensor_reduce(Q1[3], RR[4], AX.X, ALU.add))
            ps = psum.get(v, "pos")
            lk(V.tensor_tensor(RR[5], RR[3], ps[:, 0:NT * E].rearrange("p (t e) -> p t e", t=NT), ALU.mult),
               psum.drain("pos"))
            lk(V.tensor_reduce(Q1[4], RR[5], AX.X, ALU.add))
            lk(V.tensor_tensor(RR[6], RR[3], ebase.unsqueeze(1).broadcast_to([P, NT, E]), ALU.mult))
            lk(V.tensor_reduce(Q1[5], RR[6], AX.X, ALU.add))
            lk(V.tensor_tensor(Q1[5], Q1[5], Q1[4], ALU.add))
            lk(V.tensor_scalar(Q1[6], Q1[4], float(CAP), None, ALU.is_le))
            lk(V.tensor_tensor(Q1[3], Q1[3], Q1[6], ALU.mult))
            lk(V.tensor_tensor(Q1[5], Q1[5], Q1[6], ALU.mult))
            lk(V.tensor_copy(slot_u[:, 1, :], Q1[5]))
            lk(V.tensor_tensor(Q1[7], dump, Q1[6], ALU.mult))
            lk(V.tensor_tensor(Q1[7], dump, Q1[7], ALU.subtract))
            lk(V.tensor_tensor(Q1[7], Q1[7], Q1[5], ALU.add))
            lk(V.tensor_copy(slot_u[:, 0, :], Q1[7]), sg["slots_ready"])

            def shared(hf):
                for c, (_, m) in enumerate(HC):
                    v.wait_ge(*psum.empty("sh1", hf, c))
                    ps = psum.get(v, "sh3", hf, c)
                    lk(V.tensor_tensor(hs[0:m, c, :], hs[0:m, c, :], ps[0:m, :], ALU.mult), psum.drain("sh3", hf, c))

            def shared_add(hf):
                for t in range(0, 4, 2):
                    ps = psum.get(v, "sh2", hf, t)
                    xt = x_tok[:, 4 * hf + t:4 * hf + t + 2, :].rearrange("p a b -> p (a b)")
                    V.tensor_tensor(xt, xt, ps[:, :], ALU.add).then_inc(*psum.drain("sh2", hf, t).inc())

            shared(0)
            v.wait_ge(*sg["xd_scattered"].nth(NT - 1, 16))
            shared_add(0)
            shared(1)
            shared_add(1)
            for e in range(0, E, 2):
                ps = psum.get(v, "xdt", e)
                V.tensor_copy(xd_feat[:, :, e * P:(e + 2) * P], ps[:, :].rearrange("p (k t) -> p k t", k=KD)).then_inc(*psum.drain("xdt", e).inc())
            for e in range(E):
                ps = psum.get(v, "e3", e)
                v.wait_ge(*psum.empty("e1", e))
                if e >= 2:
                    v.wait_ge(*psum.full("e2", e - 2))
                V.tensor_tensor(e_hid[:, e % 2, 0:2 * P], e_gate[:, 0:2 * P], ps[:, 0:2 * P], ALU.mult).then_inc(*sg["dve_step"].inc())
                V.tensor_tensor(e_hid[0:96, e % 2, 2 * P:3 * P], e_gate[0:96, 2 * P:3 * P], ps[0:96, 2 * P:3 * P],
                                     ALU.mult).then_inc(*psum.drain("e3", e).inc())
            v.wait_ge(*sg["oe_gathered"].nth(NT - 1, 16))
            for b in range(B):
                def get():
                    for h in range(2):
                        t = 2 * b + h
                        V.scalar_tensor_tensor(ln_r[:, h, :], og[:, t, :], Q1[3][:, t:t + 1], x_tok[:, t, :],
                                                    ALU.mult, ALU.add).then_inc(*sg["dve_step"].inc())
                norm(b, get, sg["final_ready"])

        @block.scalar
        def _(eng):
            act = Engine(eng)
            A = nc.scalar.activation

            def copy(dst, src, signal=None):
                return A(dst, src, ACT.Copy).then_inc(*(signal or sg["act_step"]).inc())

            def drain(dst, name, *use, cut=512, rows=P):
                ps = psum.get(act, name, *use)
                src = ps[0:rows, 0:cut]
                if len(dst.shape) == 3:
                    src = src.rearrange("p (a b) -> p a b", a=dst.shape[1])
                elif len(dst.shape) == 4:
                    src = src.rearrange("p (a b c) -> p a b c", a=dst.shape[1], b=dst.shape[2])
                return copy(dst, src, psum.drain(name, *use))

            act.wait_ge(*loaded("ld_ssm"))
            A(ssm_p[:, :, 7:23], ssm_p[:, :, 7:23], ACT.Exp).then_inc(*sg["a_exp"].inc())
            act.wait_ge(*sg["pads_clear"].nth(0))

            def xin(hf):
                for et in range(2):
                    if hf:
                        act.wait_ge(*sg["conv_ready"].nth(1))
                    drain(x_pad[:, et, :, DC - 1:], "xin", hf, et)

            def silu_u(hf):
                for et in range(2):
                    act.wait_ge(*sg["conv_ready"].nth(2 * hf + et))
                    A(u[:, et, 2 * hf:2 * hf + 2, :].rearrange("p b s -> p (b s)"), tmp_a[:, et, :], ACT.Silu).then_inc(*sg["u_ready"].inc())

            def qkv0(t):
                drain(qkv[:, t, 0:512], "qk0", t)
                drain(qkv[:, t, 512:768], "v0", t, cut=256)

            def softplus(hf):
                cols = slice(hf * 512, (hf + 1) * 512)
                act.wait_ge(*sg["expo_arg"].nth(hf))
                A(tmp_b[:, :, :], tmp_a[:, :, :], ACT.Exp).then_inc(*sg["softplus_t"].inc())
                act.wait_ge(*sg["softplus_w"].nth(hf))
                A(du[:, :, :, :].rearrange("p e b s -> p e (b s)")[:, :, cols], tmp_a[:, :, :], ACT.Ln).then_inc(*sg["softplus_ln"].inc())

            xin(0)
            xin(1)
            for t in range(4):
                qkv0(t)
            silu_u(0)
            qkv0(4)
            qkv0(5)
            softplus(0)
            silu_u(1)
            qkv0(6)
            qkv0(7)
            softplus(1)
            act.wait_ge(*sg["s0_arg"].nth(0))
            s0f = s0.rearrange("p n l h m -> p (n l h m)")
            A(s0f, s0f, ACT.Exp, scale=float(DH) ** -0.5).then_inc(*sg["s0_exp"].inc())
            for t in range(0, NT, 2):
                act.wait_ge(*psum.full("v0", NT - 1))
                drain(o0_feat[:, :, t * P:(t + 2) * P], "o0t", t)
            act.wait_ge(*sg["x1_ready"].nth(NT - 1))
            A(silu_z[:, :, :].rearrange("p a b -> p (a b)"), x_tok[:, :, :].rearrange("p a b -> p (a b)"), ACT.Silu).then_inc(*sg["silu_z_ready"].inc())

            def ssm_core(b):
                act.wait_ge(*sg["a_ready"].nth(0))
                act.wait_ge(*sg["delta_ready"].nth(b // 2))
                for n in range(DS):
                    k = b * DS + n
                    if k >= NB:
                        act.wait_ge(*sg["decay_used"].nth(k - NB))
                    for et in range(2):
                        A(decay[:, n % NB, et, 1:], delta[:, et, b, 1:], ACT.Exp, scale=a_neg[:, et, n:n + 1]).then_inc(*sg["decay_ready"].inc())

            def moe0(b):
                drain(x_feat[:, :, :], "x2t", b)
                act.wait_ge(*sg["gate_arg"].nth(b))
                A(g8[:, 1, :, :], g8[:, 0, :, :], ACT.Exp).then_inc(*sg["gate_exp"].inc())
                ps = psum.get(act, "hid0", b)
                A(h_relu[:, :], ps[:, 0:S], ACT.Relu, bias=b_d[:, 0:1]).then_inc(*psum.drain("hid0", b).inc())

            def attn1(b):
                act.wait_ge(*psum.full("hid0", b))
                drain(x_feat[:, :, :], "x3t", b)
                ps = psum.get(act, "v1", b)
                act.wait_ge(*sg["ones_ready"].nth(0))
                if b:
                    act.wait_ge(*psum.full("ov1", b - 1, 1))
                for h in range(2):
                    A(v_aug[:, h, :, 0:DH], ps[:, h * D:(h + 1) * D].rearrange("p (h d) -> p h d", h=HEADS), ACT.Copy).then_inc(*(psum.drain("v1", b) if h else sg["act_step"]).inc())
                drain(q_feat, "q1t", b)
                drain(k_feat, "k1t", b)
                ps = psum.get(act, "nm1", b)
                copy(nm_feat[0:96, :], ps[:, :].bitcast(BF16)[0:96, 0:S], psum.drain("nm1", b))
                for g in range(4):
                    for name, i in (("st0", 2 * g), ("st0", 2 * g + 1), ("st1", g)):
                        ps = psum.get(act, name, b, i)
                        dst = p_t0[:, 2 * i:2 * i + 2, :] if name == "st0" else p_t1[:, 4 * i:4 * i + 4, :]
                        A(dst.rearrange("p a b -> p (a b)"), ps[:, :], ACT.Exp, scale=float(DH) ** -0.5).then_inc(*psum.drain(name, b, i).inc())
                    if g >= 2:
                        drain(o_heads[:, 2 * (g - 2):2 * (g - 2) + 2, :], "ov1", b, g - 2)
                drain(o_feat, "o1t", b)

            def xattn(b):
                for g in range(0, XKV, 2):
                    drain(kx_feat[:, g:g + 2, :], "kx", b, g)
                for kt in range(2):
                    for i in range(2):
                        drain(vx_tok[:, kt, i * 512:(i + 1) * 512], "vx", b, kt, i)
                drain(x_feat[:, :, :], "x4t", b)
                for i in range(XH + 3):
                    if i < XH:
                        if i >= 2:
                            act.wait_ge(*psum.full("sx", b, i - 2))
                        drain(qx_feat[:, i % 2, :], "qx", b, i, cut=S)
                    if 1 <= i < XH + 1:
                        h = i - 1
                        j = h % NX
                        act.wait_ge(*sg["smax_ready"].nth(b * XH + h))
                        for qt in range(2):
                            A(px[:, j, qt, :], px[:, j, qt, :], ACT.Exp, bias=x_nmax[:, j, qt:qt + 1],
                                     accum_out=x_sum[:, j, qt:qt + 1]).then_inc(*sg["sexp_ready"].inc())
                    if i >= 3:
                        h = i - 3
                        if h >= 2:
                            act.wait_ge(*sg["ox_used"].nth(b * (XH - 1) + h - 2))
                        drain(ox_feat[:, h % 2, :], "pvx", b, h, cut=S)

            for b in range(B):
                ssm_core(b)
                moe0(b)
                attn1(b)
                xattn(b)

            act.wait_ge(*o_psum.empty("ox", B - 1, 1))
            for t in range(0, NT, 2):
                drain(x5_feat[:, :, t * P:(t + 2) * P], "x5t", t)
            act.wait_ge(*psum.empty("route"))
            A(r8[:, 1, :, :], r8[:, 0, :, :], ACT.Exp).then_inc(*sg["route_exp"].inc())

            def shared(hf):
                for c, (_, m) in enumerate(HC):
                    ps = psum.get(act, "sh1", hf, c)
                    if hf:
                        act.wait_ge(*psum.full("sh2", 0, 2))
                    A(hs[0:m, c, :], ps[0:m, :], ACT.Silu).then_inc(*psum.drain("sh1", hf, c).inc())

            shared(0)
            shared(1)

            def expert_out(e):
                drain(oe[:, e, :], "e2", e, cut=D)

            for e in range(E):
                ps = psum.get(act, "e1", e)
                if e:
                    act.wait_ge(*psum.empty("e3", e - 1))
                A(e_gate[:, 0:2 * P], ps[:, 0:2 * P], ACT.Silu).then_inc(*sg["act_step"].inc())
                A(e_gate[0:96, 2 * P:3 * P], ps[0:96, 2 * P:3 * P], ACT.Silu).then_inc(*psum.drain("e1", e).inc())
                if e:
                    expert_out(e - 1)
            expert_out(E - 1)

        @block.gpsimd
        def _(eng):
            pool = Engine(eng)
            G = nc.gpsimd
            G.memset(x_pad[:, :, :, 0:DC - 1], 0.0).then_inc(*sg["pool_step"].inc())
            G.memset(half_neg[:, :], -0.5).then_inc(*sg["pool_step"].inc())
            G.memset(small[:, :], 0.0).then_inc(*sg["pads_clear"].inc())
            pool.wait_ge(*last())

            for i in range(4 + 4 * B):
                pool.wait_ge(*sg["var_ready"].nth(i))
                G.tensor_tensor(ln_rs[:, i % 2, :], ln_var[:, i % 2, :], half_neg[:, :], ALU.pow).then_inc(*sg["rstd_ready"].inc())
                if i == 3:
                    pool.wait_ge(*sg["x1_ready"].nth(NT - 1))
                    pool.wait_ge(*sg["delta_ready"].nth(1))
                    G.memset(v_aug[:, :, :, DH:], 0.0).then_inc(*sg["pool_step"].inc())
                    pool.wait_ge(*last())
                    G.memset(v_aug[:, :, :, DH:DH + 1], 1.0).then_inc(*sg["ones_ready"].inc())
                b = (i - 6) // 4 + 1
                if i == 3 or (i - 6) % 4 == 0 and i > 3 and b < B:
                    if i > 3:
                        pool.wait_ge(*sg["x4_ready"].nth(2 * b - 1))
                    G.memset(decay[:, :, :, 0:1], 0.0).then_inc(*sg["decay_clear"].inc())
            pool.wait_ge(*sg["slots_ready"].nth(0))
            pool.wait_ge(*sg["zeroed"].nth(0, 16))
            for t in range(NT):
                G.indirect_dma_start(
                    xd_dram, bass.IndirectOffsetOnAxis(ap=slot_u[:, 0, t:t + 1], axis=0), x_tok[:, t, :], None).then_inc(*sg["xd_scattered"].inc(16))
            pool.wait_ge(*sg["oe_stored"].nth(E - 1, 16))
            for t in range(NT):
                G.indirect_dma_start(
                    og[:, t, :], None, oe_dram, bass.IndirectOffsetOnAxis(ap=slot_u[:, 1, t:t + 1], axis=0)).then_inc(*sg["oe_gathered"].inc(16))
            for b in range(B):
                i = 4 + 4 * B + b
                pool.wait_ge(*sg["var_ready"].nth(i))
                G.tensor_tensor(ln_rs[:, i % 2, :], ln_var[:, i % 2, :], half_neg[:, :], ALU.pow).then_inc(*sg["rstd_ready"].inc())

        @block.sync
        def _(eng):
            sp = Engine(eng)

            def load(dst, src, name):
                eng.dma_start(dst, src).then_inc(*sg[name].inc(16))

            load(in_pt, a["in_pt"], "ld_ssm")
            load(ctx_t[:, :], a["ctx_t"], "ld_ssm")
            load(ssm_p[:, :, :], a["ssm_p"], "ld_ssm")
            load(x_pt, a["x_pt"], "ld_ssm")
            load(dt_pt, a["dt_pt"], "ld_ssm")
            load(x0_feat, a["x_t"], "ld_attn0")
            load(w_qkv, a["w_qkv"], "ld_attn0")
            load(w_o0, a["w_o0"], "ld_attn0")
            load(row_pick[:, :, :], a["row_pick"], "ld_const")
            load(ident[:, :], a["ident"], "ld_const")
            load(ident_bf[:, :], a["ident_bf"], "ld_const")
            load(mask_qk[:, :], a["mask_qk"], "ld_const")
            load(mask_kq[:, :], a["mask_kq"], "ld_const")
            load(eid_rev[:, :], a["eid_rev"], "ld_const")
            load(x_tok[:, :, :], a["x"], "ld_x")
            load(w_r[:, :, :], a["w_r"], "ld_moe0")
            load(b_r[:, :], a["b_r"].partition_broadcast(P), "ld_moe0")
            load(w_d[:, :, :], a["w_d"], "ld_moe0")
            load(b_d[:, :], a["b_d"], "ld_moe0")
            load(w_u[:, :], a["w_u"], "ld_moe0")
            load(b_u[:, :], a["b_u"], "ld_moe0")
            load(spread[:, :], a["spread"], "ld_moe0")
            load(wx_k, a["wx_k"], "ld_xattn")
            load(wx_v, a["wx_v"], "ld_xattn")
            load(wx_q, a["wx_q"], "ld_xattn")
            load(wx_o, a["wx_o"], "ld_xattn")
            load(mask_raw, a["mask"].partition_broadcast(P), "ld_xattn")
            load(rope[:, :, :, :], a["rope"], "ld_rope")
            load(head_of[:, :], a["head_of"], "ld_rope")
            load(xd_dram[0:T, :], a["zeros"], "zeroed")
            sp.wait_ge(*sg["x1_ready"].nth(NT - 1))
            sp.wait_ge(*sg["delta_ready"].nth(1))
            load(w_qk1, a["w_qk1"], "ld_attn1")
            load(w_v1, a["w_v1"], "ld_attn1")
            load(w_o1, a["w_o1"], "ld_attn1")
            sp.wait_ge(*sg["x4_ready"].nth(2 * B - 1))
            load(w_1, a["w_1"], "ld_w13")
            load(w_3, a["w_3"], "ld_w13")
            sp.wait_ge(*o_psum.empty("ox", B - 1, 1))
            sp.wait_ge(*sg["x5_ready"].nth(2 * B - 1))
            load(w_g, a["w_g"], "ld_shared")
            load(ws_1, a["ws_1"], "ld_shared")
            load(ws_3, a["ws_3"], "ld_shared")
            load(ws_2, a["ws_2"], "ld_shared")
            load(tri, a["tri"], "ld_moe1")
            load(ones, a["ones"], "ld_moe1")
            load(dump, a["dump"], "ld_moe1")
            load(ebase, a["ebase"], "ld_moe1")
            load(w_2, a["w_2"], "ld_w2")
            sp.wait_ge(*sg["xd_scattered"].nth(NT - 1, 16))
            load(xd_tok, xd_dram[0:T, :].rearrange("(e p) d -> p e d", p=P), "xd_loaded")
            for e in range(E):
                sp.wait_ge(*psum.empty("e2", e))
                load(oe_dram[e * P:(e + 1) * P, :], oe[:, e, :], "oe_stored")
            for t in range(NT):
                sp.wait_ge(*sg["final_ready"].nth(t))
                load(out[t * P:(t + 1) * P, :], x_tok[:, t, :], "out_stored")
            sp.wait_ge(*sg["out_stored"].nth(NT - 1, 16))
            assert all(sg[n].n == 16 * k for n, k in loads.items())


_SHAPE_CONSTANTS = ("row_pick", "ident", "ident_bf", "mask_qk", "mask_kq", "eid_rev", "spread", "rope", "head_of",
                    "tri", "ones", "dump", "ebase", "zeros")


def shape_constants():
    bf = mybir.dt.np(BF16)
    i = np.arange(P)
    pick = np.zeros((96, 32, P), np.float32)
    for part in range(3):
        for n in range(32):
            pick[32 * part + n, n, :] = 1.0
    c = {"row_pick": pick.astype(bf), "ident": np.eye(P, dtype=np.float32), "ident_bf": np.eye(P).astype(bf)}
    c["mask_qk"] = np.where(i[None, :] > i[:, None], NEG, 0.0).astype(bf)
    c["mask_kq"] = np.ascontiguousarray(c["mask_qk"].T)
    c["eid_rev"] = np.tile(np.arange(E, 0, -1, dtype=np.float32), (P, 1))
    c["spread"] = (np.arange(P)[None, :] // R == np.arange(E)[:, None]).astype(np.float32)
    freq = (1.0 / 10000.0 ** (np.arange(0, DH, 2, dtype=np.float32) / DH)).astype(np.float32)
    ang = np.outer(np.arange(S, dtype=np.float32), freq).astype(np.float32)
    r = np.stack([np.cos(ang), -np.sin(ang), np.sin(ang)], 1).astype(np.float32)
    c["rope"] = np.ascontiguousarray(r.reshape(2, P, 3, 8).transpose(1, 0, 2, 3))
    c["head_of"] = (i[:, None] // DH == np.arange(8)[None, :]).astype(np.float32)
    c["tri"] = (i[:, None] <= i[None, :]).astype(bf)
    c["ones"] = np.ones((P, P)).astype(bf)
    c["dump"] = (T + np.arange(NT)[None, :] * P + i[:, None]).astype(np.float32)
    c["ebase"] = np.tile(np.arange(E, dtype=np.float32) * CAP - 1, (P, 1))
    c["zeros"] = np.zeros((T, D), np.float32)
    return c


def kernel(**inputs):
    import concourse.bacc as bacc
    from concourse.bass_utils import run_bass_kernel_spmd as run

    w = {k: np.asarray(x) for k, x in inputs.items()}

    def tiles(m, p=P):
        return m.reshape(m.shape[0] // p, p, *m.shape[1:]).swapaxes(0, 1)

    def hid_rows(m):
        pad = np.zeros((*m.shape[:-2], 3 * P - HID, m.shape[-1]), m.dtype)
        m = np.concatenate([m, pad], -2)
        m = m.reshape(*m.shape[:-2], 3, P, m.shape[-1])
        return np.moveaxis(m, -2, 0)

    xp = w["L0_xattn_x_proj_w"]
    bc_rows = xp[DR:]
    x = w["x"].reshape(T, D)
    arrays = dict(
        x=tiles(x), x_t=tiles(x.T), ctx_t=w["ctx_1024"].reshape(T, CTX).T,
        mask=w["mask_BxS2_bf1"].reshape(T).view(np.uint8),
        w_qkv=tiles(w["L0_attn_weight_qkv"].T), w_o0=tiles(w["L0_attn_weight_out"].T),
        in_pt=w["L0_xattn_in_proj_w"].T,
        x_pt=tiles(np.concatenate([bc_rows, bc_rows, bc_rows, xp[:DR]], 0).T),
        dt_pt=w["L0_xattn_dt_proj_w"].T,
        ssm_p=tiles(np.concatenate([w["L0_xattn_conv_w"], w["L0_xattn_conv_b"][:, None],
                                    w["L0_xattn_dt_proj_b"][:, None], w["L0_xattn_D"][:, None],
                                    w["L0_xattn_A_log"]], 1)),
        w_r=tiles(w["L0_ffn_Wr"]), b_r=w["L0_ffn_br"],
        w_d=tiles(w["L0_ffn_Wd"].transpose(1, 0, 2).reshape(D, E * R)),
        b_d=w["L0_ffn_bd"].reshape(P, 1), w_u=w["L0_ffn_Wu"].reshape(E * R, D), b_u=w["L0_ffn_bu"],
        w_qk1=tiles(np.concatenate([w["L1_attn_Wq"].T, w["L1_attn_Wk"].T], 1)),
        w_v1=tiles(w["L1_attn_Wv"].T), w_o1=tiles(w["L1_attn_Wo"].T),
        wx_q=tiles(w["L1_xattn_Wq"]), wx_k=w["L1_xattn_Wk"], wx_v=w["L1_xattn_Wv"], wx_o=tiles(w["L1_xattn_Wo"]),
        w_g=tiles(w["L1_ffn_Wg"]),
        w_1=w["L1_ffn_W1"].reshape(E, KD, P, HID).transpose(2, 0, 1, 3),
        w_3=w["L1_ffn_W3"].reshape(E, KD, P, HID).transpose(2, 0, 1, 3),
        w_2=hid_rows(w["L1_ffn_W2"]), ws_1=tiles(w["L1_ffn_sw1"]), ws_3=tiles(w["L1_ffn_sw3"]),
        ws_2=hid_rows(w["L1_ffn_sw2"]),
    )
    arrays.update(shape_constants())
    arrays = {f"in_{k}": np.ascontiguousarray(v) for k, v in arrays.items()}
    nc = bacc.Bacc("TRN2", target_bir_lowering=False, num_devices=1)
    aps = {k[3:]: nc.dram_tensor(k, v.shape, mybir.dt.from_np(v.dtype), kind="ExternalInput").ap()
           for k, v in arrays.items()}
    out = nc.dram_tensor("out", (T, D), F32, kind="ExternalOutput").ap()
    decoder(nc, aps, out)
    r = run(nc, [arrays], core_ids=[0])
    return r.results[0]["out"].reshape(B, S, D)
```

```python
from contextlib import ExitStack

import numpy as np

import concourse.bass as bass
from concourse import mybir

F32 = mybir.dt.float32
BF16 = mybir.dt.bfloat16
U32 = mybir.dt.uint32
U8 = mybir.dt.uint8
ALU = mybir.AluOpType
ACT = mybir.ActivationFunctionType
AX = mybir.AxisListType

P = 128
B, S, D = 4, 256, 256
T = B * S
NT = T // P
KD = D // P
HEADS, DH = 16, 16
CTX = 128
DI, DS, DC, DR = 256, 16, 4, 8
E, R = 8, 16
XH, XKV, XD = 16, 8, 128
HID = 352
HC = [(0, 128), (128, 128), (256, 96)]
CAP = T // E
EPS = 1e-5
BONUS = 3.0 * (1.0 - min(1 / 625, 1.0))
NEG = -1e30
XSCALE = 1.0 / float(np.float32(np.sqrt(XD)))


_LAST = []


def last():
    return _LAST[-1]


class Signal:

    def __init__(self, ctx, nc, name):
        self.sem, self.n = ctx.enter_context(nc.semaphore(name)), 0

    def inc(self, step=1):
        self.n += step
        _LAST[:] = [(self.sem, self.n)]
        return self.sem, step

    def nth(self, i, step=1):
        return self.sem, (i + 1) * step


class Drained:

    def __init__(self, sem, value):
        self.sem, self.value = sem, value

    def inc(self):
        _LAST[:] = [(self.sem, self.value)]
        return self.sem, 1


class Banks:

    def __init__(self, ctx, nc, name, n):
        self.banks = [ctx.enter_context(nc.psum_tensor(f"{name}{i}", [P, 512], F32)) for i in range(n)]
        self.filled = Signal(ctx, nc, f"{name}_filled")
        self.drained = [Signal(ctx, nc, f"{name}{i}_drained") for i in range(n)]
        self.table, self.used = {}, 0

    def take(self, pe, *use):
        i, k = self.used % len(self.banks), self.used // len(self.banks)
        assert use not in self.table
        self.table[use] = (i, k, self.used)
        self.used += 1
        if k:
            pe.wait_ge(self.drained[i].sem, k)
        return self.banks[i]

    def get(self, eng, *use):
        i, _, n = self.table[use]
        eng.wait_ge(*self.filled.nth(n))
        return self.banks[i]

    def full(self, *use):
        return self.filled.nth(self.table[use][2])

    def drain(self, *use):
        i, k, _ = self.table[use]
        return Drained(self.drained[i].sem, k + 1)

    def empty(self, *use):
        i, k, _ = self.table[use]
        return self.drained[i].sem, k + 1


class Engine:

    def __init__(self, eng):
        self.eng, self.passed = eng, {}

    def wait_ge(self, sem, value):
        if self.passed.get(id(sem), 0) < value:
            self.eng.wait_ge(sem, value)
            self.passed[id(sem)] = value


FRONT_STEPS, ATTN0_STEPS, SSM_STEPS, MOE0_STEPS, A_STEPS, X_STEPS = 6, 8, DS + 7, 8, 21, XH + 6


def in_turns(*under_way):
    ticks = 4 * max(steps for _, steps in under_way)
    done = [0] * len(under_way)
    for tick in range(1, ticks + 1):
        for i, (stage, steps) in enumerate(under_way):
            while done[i] * ticks < tick * steps:
                next(stage)
                done[i] += 1
    for stage, _ in under_way:
        assert next(stage, None) is None


def run_layers(ssm_front, attn0, ssm, moe0, attn1, xattn):
    def front(b):
        yield from moe0(b)
        yield from attn1(b)

    def last_attn0():
        for b in range(2, B):
            yield from attn0(b)

    in_turns((ssm_front(0), FRONT_STEPS), (attn0(0), ATTN0_STEPS))
    in_turns((ssm_front(1), FRONT_STEPS), (attn0(1), ATTN0_STEPS), (ssm(0), SSM_STEPS))
    for slot in range(1, B + 2):
        under_way = [(stage(slot - lag), steps) for lag, stage, steps in (
            (2, xattn, X_STEPS), (1, front, MOE0_STEPS + A_STEPS), (0, ssm, SSM_STEPS)) if 0 <= slot - lag < B]
        if slot == 1:
            under_way.append((last_attn0(), ATTN0_STEPS * (B - 2)))
        in_turns(*under_way)


def decoder(nc, a, out):
    ctx = ExitStack()
    with ctx:
        def sb(name, shape, dt=F32):
            return ctx.enter_context(nc.sbuf_tensor(name, shape, dt))

        def signal(name):
            return Signal(ctx, nc, name)

        x_tok = sb("x_tok", [P, NT, D])
        ctx_t = sb("ctx_t", [CTX, T])
        ident = sb("ident", [P, P])
        ident_bf = sb("ident_bf", [P, P], BF16)
        mask_qk = sb("mask_qk", [P, P], BF16)
        head_of = sb("head_of", [P, 8])
        small = sb("small", [P, 64])
        eid_rev = sb("eid_rev", [P, E])
        delta = sb("delta", [P, 2, B, S])
        u = sb("u", [P, 2, B, S])
        du = sb("du", [P, 2, B, S])
        silu_z = sb("silu_z", [P, 2, D])
        NBC = 4
        bc_all = sb("bc_all", [P, NBC, 2, S])
        y_sum = sb("y_sum", [P, 2, S])
        a_neg = sb("a_neg", [P, 2, DS])
        ln_r = sb("ln_r", [P, 3, 2, D])
        ln_st = sb("ln_st", [P, 3, 2, 6])
        ln_mv = sb("ln_mv", [P, 3, 2, 2])
        ln_var = sb("ln_var", [P, 3, 2])
        ln_rs = sb("ln_rs", [P, 3, 2])
        half_neg = sb("half_neg", [P, 2])
        x_feat = sb("x_feat", [P, KD, S])
        xx_feat = sb("xx_feat", [P, KD, S])
        ssm_p = sb("ssm_p", [P, 2, 4 + 1 + 1 + 1 + DS])
        w_r = sb("w_r", [P, KD, E])
        b_r = sb("b_r", [P, E])
        w_d = sb("w_d", [P, KD, P])
        b_d = sb("b_d", [P, 1])
        w_u = sb("w_u", [P, D])
        b_u = sb("b_u", [E, D])
        spread = sb("spread", [E, P])
        rope = sb("rope", [P, 2, 3, 8])
        g8 = sb("g8", [P, 10, 2, E])
        w_e_t = sb("w_e_t", [E, S])
        h_relu = sb("h_relu", [P, S])
        h_w = sb("h_w", [P, S])

        NB, NSTATE = 2, 3
        decay = sb("decay", [P, NB, 2, S])
        drive = sb("drive", [P, NB, 2, S])
        state = sb("state", [P, NSTATE, 2, S])

        def arena(name, words):
            t = sb(name, [P, words])
            at = [0]

            def reset():
                at[0] = 0

            def view(shape, dt=F32):
                n = int(np.prod(shape))
                w = n if dt != BF16 else n // 2
                v = t[:, at[0]:at[0] + w]
                at[0] += w
                assert at[0] <= words, (name, at[0])
                if dt != F32:
                    v = v.bitcast(dt)
                if len(shape) > 1:
                    names = "abcd"[:len(shape)]
                    v = v.rearrange(f"p ({' '.join(names)}) -> p {' '.join(names)}",
                                    **{c: n for c, n in zip(names, shape)})
                return v
            return view, reset

        one, one_again = arena("arena_one", 13872)
        x0_feat = one([KD, T])
        in_pt = one([DI])
        x_pt = one([2, 2 * DS + DR])
        dt_pt = one([DI])[2 * DS:2 * DS + DR, :]
        w_qkv = one([KD, 3 * D])
        x_pad = one([2, 2, S + DC - 1])
        tmp_a = one([2, 2 * S])
        tmp_b = one([2, 2 * S])
        bcd = one([T])[0:2 * DS + DR, :]
        one_again()
        w_qk1 = one([KD, 2 * D])
        w_v1 = one([KD, D])
        w_o1 = one([KD, D])
        qk_rot = one([2, 2 * D])
        rot_b = one([2 * D])
        q_feat = one([KD, S])
        k_feat = one([KD, S])
        k_head = one([2, 4, S])
        p_qk = one([2, 12, P])
        p_t0 = one([2, 4, S])
        p_t1 = one([2, 4, P])
        v_aug = one([2, HEADS, 32])
        o_heads, o_norm, o_feat = qk_rot.rearrange("p a (b s) -> p (a b) s", b=2), k_feat, q_feat
        neg_max = one([2, 8])
        o_den = one([2, HEADS])
        one_again()
        w_1 = one([E, KD, HID])
        w_3 = one([E, KD, HID])
        e_gate = one([3 * P])
        e_hid = one([2, 3 * P])

        two, two_again = arena("arena_two", 18480)
        wx_q = two([KD, XH * XD])
        wx_k = two([XKV * XD])
        wx_v = two([XKV * XD])
        wx_o = two([XH, D])
        before_xattn = two([7840])
        two_again()
        two([(2 * KD * XH // 2 + 2 * XKV + 2 * XH) * XD])
        kx_feat = two([XKV, S])
        vx_tok = two([2, XKV * XD])
        NX = 3
        qx_feat = two([2, S])
        px = two([NX, 2, S])
        px_t = two([2, 2, S])
        ox_feat = two([2, S])
        x_max = two([NX, 2])
        x_nmax = two([NX, 2])
        x_sum = two([NX, 2])
        x_inv = two([NX, 2])
        mask_add = two([B, S], BF16)
        mask_raw = px_t.rearrange("p a b s -> p (a b s)")[:, 0:T // 4].bitcast(U8)
        mask_any = two([B])
        qkv = before_xattn[:, 0:NT * 3 * D].rearrange("p (t c) -> p t c", t=NT)
        before_xattn = before_xattn[:, NT * 3 * D:]
        w_o0 = before_xattn[:, 0:KD * D].rearrange("p (k c) -> p k c", k=KD)
        prod0 = before_xattn[:, KD * D:KD * D + 4 * D].rearrange("p (m c) -> p m c", m=4)
        s0 = before_xattn[:, (KD + 4) * D:(KD + 4) * D + 8 * HEADS].rearrange("p (n h m) -> p n h m", n=2, h=HEADS)
        s0_stat = before_xattn[:, (KD + 4) * D + 8 * HEADS:][:, 0:2 * HEADS].rearrange("p (n h) -> p n h", n=2)
        two_again()
        w_2 = two([E, 3, D])
        ws_1 = two([KD, HID])
        ws_3 = two([KD, HID])
        ws_2 = two([3, D])
        w_g = two([KD, E])
        hs = two([3, 512])
        x5_feat = two([KD, T])
        r8 = two([8, NT, E])
        oh_bf = two([NT, E], BF16)
        tri = two([P], BF16)
        ones = two([P], BF16)
        r1 = two([8, NT])
        dump = two([NT])
        ebase = two([E])
        slot_u = two([2, NT]).bitcast(U32)
        og = two([NT, D])
        xd_tok, xd_feat, oe = delta, du, u
        xd_tok = xd_tok[:, :, :, :].rearrange("p a b c -> p (a b c)").rearrange("p (e d) -> p e d", e=E)
        xd_feat = xd_feat[:, :, :, :].rearrange("p a b c -> p (a b c)").rearrange("p (k t) -> p k t", k=KD)
        oe = oe[:, :, :, :].rearrange("p a b c -> p (a b c)").rearrange("p (e d) -> p e d", e=E)

        bc_dram = nc.dram_tensor("bc_dram", (2, DS, B, S), F32).ap()
        xd_dram = nc.dram_tensor("xd_dram", (2 * T, D), F32).ap()
        oe_dram = nc.dram_tensor("oe_dram", (T, D), F32).ap()

        psum = Banks(ctx, nc, "psum", 4)
        x_psum = Banks(ctx, nc, "x_psum", 3)
        o_psum = Banks(ctx, nc, "o_psum", 1)

        names = """ld_attn0 ld_ssm ld_const ld_moe0 ld_x ld_rope ld_attn1 ld_xattn ld_w13 ld_w2 ld_shared ld_moe1
            zeroed xd_scattered xd_loaded oe_stored oe_gathered out_stored pe_step act_step dve_step
            pool_step pads_clear final_ready u_ready conv_ready expo_arg softplus_t softplus_w softplus_ln
            delta_ready a_ready a_exp s0_arg s0_exp o0_ready decay_ready decay_used bc_stored0 bc_stored1 ld_mask drive_ready seen_ready y_added silu_z_ready
            y_ready x1_ready x2_ready x3_ready x4_ready x5_ready var_ready rstd_ready gate_arg gate_exp
            w_ready qk_ready khead_ready max_ready ones_ready decay_clear smax_ready sexp_ready pn_ready
            ox_used route_exp oh_ready slots_ready""".split()
        sg = {n: signal(n) for n in names}
        bc_loaded = [signal(f"bc_loaded{i}") for i in range(NBC)]

        def bc_rows(hf):
            return bc_dram.rearrange("j n b s -> (j n) (b s)")[:, hf * 512:(hf + 1) * 512]

        def bc_here(k):
            return bc_loaded[k % NBC].nth(k // NBC, 16)

        def added(k):
            return sg["y_added"].nth(k // DS * (DS - 1) + max(k % DS - 1, 0))

        block = ctx.enter_context(nc.Block())

        loads = dict(ld_ssm=5, ld_attn0=3, ld_const=4, ld_x=1, ld_moe0=7, ld_xattn=4, ld_mask=1, ld_rope=2, ld_attn1=3,
                     ld_w13=2, ld_w2=1, ld_shared=4, ld_moe1=4)

        def loaded(name):
            return sg[name].sem, 16 * loads[name]

        qkv0_steps = {0: ((0, 1), (), (), ()), 1: ((2, 3), (4, 5), (6,), (7,)), 2: ((), ) * 4, 3: ((), ) * 4}

        def T2(t, b):
            return t[:, 2 * b:2 * b + 2, :]

        @block.tensor
        def _(eng):
            pe = Engine(eng)
            mm, tr = nc.tensor.matmul, nc.tensor.transpose

            def turn(name, b, tiles, psum=psum):
                ps = psum.take(pe, name, b)
                for k in range(KD):
                    for h in range(2):
                        ins = tr(ps[:, k * S + h * P:k * S + h * P + P], tiles(h, k), ident[:, :])
                ins.then_inc(*psum.filled.inc())

            def project(name, b, feat, w):
                ps = psum.take(pe, name, b)
                for h in range(2):
                    for k in range(KD):
                        ins = mm(ps[:, h * D:(h + 1) * D], feat(h, k), w[:, k, :], start=(k == 0), stop=(k == KD - 1))
                ins.then_inc(*psum.filled.inc())

            def ssm_front(hf):
                cols = slice(hf * 512, (hf + 1) * 512)
                pe.wait_ge(*loaded("ld_ssm"))
                for et in range(2):
                    ps = psum.take(pe, "xin", hf, et)
                    mm(ps[:, :], in_pt[:, et * P:(et + 1) * P], ctx_t[:, cols],
                       start=True, stop=True).then_inc(*psum.filled.inc())
                yield
                yield
                pe.wait_ge(*sg["u_ready"].nth(2 * hf + 1))
                uf = u[:, :, :, :].rearrange("p e b s -> p e (b s)")
                ps = psum.take(pe, "bc", hf)
                for et in range(2):
                    ins = mm(ps[0:2 * DS + DR, :], x_pt[:, et, :], uf[:, et, cols], start=(et == 0), stop=(et == 1))
                ins.then_inc(*psum.filled.inc())
                yield
                pe.wait_ge(*psum.empty("bc", hf))
                for et in range(2):
                    ps = psum.take(pe, "dp", hf, et)
                    mm(ps[:, :], dt_pt[:, et * P:(et + 1) * P], bcd[2 * DS:2 * DS + DR, cols],
                       start=True, stop=True).then_inc(*psum.filled.inc())
                yield
                yield
                yield

            def qkv0(t):
                for name, c0, c1 in (("qk0", 0, 512), ("v0", 512, 768)):
                    ps = psum.take(pe, name, t)
                    for k in range(KD):
                        ins = mm(ps[:, 0:c1 - c0], x0_feat[:, k, t * P:(t + 1) * P], w_qkv[:, k, c0:c1],
                                 start=(k == 0), stop=(k == KD - 1))
                    ins.then_inc(*psum.filled.inc())

            def attn0(b):
                pe.wait_ge(*loaded("ld_attn0"))
                for i in range(4):
                    for t in qkv0_steps[b][i]:
                        qkv0(t)
                    yield
                pe.wait_ge(*sg["o0_ready"].nth(b))
                pe.wait_ge(*loaded("ld_const"))
                turn("o0t", b, lambda h, k: qkv[:, 2 * b + h, k * P:(k + 1) * P])
                yield
                pe.wait_ge(*psum.empty("o0t", b))
                project("proj0", b, lambda h, k: xx_feat[:, k, h * P:(h + 1) * P], w_o0)
                yield
                yield
                yield

            def ssm(b):
                for _ in range(DS + 4):
                    yield
                pe.wait_ge(*sg["y_ready"].nth(b))
                ps = psum.take(pe, "yt", b)
                for lt in range(2):
                    for et in range(2):
                        ins = tr(ps[:, lt * DI + et * P:lt * DI + (et + 1) * P], y_sum[:, et, lt * P:(lt + 1) * P],
                                 ident[:, :])
                ins.then_inc(*psum.filled.inc())
                yield
                yield
                yield

            def moe0(b):
                pe.wait_ge(*sg["x2_ready"].nth(2 * b + 1))
                pe.wait_ge(*loaded("ld_moe0"))
                turn("x2t", b, lambda h, k: x_tok[:, 2 * b + h, k * P:(k + 1) * P])
                yield
                pe.wait_ge(*psum.empty("x2t", b))
                ps = psum.take(pe, "gate0", b)
                for h in range(2):
                    for k in range(KD):
                        ins = mm(ps[:, h * E:(h + 1) * E], x_feat[:, k, h * P:(h + 1) * P], w_r[:, k, :],
                                 start=(k == 0), stop=(k == KD - 1))
                ins.then_inc(*psum.filled.inc())
                ps = psum.take(pe, "hid0", b)
                for k in range(KD):
                    ins = mm(ps[:, 0:S], w_d[:, k, :], x_feat[:, k, :], start=(k == 0), stop=(k == KD - 1))
                ins.then_inc(*psum.filled.inc())
                yield
                yield
                yield
                pe.wait_ge(*sg["w_ready"].nth(b))
                ps = psum.take(pe, "wt0", b)
                for h in range(2):
                    ins = tr(ps[0:E, h * P:(h + 1) * P], g8[:, 9, h, :], ident[:, :])
                ins.then_inc(*psum.filled.inc())
                yield
                pe.wait_ge(*psum.empty("wt0", b))
                ps = psum.take(pe, "spread0", b)
                mm(ps[:, 0:S], spread[:, :], w_e_t[:, :], start=True, stop=True).then_inc(*psum.filled.inc())
                yield
                pe.wait_ge(*psum.empty("spread0", b))
                ps = psum.take(pe, "out0", b)
                for h in range(2):
                    mm(ps[:, h * D:(h + 1) * D], h_w[:, h * P:(h + 1) * P], w_u[:, :], start=True, stop=False)
                    ins = mm(ps[:, h * D:(h + 1) * D], w_e_t[:, h * P:(h + 1) * P], b_u[:, :], start=False, stop=True)
                ins.then_inc(*psum.filled.inc())
                yield
                yield

            def attn1(b):
                pe.wait_ge(*sg["x3_ready"].nth(2 * b + 1))
                pe.wait_ge(*loaded("ld_attn1"))
                turn("x3t", b, lambda h, k: x_tok[:, 2 * b + h, k * P:(k + 1) * P])
                yield
                pe.wait_ge(*psum.empty("x3t", b))
                for h in range(2):
                    ps = psum.take(pe, "qk1", b, h)
                    for k in range(KD):
                        ins = mm(ps[:, :], x_feat[:, k, h * P:(h + 1) * P], w_qk1[:, k, :],
                                 start=(k == 0), stop=(k == KD - 1))
                    ins.then_inc(*psum.filled.inc())
                project("v1", b, lambda h, k: x_feat[:, k, h * P:(h + 1) * P], w_v1)
                yield
                pe.wait_ge(*sg["qk_ready"].nth(2 * b + 1))
                for name, c0 in (("q1t", 0), ("k1t", D)):
                    ps = psum.take(pe, name, b)
                    for k in range(KD):
                        for h in range(2):
                            ins = tr(ps[:, k * S + h * P:k * S + (h + 1) * P],
                                     qk_rot[:, h, c0 + k * P:c0 + (k + 1) * P], ident[:, :])
                    ins.then_inc(*psum.filled.inc())
                yield
                yield
                yield
                pe.wait_ge(*psum.empty("q1t", b))
                pe.wait_ge(*psum.empty("v1", b))
                pe.wait_ge(*sg["ones_ready"].nth(0))
                causal = mask_qk[:, :].unsqueeze(1)
                for g in range(4 + 2):
                    if 1 <= g < 5:
                        c = g - 1
                        pe.wait_ge(*psum.empty("s1a", b, c))
                        ps = psum.take(pe, "pta", b, c)
                        for j in range(4):
                            ins = tr(ps[:, j * P:(j + 1) * P], p_qk[:, c % 2, j, :], ident[:, :])
                        ins.then_inc(*psum.filled.inc())
                    if g < 4:
                        pe.wait_ge(*sg["khead_ready"].nth(b * HEADS + 4 * g + 3))
                        ps = psum.take(pe, "s1a", b, g)
                        mm(ps[:, :], q_feat[:, g // 2, 0:P], k_head[:, g % 2, :, 0:P], start=True, stop=False)
                        mm(ps[:, :], ident_bf[:, :], causal.broadcast_to([P, 4, P]),
                           start=False, stop=True).then_inc(*psum.filled.inc())
                    yield
                    if 1 <= g < 5:
                        c = g - 1
                        for i in range(2):
                            pe.wait_ge(*psum.empty("s1b", b, 2 * c + 1))
                            ps = psum.take(pe, "ptb", b, c, i)
                            for j in range(4):
                                ins = tr(ps[:, j * P:(j + 1) * P], p_qk[:, c % 2, 4 + 2 * j + i, :], ident[:, :])
                            ins.then_inc(*psum.filled.inc())
                    if g < 4:
                        for i in range(2):
                            ps = psum.take(pe, "s1b", b, 2 * g + i)
                            mm(ps[:, :], q_feat[:, g // 2, P:S], k_head[:, g % 2, 2 * i:2 * i + 2, :], start=True, stop=False)
                            mm(ps[:, :].rearrange("p (h k) -> p h k", h=2)[:, :, P:S], ident_bf[:, :],
                               causal.broadcast_to([P, 2, P]), start=False, stop=True).then_inc(*psum.filled.inc())
                    if g >= 2:
                        c = g - 2
                        pe.wait_ge(*psum.empty("pta", b, c))
                        pe.wait_ge(*psum.empty("ptb", b, c, 0))
                        pe.wait_ge(*psum.empty("ptb", b, c, 1))
                        ps = psum.take(pe, "ov1", b, c)
                        for j in range(4):
                            h = 4 * c + j
                            o = ps[32 * j:32 * j + 32, 0:S]
                            mm(o, v_aug[:, 0, h, :], p_t0[:, c % 2, j, :], start=True, stop=False)
                            ins = mm(o[:, P:S], v_aug[:, 1, h, :], p_t1[:, c % 2, j, :], start=False, stop=True)
                        ins.then_inc(*psum.filled.inc())
                    yield
                for h in range(2):
                    for c in range(4):
                        pe.wait_ge(*psum.empty("ov1", b, c))
                    ps = psum.take(pe, "on1", b, h)
                    for g in range(4):
                        ins = tr(ps[:, g * P:(g + 1) * P], o_heads[:, g, h * P:(h + 1) * P], ident[:, :])
                    ins.then_inc(*psum.filled.inc())
                yield
                pe.wait_ge(*psum.empty("on1", b, 0))
                pe.wait_ge(*psum.empty("on1", b, 1))
                turn("o1t", b, lambda h, k: o_norm[:, h, k * P:(k + 1) * P])
                yield
                pe.wait_ge(*psum.empty("o1t", b))
                project("proj1", b, lambda h, k: o_feat[:, k, h * P:(h + 1) * P], w_o1)
                yield
                yield

            def xattn(b):
                pe.wait_ge(*loaded("ld_xattn"))
                for g in range(0, XKV, 2):
                    ps = x_psum.take(pe, "kx", b, g)
                    for i in range(2):
                        ins = mm(ps[:, i * S:(i + 1) * S], wx_k[:, (g + i) * XD:(g + i + 1) * XD],
                                 ctx_t[:, b * S:(b + 1) * S], start=True, stop=True)
                    ins.then_inc(*x_psum.filled.inc())
                for kt in range(2):
                    for i in range(2):
                        ps = x_psum.take(pe, "vx", b, kt, i)
                        mm(ps[:, :], ctx_t[:, b * S + kt * P:b * S + (kt + 1) * P],
                                     wx_v[:, i * 512:(i + 1) * 512], start=True, stop=True).then_inc(*x_psum.filled.inc())
                pe.wait_ge(*sg["x4_ready"].nth(2 * b + 1))
                turn("x4t", b, lambda h, k: x_tok[:, 2 * b + h, k * P:(k + 1) * P], x_psum)
                pe.wait_ge(*x_psum.empty("x4t", b))
                pe.wait_ge(*x_psum.empty("vx", b, 1, 1))
                acc = o_psum.take(pe, "ox", b)
                yield
                for i in range(XH + 4):
                    if 3 <= i < XH + 3:
                        h = i - 3
                        pe.wait_ge(*sg["pn_ready"].nth(2 * (b * XH + h) + 1))
                        ps = x_psum.take(pe, "pxt", b, h)
                        for kt in range(2):
                            for qt in range(2):
                                ins = tr(ps[:, kt * S + qt * P:kt * S + (qt + 1) * P],
                                         px[:, h % NX, qt, kt * P:(kt + 1) * P], ident[:, :])
                        ins.then_inc(*x_psum.filled.inc())
                    if i < XH:
                        ps = x_psum.take(pe, "qx", b, i)
                        for k in range(KD):
                            ins = mm(ps[:, 0:S], wx_q[:, k, i * XD:(i + 1) * XD], xx_feat[:, k, :],
                                     start=(k == 0), stop=(k == KD - 1))
                        ins.then_inc(*x_psum.filled.inc())
                    if 1 <= i < XH + 1:
                        h = i - 1
                        pe.wait_ge(*x_psum.empty("qx", b, h))
                        ps = x_psum.take(pe, "sx", b, h)
                        for qt in range(2):
                            ins = mm(ps[:, qt * S:(qt + 1) * S], qx_feat[:, h % 2, qt * P:(qt + 1) * P],
                                     kx_feat[:, h // 2, :], start=True, stop=True)
                        ins.then_inc(*x_psum.filled.inc())
                    if 3 <= i < XH + 3:
                        h = i - 3
                        pe.wait_ge(*x_psum.empty("pxt", b, h))
                        ps = x_psum.take(pe, "pvx", b, h)
                        for kt in range(2):
                            ins = mm(ps[:, 0:S], vx_tok[:, kt, h // 2 * XD:(h // 2 + 1) * XD], px_t[:, h % 2, kt, :],
                                     start=(kt == 0), stop=(kt == 1))
                        ins.then_inc(*x_psum.filled.inc())
                    if i >= 4:
                        h = i - 4
                        pe.wait_ge(*x_psum.empty("pvx", b, h))
                        for qt in range(2):
                            ins = mm(acc[:, qt * D:(qt + 1) * D], ox_feat[:, h % 2, qt * P:(qt + 1) * P], wx_o[:, h, :],
                                     start=(h == 0 and qt == 0), stop=(h == XH - 1), skip_group_check=True)
                        ins.then_inc(*(o_psum.filled if h == XH - 1 else sg["ox_used"]).inc())
                    yield
                yield

            run_layers(ssm_front, attn0, ssm, moe0, attn1, xattn)

            for t in range(0, NT, 2):
                pe.wait_ge(*sg["x5_ready"].nth(t + 1))
                turn("x5t", t, lambda h, k: x_tok[:, t + h, k * P:(k + 1) * P])
            for t in range(0, NT, 2):
                pe.wait_ge(*psum.empty("x5t", t))
            pe.wait_ge(*loaded("ld_shared"))
            ps = psum.take(pe, "route")
            for t in range(NT):
                for k in range(KD):
                    ins = mm(ps[:, t * E:(t + 1) * E], x5_feat[:, k, t * P:(t + 1) * P], w_g[:, k, :],
                             start=(k == 0), stop=(k == KD - 1))
            ins.then_inc(*psum.filled.inc())

            def shared_hidden(hf, chunks):
                for c in chunks:
                    c0, m = HC[c]
                    for name, w in (("sh1", ws_1), ("sh3", ws_3)):
                        ps = psum.take(pe, name, hf, c)
                        for k in range(KD):
                            ins = mm(ps[0:m, :], w[:, k, c0:c0 + m], x5_feat[:, k, hf * 512:(hf + 1) * 512],
                                     start=(k == 0), stop=(k == KD - 1))
                        ins.then_inc(*psum.filled.inc())

            def shared_out(hf):
                for c in range(3):
                    pe.wait_ge(*psum.empty("sh3", hf, c))
                for t in range(0, 4, 2):
                    ps = psum.take(pe, "sh2", hf, t)
                    for i in range(2):
                        for c, (c0, m) in enumerate(HC):
                            ins = mm(ps[:, i * D:(i + 1) * D], hs[0:m, c, (t + i) * P:(t + i + 1) * P], ws_2[0:m, c, :],
                                     start=(c == 0), stop=(c == 2))
                    ins.then_inc(*psum.filled.inc())

            shared_hidden(0, (0,))
            pe.wait_ge(*sg["oh_ready"].nth(0))
            pe.wait_ge(*loaded("ld_moe1"))
            ps = psum.take(pe, "pos")
            for t in range(NT):
                for j in range(t):
                    mm(ps[:, t * E:(t + 1) * E], ones, oh_bf[:, j, :], start=(j == 0), stop=False)
                ins = mm(ps[:, t * E:(t + 1) * E], tri, oh_bf[:, t, :], start=(t == 0), stop=True)
            ins.then_inc(*psum.filled.inc())
            shared_hidden(0, (1, 2))
            shared_out(0)
            shared_hidden(1, (0, 1, 2))
            shared_out(1)
            pe.wait_ge(*sg["xd_loaded"].nth(0, 16))
            for e in range(0, E, 2):
                turn("xdt", e, lambda h, k: xd_tok[:, e + h, k * P:(k + 1) * P])
            pe.wait_ge(*loaded("ld_w13"))
            pe.wait_ge(*loaded("ld_w2"))
            for e in range(E + 1):
                if e < E:
                    pe.wait_ge(*psum.empty("xdt", e // 2 * 2))
                    for name, w in (("e1", w_1), ("e3", w_3)):
                        ps = psum.take(pe, name, e)
                        for c, (c0, m) in enumerate(HC):
                            for k in range(KD):
                                ins = mm(ps[0:m, c * P:(c + 1) * P], w[:, e, k, c0:c0 + m],
                                         xd_feat[:, k, e * P:(e + 1) * P], start=(k == 0), stop=(k == KD - 1))
                        ins.then_inc(*psum.filled.inc())
                if e:
                    pe.wait_ge(*psum.empty("e3", e - 1))
                    ps = psum.take(pe, "e2", e - 1)
                    for c, (c0, m) in enumerate(HC):
                        ins = mm(ps[:, 0:D], e_hid[0:m, (e - 1) % 2, c * P:(c + 1) * P], w_2[0:m, e - 1, c, :],
                                 start=(c == 0), stop=(c == 2))
                    ins.then_inc(*psum.filled.inc())

        @block.vector
        def _(eng):
            v = Engine(eng)
            V = nc.vector

            def lk(ins, signal=None):
                ins.then_inc(*(signal or sg["dve_step"]).inc())
                v.wait_ge(*last())

            norms = [0, {}]

            def norm_stats(b, get, k=0):
                get(k)
                v.wait_ge(*last())
                for h in range(2):
                    V.bn_stats(ln_st[:, k, h, :], ln_r[:, k, h, :]).then_inc(*sg["dve_step"].inc())
                v.wait_ge(*last())
                for h in range(2):
                    V.bn_aggr(ln_mv[:, k, h, :], ln_st[:, k, h, :]).then_inc(*sg["dve_step"].inc())
                v.wait_ge(*last())
                V.tensor_scalar(ln_var[:, k, :], ln_mv[:, k, :, 1], EPS, None,
                                ALU.add).then_inc(*sg["var_ready"].inc())
                norms[1][k] = norms[0]
                norms[0] += 1

            def norm_scale(b, done, k=0):
                v.wait_ge(*sg["rstd_ready"].nth(norms[1][k]))
                for h in range(2):
                    V.tensor_scalar(x_tok[:, 2 * b + h, :], ln_r[:, k, h, :], ln_mv[:, k, h, 0:1],
                                    ln_rs[:, k, h:h + 1], ALU.subtract, ALU.mult).then_inc(*done.inc())
                v.wait_ge(*last())

            def add_branch(b, name, *use):
                def get(k):
                    ps = psum.get(v, name, *use)
                    V.tensor_tensor(ln_r[:, k, :, :].rearrange("p a b -> p (a b)"), ps[:, :],
                                    T2(x_tok, b).rearrange("p a b -> p (a b)"),
                                    ALU.add).then_inc(*psum.drain(name, *use).inc())
                return get

            v.wait_ge(*loaded("ld_ssm"))
            v.wait_ge(*sg["a_exp"].nth(0))
            V.tensor_scalar(a_neg[:, :, :], ssm_p[:, :, 7:23], -1.0, None, ALU.mult).then_inc(*sg["a_ready"].inc())
            ssm_flat = {n: t[:, :, :, :].rearrange("p e b s -> p e (b s)") for n, t in (("u", u), ("delta", delta), ("du", du))}
            def ssm_front(hf):
                yield
                cols = slice(hf * 512, (hf + 1) * 512)
                v.wait_ge(*psum.empty("xin", hf, 0))
                v.wait_ge(*psum.empty("xin", hf, 1))
                v.wait_ge(*sg["pads_clear"].nth(0))
                if hf:
                    v.wait_ge(*sg["u_ready"].nth(2 * hf - 1))
                for j in range(DC):
                    for et in range(2):
                        o = tmp_a[:, et, :].rearrange("p (b s) -> p b s", b=2)
                        src = x_pad[:, et, :, j:j + S]
                        if j == 0:
                            V.tensor_scalar(o, src, ssm_p[:, et, 0:1], ssm_p[:, et, 4:5], ALU.mult, ALU.add).then_inc(*sg["dve_step"].inc())
                        else:
                            V.scalar_tensor_tensor(o, src, ssm_p[:, et, j:j + 1], o, ALU.mult, ALU.add).then_inc(*(sg["conv_ready"] if j == DC - 1 else sg["dve_step"]).inc())
                    v.wait_ge(*last())
                yield
                ps = psum.get(v, "bc", hf)
                lk(V.tensor_copy(bcd[:, cols], ps[0:2 * DS + DR, :]), psum.drain("bc", hf))
                yield
                xb = ssm_flat["delta"][:, :, cols]
                for et in range(2):
                    ps = psum.get(v, "dp", hf, et)
                    V.tensor_scalar(xb[:, et, :], ps[:, :], ssm_p[:, et, 5:6], None, ALU.add).then_inc(*psum.drain("dp", hf, et).inc())
                v.wait_ge(*last())
                lk(V.scalar_tensor_tensor(tmp_a[:, :, :], xb, -1.0, xb, ALU.mult, ALU.min), sg["expo_arg"])
                yield
                v.wait_ge(*sg["softplus_t"].nth(hf))
                lk(V.tensor_scalar(tmp_a[:, :, :], tmp_b[:, :, :], 1.0, None, ALU.add), sg["softplus_w"])
                yield
                v.wait_ge(*sg["softplus_ln"].nth(hf))
                lk(V.scalar_tensor_tensor(tmp_a[:, :, :], tmp_a[:, :, :], -1.0, tmp_b[:, :, :], ALU.add, ALU.subtract))
                lk(V.tensor_tensor(tmp_a[:, :, :], ssm_flat["du"][:, :, cols], tmp_a[:, :, :], ALU.subtract))
                lk(V.scalar_tensor_tensor(xb, xb, 0.0, tmp_a[:, :, :], ALU.max, ALU.add))
                lk(V.tensor_tensor(ssm_flat["du"][:, :, cols], xb, ssm_flat["u"][:, :, cols], ALU.mult), sg["delta_ready"])
                yield

            kv = qkv.rearrange("p (m n) c -> p n m c", n=2)

            def attn0(b):
                m = b + 1
                yield
                for t in range(2 * b, 2 * b + 2):
                    v.wait_ge(*psum.empty("qk0", t))
                    v.wait_ge(*psum.empty("v0", t))
                for n in range(2):
                    q = kv[:, n, b, 0:D].unsqueeze(1).broadcast_to([P, m, D])
                    lk(V.tensor_tensor(prod0[:, 0:m, :], q, kv[:, n, 0:m, D:2 * D], ALU.mult))
                    lk(V.tensor_reduce(s0[:, n, :, 0:m].rearrange("p h m -> p m h"),
                                       prod0[:, 0:m, :].rearrange("p m (h d) -> p m h d", h=HEADS), AX.X, ALU.add))
                sm = s0[:, :, :, 0:m]
                wide = s0_stat.unsqueeze(3).broadcast_to([P, 2, HEADS, m])
                lk(V.tensor_reduce(s0_stat, sm, AX.X, ALU.max))
                lk(V.tensor_tensor(sm, sm, wide, ALU.subtract), sg["s0_arg"])
                yield
                v.wait_ge(*sg["s0_exp"].nth(b))
                lk(V.tensor_reduce(s0_stat, sm, AX.X, ALU.add))
                lk(V.reciprocal(s0_stat, s0_stat))
                lk(V.tensor_tensor(sm, sm, wide, ALU.mult))
                yield
                for n in range(2):
                    o = prod0.rearrange("p a b -> p (a b)")[:, 0:D * m].rearrange("p (h d m) -> p h d m", h=HEADS, m=m)
                    pr = s0[:, n, :, 0:m].unsqueeze(2).broadcast_to([P, HEADS, DH, m])
                    vv = kv[:, n, 0:m, 2 * D:3 * D].rearrange("p m (h d) -> p h d m", h=HEADS)
                    lk(V.tensor_tensor(o, pr, vv, ALU.mult))
                    lk(V.tensor_reduce(kv[:, n, b, 0:D].rearrange("p (h d) -> p h d", h=HEADS), o, AX.X, ALU.add),
                       sg["o0_ready"] if n else None)
                yield
                yield
                yield
                v.wait_ge(*loaded("ld_x"))
                norm_stats(b, add_branch(b, "proj0", b), 1)
                yield
                norm_scale(b, sg["x1_ready"], 1)
                yield

            def ssm(b):
                v.wait_ge(*sg["delta_ready"].nth(b // 2))
                v.wait_ge(*sg["decay_clear"].nth(0))
                scanned = {}
                for i in range(DS + 2):
                    if 1 <= i <= DS:
                        k = b * DS + i - 1
                        v.wait_ge(*sg["decay_ready"].nth(2 * k + 1))
                        v.wait_ge(*sg["drive_ready"].nth(k))
                        if k >= NSTATE:
                            v.wait_ge(*added(k - NSTATE))
                        V.tensor_tensor_scan(state[:, k % NSTATE, :, :].rearrange("p e s -> p (e s)"),
                                             decay[:, k % NB, :, :].rearrange("p e s -> p (e s)"),
                                             drive[:, k % NB, :, :].rearrange("p e s -> p (e s)"),
                                             0.0, ALU.mult, ALU.add).then_inc(*sg["decay_used"].inc())
                        scanned[k] = last()
                    if i >= 2:
                        k = b * DS + i - 2
                        v.wait_ge(*bc_here(k))
                        v.wait_ge(*scanned[k])
                        V.tensor_tensor(state[:, k % NSTATE, :, :], state[:, k % NSTATE, :, :],
                                        bc_all[:, k % NBC, 1, :].unsqueeze(1).broadcast_to([P, 2, S]),
                                        ALU.mult).then_inc(*sg["seen_ready"].inc())
                    yield
                yield
                v.wait_ge(*sg["y_added"].nth((b + 1) * (DS - 1) - 1))
                for et in range(2):
                    V.scalar_tensor_tensor(y_sum[:, et, :], u[:, et, b, :], ssm_p[:, et, 6:7], y_sum[:, et, :],
                                           ALU.mult, ALU.add).then_inc(*sg["dve_step"].inc())
                v.wait_ge(*last())
                v.wait_ge(*sg["silu_z_ready"].nth(b))
                V.tensor_tensor(y_sum[:, :, :], y_sum[:, :, :], silu_z[:, :, :], ALU.mult).then_inc(*sg["y_ready"].inc())
                yield
                yield
                norm_stats(b, add_branch(b, "yt", b), 2)
                yield
                norm_scale(b, sg["x2_ready"], 2)
                yield

            def first_of_max(g, score, hit, stat, rev, n, signal=None):
                shape = list(g.shape)
                lk(V.tensor_reduce(stat, g, AX.X, ALU.max))
                lk(V.tensor_tensor(hit, g, stat.unsqueeze(2).broadcast_to(shape), ALU.is_equal))
                lk(V.tensor_tensor(score, hit, rev.unsqueeze(1).broadcast_to(shape), ALU.mult))
                lk(V.tensor_reduce(stat, score, AX.X, ALU.max))
                lk(V.tensor_tensor(hit, score, stat.unsqueeze(2).broadcast_to(shape), ALU.is_equal), signal)

            def moe0(b):
                v.wait_ge(*loaded("ld_moe0"))
                v.wait_ge(*loaded("ld_const"))
                G = [g8[:, i, :, :] for i in range(10)]
                stat = small[:, 8:10]
                if b:
                    v.wait_ge(*psum.full("wt0", b - 1))
                yield
                ps = psum.get(v, "gate0", b)
                lk(V.scalar_tensor_tensor(G[0], ps[:, 0:2 * E].rearrange("p (h e) -> p h e", h=2), float(BONUS),
                                          b_r[:, :].unsqueeze(1).broadcast_to([P, 2, E]), ALU.add, ALU.add),
                   psum.drain("gate0", b))
                lk(V.tensor_reduce(stat, G[0], AX.X, ALU.max))
                lk(V.tensor_tensor(G[0], G[0], stat.unsqueeze(2).broadcast_to([P, 2, E]), ALU.subtract), sg["gate_arg"])
                yield
                v.wait_ge(*sg["gate_exp"].nth(b))
                first_of_max(G[1], G[2], G[3], stat, eid_rev[:, :], 2)
                lk(V.scalar_tensor_tensor(G[4], G[3], -4.0, G[1], ALU.mult, ALU.add))
                yield
                first_of_max(G[4], G[5], G[6], stat, eid_rev[:, :], 2)
                lk(V.tensor_tensor(G[7], G[3], G[6], ALU.add))
                lk(V.tensor_tensor(G[8], G[7], G[1], ALU.mult))
                lk(V.tensor_reduce(stat, G[8], AX.X, ALU.add))
                lk(V.reciprocal(stat, stat))
                lk(V.tensor_tensor(G[9], G[8], stat.unsqueeze(2).broadcast_to([P, 2, E]), ALU.mult), sg["w_ready"])
                yield
                ps = psum.get(v, "wt0", b)
                V.tensor_copy(w_e_t[:, :], ps[0:E, 0:S]).then_inc(*psum.drain("wt0", b).inc())
                yield
                v.wait_ge(*psum.empty("hid0", b))
                ps = psum.get(v, "spread0", b)
                lk(V.tensor_tensor(h_w[:, :], h_relu[:, :], ps[:, 0:S], ALU.mult), psum.drain("spread0", b))
                yield
                norm_stats(b, add_branch(b, "out0", b))
                yield
                norm_scale(b, sg["x3_ready"])
                yield

            def attn1(b):
                yield
                v.wait_ge(*loaded("ld_rope"))
                for h in range(2):
                    ps = psum.get(v, "qk1", b, h)[:, :].rearrange("p (g i c) -> p g i c", i=8, c=2)
                    dst = qk_rot[:, h, :].rearrange("p (g i c) -> p g i c", i=8, c=2)
                    tb = rot_b.rearrange("p (g i c) -> p g i c", i=8, c=2)
                    cos, nsin, sin = (rope[:, h, i, :].unsqueeze(1).broadcast_to([P, 32, 8]) for i in range(3))
                    if b and not h:
                        v.wait_ge(*psum.full("k1t", b - 1))
                    V.tensor_tensor(dst[:, :, :, 0], ps[:, :, :, 0], cos, ALU.mult).then_inc(*sg["dve_step"].inc())
                    V.tensor_tensor(dst[:, :, :, 1], ps[:, :, :, 1], cos, ALU.mult).then_inc(*sg["dve_step"].inc())
                    V.tensor_tensor(tb[:, :, :, 0], ps[:, :, :, 1], nsin, ALU.mult).then_inc(*sg["dve_step"].inc())
                    lk(V.tensor_tensor(tb[:, :, :, 1], ps[:, :, :, 0], sin, ALU.mult), psum.drain("qk1", b, h))
                    lk(V.tensor_tensor(qk_rot[:, h, :], qk_rot[:, h, :], rot_b, ALU.add), sg["qk_ready"])
                yield
                yield
                v.wait_ge(*psum.empty("k1t", b))

                def keys(g):
                    for j in range(4):
                        if g >= 2 or b:
                            v.wait_ge(*psum.full("s1b", b if g >= 2 else b - 1, 2 * ((g - 2) % 4) + 1))
                        h = 4 * g + j
                        V.tensor_scalar(k_head[:, g % 2, j, :], k_feat[:, h // 8, :], head_of[:, h % 8:h % 8 + 1], None,
                                        ALU.mult).then_inc(*sg["khead_ready"].inc())

                keys(0)
                yield
                keys(1)
                yield
                for g in range(4):
                    if g >= 2 or b:
                        v.wait_ge(*psum.empty("s1b", b if g >= 2 else b - 1, 2 * ((g - 2) % 4) + 1))
                    ps = psum.get(v, "s1a", b, g)
                    V.tensor_reduce(neg_max[:, g % 2, 0:4], ps[:, :].rearrange("p (h k) -> p h k", h=4),
                                    AX.X, ALU.max, negate=True).then_inc(*sg["max_ready"].inc())
                    yield
                    for i in range(2):
                        ps = psum.get(v, "s1b", b, 2 * g + i)
                        V.tensor_reduce(neg_max[:, g % 2, 4 + 2 * i:6 + 2 * i], ps[:, :].rearrange("p (h k) -> p h k", h=2),
                                        AX.X, ALU.max, negate=True).then_inc(*sg["max_ready"].inc())
                    if g < 2:
                        keys(g + 2)
                    yield
                for _ in range(4):
                    yield
                for h in range(2):
                    ps = psum.get(v, "on1", b, h)[:, :].rearrange("p (h c) -> p h c", h=HEADS)
                    if b and not h:
                        v.wait_ge(*psum.full("o1t", b - 1))
                    lk(V.reciprocal(o_den[:, h, :], ps[:, :, DH]))
                    lk(V.tensor_tensor(o_norm[:, h, :].rearrange("p (h d) -> p h d", h=HEADS), ps[:, :, 0:DH],
                                       o_den[:, h, :].unsqueeze(2).broadcast_to([P, HEADS, DH]), ALU.mult),
                       psum.drain("on1", b, h))
                yield
                yield
                norm_stats(b, add_branch(b, "proj1", b))
                yield
                norm_scale(b, sg["x4_ready"])
                yield

            def xattn(b):
                if not b:
                    v.wait_ge(*loaded("ld_mask"))
                    lk(V.tensor_scalar(mask_add.rearrange("p b s -> p (b s)"), mask_raw, -NEG, NEG, ALU.mult, ALU.add))
                    lk(V.tensor_reduce(mask_any, mask_raw.rearrange("p (b s) -> p b s", b=B), AX.X, ALU.max))
                yield
                for i in range(XH + 4):
                    if 3 <= i < XH + 3:
                        h = i - 3
                        ps = x_psum.get(v, "pxt", b, h)
                        if h >= 2:
                            v.wait_ge(*x_psum.full("pvx", b, h - 2))
                        V.tensor_copy(px_t[:, h % 2, :, :].rearrange("p a b -> p (a b)"),
                                      ps[:, :]).then_inc(*x_psum.drain("pxt", b, h).inc())
                    if 2 <= i < XH + 2:
                        h = i - 2
                        j = h % NX
                        v.wait_ge(*sg["sexp_ready"].nth(2 * (b * XH + h) + 1))
                        lk(V.reciprocal(x_inv[:, j, :], x_sum[:, j, :]))
                        for qt in range(2):
                            V.tensor_scalar(px[:, j, qt, :], px[:, j, qt, :], x_inv[:, j, qt:qt + 1],
                                            mask_any[:, b:b + 1], ALU.mult, ALU.mult).then_inc(*sg["pn_ready"].inc())
                    if 1 <= i < XH + 1:
                        h = i - 1
                        j = h % NX
                        ps = x_psum.get(v, "sx", b, h)
                        if h >= NX:
                            v.wait_ge(*x_psum.full("pxt", b, h - NX))
                        for qt in range(2):
                            V.tensor_tensor_reduce(px[:, j, qt, :], ps[:, qt * S:(qt + 1) * S], mask_add[:, b, :],
                                                   XSCALE, -3e38, ALU.add, ALU.max, x_max[:, j, qt:qt + 1]
                                                   ).then_inc(*(x_psum.drain("sx", b, h) if qt else sg["dve_step"]).inc())
                        v.wait_ge(*last())
                        V.tensor_scalar(x_nmax[:, j, :], x_max[:, j, :], -1.0, None,
                                        ALU.mult).then_inc(*sg["smax_ready"].inc())
                    yield

                def get(k):
                    ps = o_psum.get(v, "ox", b)
                    V.tensor_tensor(ln_r[:, k, :, :].rearrange("p a b -> p (a b)"), ps[:, :],
                                    T2(x_tok, b).rearrange("p a b -> p (a b)"),
                                    ALU.add).then_inc(*o_psum.drain("ox", b).inc())
                norm_stats(b, get, 1)
                norm_scale(b, sg["x5_ready"], 1)
                yield

            run_layers(ssm_front, attn0, ssm, moe0, attn1, xattn)

            RR = [r8[:, i, :, :] for i in range(8)]
            Q1 = [r1[:, i, :] for i in range(8)]
            v.wait_ge(*loaded("ld_moe1"))
            v.wait_ge(*o_psum.empty("ox", B - 1))
            ps = psum.get(v, "route")
            lg = ps[:, 0:NT * E].rearrange("p (t e) -> p t e", t=NT)
            lk(V.tensor_reduce(Q1[0], lg, AX.X, ALU.max))
            lk(V.tensor_tensor(RR[0], lg, Q1[0].unsqueeze(2).broadcast_to([P, NT, E]), ALU.subtract), psum.drain("route"))
            v.wait_ge(*sg["route_exp"].nth(0))
            lk(V.tensor_reduce(Q1[1], RR[1], AX.X, ALU.add))
            lk(V.reciprocal(Q1[1], Q1[1]))
            lk(V.tensor_tensor(RR[1], RR[1], Q1[1].unsqueeze(2).broadcast_to([P, NT, E]), ALU.mult))
            first_of_max(RR[1], RR[2], RR[3], Q1[2], eid_rev[:, :], NT)
            lk(V.tensor_copy(oh_bf[:, :, :], RR[3]), sg["oh_ready"])
            lk(V.tensor_tensor(RR[4], RR[3], RR[1], ALU.mult))
            lk(V.tensor_reduce(Q1[3], RR[4], AX.X, ALU.add))
            ps = psum.get(v, "pos")
            lk(V.tensor_tensor(RR[5], RR[3], ps[:, 0:NT * E].rearrange("p (t e) -> p t e", t=NT), ALU.mult),
               psum.drain("pos"))
            lk(V.tensor_reduce(Q1[4], RR[5], AX.X, ALU.add))
            lk(V.tensor_tensor(RR[6], RR[3], ebase.unsqueeze(1).broadcast_to([P, NT, E]), ALU.mult))
            lk(V.tensor_reduce(Q1[5], RR[6], AX.X, ALU.add))
            lk(V.tensor_tensor(Q1[5], Q1[5], Q1[4], ALU.add))
            lk(V.tensor_scalar(Q1[6], Q1[4], float(CAP), None, ALU.is_le))
            lk(V.tensor_tensor(Q1[3], Q1[3], Q1[6], ALU.mult))
            lk(V.tensor_tensor(Q1[5], Q1[5], Q1[6], ALU.mult))
            lk(V.tensor_copy(slot_u[:, 1, :], Q1[5]))
            lk(V.tensor_tensor(Q1[7], dump, Q1[6], ALU.mult))
            lk(V.tensor_tensor(Q1[7], dump, Q1[7], ALU.subtract))
            lk(V.tensor_tensor(Q1[7], Q1[7], Q1[5], ALU.add))
            lk(V.tensor_copy(slot_u[:, 0, :], Q1[7]), sg["slots_ready"])

            def shared(hf):
                for c, (_, m) in enumerate(HC):
                    v.wait_ge(*psum.empty("sh1", hf, c))
                    ps = psum.get(v, "sh3", hf, c)
                    lk(V.tensor_tensor(hs[0:m, c, :], hs[0:m, c, :], ps[0:m, :], ALU.mult), psum.drain("sh3", hf, c))

            def shared_add(hf):
                for t in range(0, 4, 2):
                    ps = psum.get(v, "sh2", hf, t)
                    xt = x_tok[:, 4 * hf + t:4 * hf + t + 2, :].rearrange("p a b -> p (a b)")
                    V.tensor_tensor(xt, xt, ps[:, :], ALU.add).then_inc(*psum.drain("sh2", hf, t).inc())

            shared(0)
            v.wait_ge(*sg["xd_scattered"].nth(NT - 1, 16))
            shared_add(0)
            shared(1)
            shared_add(1)
            for e in range(0, E, 2):
                ps = psum.get(v, "xdt", e)
                V.tensor_copy(xd_feat[:, :, e * P:(e + 2) * P], ps[:, :].rearrange("p (k t) -> p k t", k=KD)).then_inc(*psum.drain("xdt", e).inc())
            for e in range(E):
                ps = psum.get(v, "e3", e)
                v.wait_ge(*psum.empty("e1", e))
                if e >= 2:
                    v.wait_ge(*psum.full("e2", e - 2))
                V.tensor_tensor(e_hid[:, e % 2, 0:2 * P], e_gate[:, 0:2 * P], ps[:, 0:2 * P], ALU.mult).then_inc(*sg["dve_step"].inc())
                V.tensor_tensor(e_hid[0:96, e % 2, 2 * P:3 * P], e_gate[0:96, 2 * P:3 * P], ps[0:96, 2 * P:3 * P],
                                     ALU.mult).then_inc(*psum.drain("e3", e).inc())
            v.wait_ge(*sg["oe_gathered"].nth(NT - 1, 16))
            for b in range(B):
                def get(k):
                    for h in range(2):
                        t = 2 * b + h
                        V.scalar_tensor_tensor(ln_r[:, k, h, :], og[:, t, :], Q1[3][:, t:t + 1], x_tok[:, t, :],
                                                    ALU.mult, ALU.add).then_inc(*sg["dve_step"].inc())
                norm_stats(b, get)
                norm_scale(b, sg["final_ready"])

        @block.scalar
        def _(eng):
            act = Engine(eng)
            A = nc.scalar.activation

            def copy(dst, src, signal=None):
                return A(dst, src, ACT.Copy).then_inc(*(signal or sg["act_step"]).inc())

            def drain(dst, name, *use, cut=512, ring=psum):
                ps = ring.get(act, name, *use)
                src = ps[:, 0:cut]
                if len(dst.shape) == 3:
                    src = src.rearrange("p (a b) -> p a b", a=dst.shape[1])
                elif len(dst.shape) == 4:
                    src = src.rearrange("p (a b c) -> p a b c", a=dst.shape[1], b=dst.shape[2])
                return copy(dst, src, ring.drain(name, *use))

            act.wait_ge(*loaded("ld_ssm"))
            A(ssm_p[:, :, 7:23], ssm_p[:, :, 7:23], ACT.Exp).then_inc(*sg["a_exp"].inc())
            act.wait_ge(*sg["pads_clear"].nth(0))

            def ssm_front(hf):
                cols = slice(hf * 512, (hf + 1) * 512)
                for et in range(2):
                    if hf:
                        act.wait_ge(*sg["conv_ready"].nth(1))
                    drain(x_pad[:, et, :, DC - 1:], "xin", hf, et)
                yield
                for et in range(2):
                    act.wait_ge(*sg["conv_ready"].nth(2 * hf + et))
                    A(u[:, et, 2 * hf:2 * hf + 2, :].rearrange("p b s -> p (b s)"), tmp_a[:, et, :],
                      ACT.Silu).then_inc(*sg["u_ready"].inc())
                yield
                yield
                if hf:
                    act.wait_ge(*psum.empty("bc", 1))
                    nc.scalar.dma_start(bc_rows(1), bcd[0:2 * DS, cols]).then_inc(*sg["bc_stored1"].inc(16))
                yield
                act.wait_ge(*sg["expo_arg"].nth(hf))
                A(tmp_b[:, :, :], tmp_a[:, :, :], ACT.Exp).then_inc(*sg["softplus_t"].inc())
                yield
                act.wait_ge(*sg["softplus_w"].nth(hf))
                A(du[:, :, :, :].rearrange("p e b s -> p e (b s)")[:, :, cols], tmp_a[:, :, :],
                  ACT.Ln).then_inc(*sg["softplus_ln"].inc())
                yield

            def attn0(b):
                for i in range(4):
                    for t in qkv0_steps[b][i]:
                        drain(qkv[:, t, 0:512], "qk0", t)
                        drain(qkv[:, t, 512:768], "v0", t, cut=256)
                    if i == 2:
                        act.wait_ge(*sg["s0_arg"].nth(b))
                        A(s0[:, :, :, 0:b + 1], s0[:, :, :, 0:b + 1], ACT.Exp,
                          scale=float(DH) ** -0.5).then_inc(*sg["s0_exp"].inc())
                    yield
                if b:
                    act.wait_ge(*psum.full("proj0", b - 1))
                drain(xx_feat[:, :, :], "o0t", b)
                for _ in range(4):
                    yield

            def ssm(b):
                act.wait_ge(*sg["a_ready"].nth(0))
                act.wait_ge(*sg["decay_clear"].nth(0))
                act.wait_ge(*sg["delta_ready"].nth(b // 2))
                for n in range(DS + 2):
                    k = b * DS + n
                    if n < DS:
                        if k >= NB:
                            act.wait_ge(*sg["decay_used"].nth(k - NB))
                        for et in range(2):
                            A(decay[:, k % NB, et, 1:], delta[:, et, b, 1:], ACT.Exp,
                              scale=a_neg[:, et, n:n + 1]).then_inc(*sg["decay_ready"].inc())
                    yield
                if b:
                    act.wait_ge(*sg["y_ready"].nth(b - 1))
                act.wait_ge(*sg["x1_ready"].nth(2 * b + 1))
                A(silu_z[:, :, :], T2(x_tok, b), ACT.Silu).then_inc(*sg["silu_z_ready"].inc())
                for _ in range(5):
                    yield

            def moe0(b):
                drain(x_feat[:, :, :], "x2t", b)
                yield
                act.wait_ge(*sg["gate_arg"].nth(b))
                A(g8[:, 1, :, :], g8[:, 0, :, :], ACT.Exp).then_inc(*sg["gate_exp"].inc())
                ps = psum.get(act, "hid0", b)
                A(h_relu[:, :], ps[:, 0:S], ACT.Relu, bias=b_d[:, 0:1]).then_inc(*psum.drain("hid0", b).inc())
                for _ in range(7):
                    yield

            def attn1(b):
                act.wait_ge(*psum.full("hid0", b))
                drain(x_feat[:, :, :], "x3t", b)
                yield
                ps = psum.get(act, "v1", b)
                act.wait_ge(*sg["ones_ready"].nth(0))
                if b:
                    act.wait_ge(*psum.full("ov1", b - 1, 3))
                for h in range(2):
                    A(v_aug[:, h, :, 0:DH], ps[:, h * D:(h + 1) * D].rearrange("p (h d) -> p h d", h=HEADS),
                      ACT.Copy).then_inc(*(psum.drain("v1", b) if h else sg["act_step"]).inc())
                yield
                ps = psum.get(act, "q1t", b)
                A(q_feat, ps[:, :].rearrange("p (k s) -> p k s", k=KD), ACT.Copy,
                  scale=float(DH) ** -0.5).then_inc(*psum.drain("q1t", b).inc())
                drain(k_feat, "k1t", b)
                for _ in range(3):
                    yield
                for g in range(4 + 2):
                    if 1 <= g < 5:
                        c = g - 1
                        if c >= 2:
                            act.wait_ge(*psum.full("ov1", b, c - 2))
                        drain(p_t0[:, c % 2, :, 0:P], "pta", b, c)
                    if g < 4:
                        if g >= 2:
                            act.wait_ge(*psum.full("ptb", b, g - 2, 1))
                        act.wait_ge(*sg["max_ready"].nth(3 * (4 * b + g)))
                        ps = psum.get(act, "s1a", b, g)
                        for j in range(4):
                            ins = A(p_qk[:, g % 2, j, :], ps[:, j * P:(j + 1) * P], ACT.Exp, bias=neg_max[:, g % 2, j:j + 1])
                            ins.then_inc(*(psum.drain("s1a", b, g) if j == 3 else sg["act_step"]).inc())
                    yield
                    if 1 <= g < 5:
                        drain(p_t0[:, c % 2, :, P:S], "ptb", b, c, 0)
                        drain(p_t1[:, c % 2, :, :], "ptb", b, c, 1)
                    if g < 4:
                        for i in range(2):
                            act.wait_ge(*sg["max_ready"].nth(3 * (4 * b + g) + 1 + i))
                            ps = psum.get(act, "s1b", b, 2 * g + i)
                            for j in range(2):
                                k = 2 * i + j
                                A(p_qk[:, g % 2, 4 + 2 * k:6 + 2 * k, :].rearrange("p a b -> p (a b)"), ps[:, j * S:(j + 1) * S],
                                  ACT.Exp, bias=neg_max[:, g % 2, 4 + k:5 + k]).then_inc(
                                      *(psum.drain("s1b", b, 2 * g + i) if j else sg["act_step"]).inc())
                    if g >= 2:
                        drain(o_heads[:, g - 2, :], "ov1", b, g - 2, cut=S)
                    yield
                yield
                drain(o_feat, "o1t", b)
                yield
                yield
                yield

            def xattn(b):
                for g in range(0, XKV, 2):
                    drain(kx_feat[:, g:g + 2, :], "kx", b, g, ring=x_psum)
                for kt in range(2):
                    for i in range(2):
                        drain(vx_tok[:, kt, i * 512:(i + 1) * 512], "vx", b, kt, i, ring=x_psum)
                drain(xx_feat[:, :, :], "x4t", b, ring=x_psum)
                yield
                for i in range(XH + 4):
                    if i < XH:
                        if i >= 2:
                            act.wait_ge(*x_psum.full("sx", b, i - 2))
                        drain(qx_feat[:, i % 2, :], "qx", b, i, cut=S, ring=x_psum)
                    if 3 <= i < XH + 3:
                        h = i - 3
                        if h >= 2:
                            act.wait_ge(*sg["ox_used"].nth(b * (XH - 1) + h - 2))
                        drain(ox_feat[:, h % 2, :], "pvx", b, h, cut=S, ring=x_psum)
                    if 1 <= i < XH + 1:
                        h = i - 1
                        j = h % NX
                        act.wait_ge(*sg["smax_ready"].nth(b * XH + h))
                        for qt in range(2):
                            A(px[:, j, qt, :], px[:, j, qt, :], ACT.Exp, bias=x_nmax[:, j, qt:qt + 1],
                              accum_out=x_sum[:, j, qt:qt + 1]).then_inc(*sg["sexp_ready"].inc())
                    yield
                yield

            run_layers(ssm_front, attn0, ssm, moe0, attn1, xattn)

            act.wait_ge(*o_psum.empty("ox", B - 1))
            for t in range(0, NT, 2):
                drain(x5_feat[:, :, t * P:(t + 2) * P], "x5t", t)
            act.wait_ge(*psum.empty("route"))
            A(r8[:, 1, :, :], r8[:, 0, :, :], ACT.Exp).then_inc(*sg["route_exp"].inc())

            def shared(hf):
                for c, (_, m) in enumerate(HC):
                    ps = psum.get(act, "sh1", hf, c)
                    if hf:
                        act.wait_ge(*psum.full("sh2", 0, 2))
                    A(hs[0:m, c, :], ps[0:m, :], ACT.Silu).then_inc(*psum.drain("sh1", hf, c).inc())

            shared(0)
            shared(1)

            def expert_out(e):
                drain(oe[:, e, :], "e2", e, cut=D)

            for e in range(E):
                ps = psum.get(act, "e1", e)
                if e:
                    act.wait_ge(*psum.empty("e3", e - 1))
                A(e_gate[:, 0:2 * P], ps[:, 0:2 * P], ACT.Silu).then_inc(*sg["act_step"].inc())
                A(e_gate[0:96, 2 * P:3 * P], ps[0:96, 2 * P:3 * P], ACT.Silu).then_inc(*psum.drain("e1", e).inc())
                if e:
                    expert_out(e - 1)
            expert_out(E - 1)

        @block.gpsimd
        def _(eng):
            pool = Engine(eng)
            G = nc.gpsimd
            G.memset(x_pad[:, :, :, 0:DC - 1], 0.0).then_inc(*sg["pool_step"].inc())
            G.memset(half_neg[:, :], -0.5).then_inc(*sg["pool_step"].inc())
            G.memset(small[:, :], 0.0).then_inc(*sg["pads_clear"].inc())
            pool.wait_ge(*last())

            norms = [0]

            def root(k=0):
                i = norms[0]
                norms[0] += 1
                pool.wait_ge(*sg["var_ready"].nth(i))
                G.tensor_tensor(ln_rs[:, k, :], ln_var[:, k, :], half_neg[:, :], ALU.pow).then_inc(*sg["rstd_ready"].inc())

            G.memset(decay[:, :, :, 0:1], 0.0).then_inc(*sg["decay_clear"].inc())

            def ssm_front(hf):
                for _ in range(FRONT_STEPS):
                    yield

            def attn0(b):
                for _ in range(ATTN0_STEPS - 2):
                    yield
                root(1)
                yield
                yield

            def ssm(b):
                pool.wait_ge(*sg["delta_ready"].nth(b // 2))
                for n in range(DS + 3):
                    k = b * DS + n
                    if n < DS:
                        pool.wait_ge(*bc_here(k))
                        if k >= NB:
                            pool.wait_ge(*sg["decay_used"].nth(k - NB))
                        G.tensor_tensor(drive[:, k % NB, :, :], du[:, :, b, :],
                                        bc_all[:, k % NBC, 0, :].unsqueeze(1).broadcast_to([P, 2, S]),
                                        ALU.mult).then_inc(*sg["drive_ready"].inc())
                    if n >= 4:
                        k -= 3
                        pool.wait_ge(*sg["seen_ready"].nth(k))
                        if b and n == 4:
                            pool.wait_ge(*psum.full("yt", b - 1))
                        if n > 4:
                            pool.wait_ge(*sg["y_added"].nth(b * (DS - 1) + n - 5))
                        G.tensor_tensor(y_sum[:, :, :], state[:, (k - 1) % NSTATE, :, :] if n == 4 else y_sum[:, :, :],
                                        state[:, k % NSTATE, :, :], ALU.add).then_inc(*sg["y_added"].inc())
                    yield
                yield
                yield
                root(2)
                yield
                yield

            def moe0(b):
                for _ in range(MOE0_STEPS - 2):
                    yield
                root()
                yield
                yield

            def attn1(b):
                if not b:
                    pool.wait_ge(*psum.full("v0", NT - 1))
                    pool.wait_ge(*sg["delta_ready"].nth(1))
                    pool.wait_ge(*sg["bc_stored1"].nth(0, 16))
                    G.memset(v_aug[:, :, :, DH:], 0.0).then_inc(*sg["pool_step"].inc())
                    pool.wait_ge(*last())
                    G.memset(v_aug[:, :, :, DH:DH + 1], 1.0).then_inc(*sg["ones_ready"].inc())
                for _ in range(A_STEPS - 2):
                    yield
                root()
                yield
                yield

            def xattn(b):
                for _ in range(XH + 5):
                    yield
                root(1)
                yield

            run_layers(ssm_front, attn0, ssm, moe0, attn1, xattn)

            pool.wait_ge(*sg["slots_ready"].nth(0))
            pool.wait_ge(*sg["zeroed"].nth(0, 16))
            for t in range(NT):
                G.indirect_dma_start(
                    xd_dram, bass.IndirectOffsetOnAxis(ap=slot_u[:, 0, t:t + 1], axis=0), x_tok[:, t, :], None).then_inc(*sg["xd_scattered"].inc(16))
            pool.wait_ge(*sg["oe_stored"].nth(E - 1, 16))
            for t in range(NT):
                G.indirect_dma_start(
                    og[:, t, :], None, oe_dram, bass.IndirectOffsetOnAxis(ap=slot_u[:, 1, t:t + 1], axis=0)).then_inc(*sg["oe_gathered"].inc(16))
            for _ in range(B):
                root()

        @block.sync
        def _(eng):
            sp = Engine(eng)

            def load(dst, src, name):
                eng.dma_start(dst, src).then_inc(*sg[name].inc(16))

            load(in_pt, a["in_pt"], "ld_ssm")
            load(ctx_t[:, :], a["ctx_t"], "ld_ssm")
            load(ssm_p[:, :, :], a["ssm_p"], "ld_ssm")
            load(x_pt, a["x_pt"], "ld_ssm")
            load(dt_pt, a["dt_pt"], "ld_ssm")
            load(x0_feat, a["x_t"], "ld_attn0")
            load(w_qkv, a["w_qkv"], "ld_attn0")
            load(w_o0, a["w_o0"], "ld_attn0")
            load(ident[:, :], a["ident"], "ld_const")
            load(ident_bf[:, :], a["ident_bf"], "ld_const")
            load(mask_qk[:, :], a["mask_qk"], "ld_const")
            load(eid_rev[:, :], a["eid_rev"], "ld_const")
            load(x_tok[:, :, :], a["x"], "ld_x")
            load(w_r[:, :, :], a["w_r"], "ld_moe0")
            load(b_r[:, :], a["b_r"].partition_broadcast(P), "ld_moe0")
            load(w_d[:, :, :], a["w_d"], "ld_moe0")
            load(b_d[:, :], a["b_d"], "ld_moe0")
            load(w_u[:, :], a["w_u"], "ld_moe0")
            load(b_u[:, :], a["b_u"], "ld_moe0")
            load(spread[:, :], a["spread"], "ld_moe0")
            load(wx_k, a["wx_k"], "ld_xattn")
            load(wx_v, a["wx_v"], "ld_xattn")
            load(wx_q, a["wx_q"], "ld_xattn")
            load(wx_o, a["wx_o"], "ld_xattn")
            load(rope[:, :, :, :], a["rope"], "ld_rope")
            load(head_of[:, :], a["head_of"], "ld_rope")
            load(xd_dram[0:T, :], a["zeros"], "zeroed")
            sp.wait_ge(*psum.empty("bc", 0))
            load(bc_rows(0), bcd[0:2 * DS, 0:512], "bc_stored0")

            def load_bc(b):
                for n in range(DS):
                    k = b * DS + n
                    if k >= NBC:
                        sp.wait_ge(*sg["seen_ready"].nth(k - NBC))
                    eng.dma_start(bc_all[:, k % NBC, :, :], bc_dram[:, n, b, :].partition_broadcast(P)).then_inc(
                        *bc_loaded[k % NBC].inc(16))

            sp.wait_ge(*sg["bc_stored0"].nth(0, 16))
            load_bc(0)
            sp.wait_ge(*psum.full("v0", NT - 1))
            sp.wait_ge(*sg["delta_ready"].nth(1))
            sp.wait_ge(*sg["bc_stored1"].nth(0, 16))
            load(w_qk1, a["w_qk1"], "ld_attn1")
            load(w_v1, a["w_v1"], "ld_attn1")
            load(w_o1, a["w_o1"], "ld_attn1")
            load_bc(1)
            sp.wait_ge(*sg["x1_ready"].nth(NT - 1))
            load(mask_raw, a["mask"].partition_broadcast(P), "ld_mask")
            load_bc(2)
            load_bc(3)
            sp.wait_ge(*sg["x4_ready"].nth(2 * B - 1))
            load(w_1, a["w_1"], "ld_w13")
            load(w_3, a["w_3"], "ld_w13")
            sp.wait_ge(*o_psum.empty("ox", B - 1))
            sp.wait_ge(*sg["x5_ready"].nth(2 * B - 1))
            load(w_g, a["w_g"], "ld_shared")
            load(ws_1, a["ws_1"], "ld_shared")
            load(ws_3, a["ws_3"], "ld_shared")
            load(ws_2, a["ws_2"], "ld_shared")
            load(tri, a["tri"], "ld_moe1")
            load(ones, a["ones"], "ld_moe1")
            load(dump, a["dump"], "ld_moe1")
            load(ebase, a["ebase"], "ld_moe1")
            load(w_2, a["w_2"], "ld_w2")
            sp.wait_ge(*sg["xd_scattered"].nth(NT - 1, 16))
            load(xd_tok, xd_dram[0:T, :].rearrange("(e p) d -> p e d", p=P), "xd_loaded")
            for e in range(E):
                sp.wait_ge(*psum.empty("e2", e))
                load(oe_dram[e * P:(e + 1) * P, :], oe[:, e, :], "oe_stored")
            for t in range(NT):
                sp.wait_ge(*sg["final_ready"].nth(t))
                load(out[t * P:(t + 1) * P, :], x_tok[:, t, :], "out_stored")
            sp.wait_ge(*sg["out_stored"].nth(NT - 1, 16))
            assert all(sg[n].n == 16 * k for n, k in loads.items())


_SHAPE_CONSTANTS = ("ident", "ident_bf", "mask_qk", "eid_rev", "spread", "rope", "head_of",
                    "tri", "ones", "dump", "ebase", "zeros")


def shape_constants():
    bf = mybir.dt.np(BF16)
    i = np.arange(P)
    c = {"ident": np.eye(P, dtype=np.float32), "ident_bf": np.eye(P).astype(bf)}
    c["mask_qk"] = np.where(i[None, :] > i[:, None], NEG, 0.0).astype(bf)
    c["eid_rev"] = np.tile(np.arange(E, 0, -1, dtype=np.float32), (P, 1))
    c["spread"] = (np.arange(P)[None, :] // R == np.arange(E)[:, None]).astype(np.float32)
    freq = (1.0 / 10000.0 ** (np.arange(0, DH, 2, dtype=np.float32) / DH)).astype(np.float32)
    ang = np.outer(np.arange(S, dtype=np.float32), freq).astype(np.float32)
    r = np.stack([np.cos(ang), -np.sin(ang), np.sin(ang)], 1).astype(np.float32)
    c["rope"] = np.ascontiguousarray(r.reshape(2, P, 3, 8).transpose(1, 0, 2, 3))
    c["head_of"] = (i[:, None] // DH == np.arange(8)[None, :]).astype(np.float32)
    c["tri"] = (i[:, None] <= i[None, :]).astype(bf)
    c["ones"] = np.ones((P, P)).astype(bf)
    c["dump"] = (T + np.arange(NT)[None, :] * P + i[:, None]).astype(np.float32)
    c["ebase"] = np.tile(np.arange(E, dtype=np.float32) * CAP - 1, (P, 1))
    c["zeros"] = np.zeros((T, D), np.float32)
    return c


def kernel(**inputs):
    import concourse.bacc as bacc
    from concourse.bass_utils import run_bass_kernel_spmd as run

    w = {k: np.asarray(x) for k, x in inputs.items()}

    def tiles(m, p=P):
        return m.reshape(m.shape[0] // p, p, *m.shape[1:]).swapaxes(0, 1)

    def hid_rows(m):
        pad = np.zeros((*m.shape[:-2], 3 * P - HID, m.shape[-1]), m.dtype)
        m = np.concatenate([m, pad], -2)
        m = m.reshape(*m.shape[:-2], 3, P, m.shape[-1])
        return np.moveaxis(m, -2, 0)

    xp = w["L0_xattn_x_proj_w"]
    x = w["x"].reshape(T, D)
    arrays = dict(
        x=tiles(x), x_t=tiles(x.T), ctx_t=w["ctx_1024"].reshape(T, CTX).T,
        mask=w["mask_BxS2_bf1"].reshape(T).view(np.uint8),
        w_qkv=tiles(w["L0_attn_weight_qkv"].T), w_o0=tiles(w["L0_attn_weight_out"].T),
        in_pt=w["L0_xattn_in_proj_w"].T,
        x_pt=tiles(np.concatenate([xp[DR:], xp[:DR]], 0).T),
        dt_pt=w["L0_xattn_dt_proj_w"].T,
        ssm_p=tiles(np.concatenate([w["L0_xattn_conv_w"], w["L0_xattn_conv_b"][:, None],
                                    w["L0_xattn_dt_proj_b"][:, None], w["L0_xattn_D"][:, None],
                                    w["L0_xattn_A_log"]], 1)),
        w_r=tiles(w["L0_ffn_Wr"]), b_r=w["L0_ffn_br"],
        w_d=tiles(w["L0_ffn_Wd"].transpose(1, 0, 2).reshape(D, E * R)),
        b_d=w["L0_ffn_bd"].reshape(P, 1), w_u=w["L0_ffn_Wu"].reshape(E * R, D), b_u=w["L0_ffn_bu"],
        w_qk1=tiles(np.concatenate([w["L1_attn_Wq"].T, w["L1_attn_Wk"].T], 1)),
        w_v1=tiles(w["L1_attn_Wv"].T), w_o1=tiles(w["L1_attn_Wo"].T),
        wx_q=tiles(w["L1_xattn_Wq"]), wx_k=w["L1_xattn_Wk"], wx_v=w["L1_xattn_Wv"], wx_o=tiles(w["L1_xattn_Wo"]),
        w_g=tiles(w["L1_ffn_Wg"]),
        w_1=w["L1_ffn_W1"].reshape(E, KD, P, HID).transpose(2, 0, 1, 3),
        w_3=w["L1_ffn_W3"].reshape(E, KD, P, HID).transpose(2, 0, 1, 3),
        w_2=hid_rows(w["L1_ffn_W2"]), ws_1=tiles(w["L1_ffn_sw1"]), ws_3=tiles(w["L1_ffn_sw3"]),
        ws_2=hid_rows(w["L1_ffn_sw2"]),
    )
    arrays.update(shape_constants())
    arrays = {f"in_{k}": np.ascontiguousarray(v) for k, v in arrays.items()}
    nc = bacc.Bacc("TRN2", target_bir_lowering=False, num_devices=1)
    aps = {k[3:]: nc.dram_tensor(k, v.shape, mybir.dt.from_np(v.dtype), kind="ExternalInput").ap()
           for k, v in arrays.items()}
    out = nc.dram_tensor("out", (T, D), F32, kind="ExternalOutput").ap()
    decoder(nc, aps, out)
    r = run(nc, [arrays], core_ids=[0])
    return r.results[0]["out"].reshape(B, S, D)
```

```python
from contextlib import ExitStack

import numpy as np

import concourse.bass as bass
from concourse import mybir

F32 = mybir.dt.float32
BF16 = mybir.dt.bfloat16
U32 = mybir.dt.uint32
U8 = mybir.dt.uint8
ALU = mybir.AluOpType
ACT = mybir.ActivationFunctionType
AX = mybir.AxisListType

P = 128
B, S, D = 4, 256, 256
T = B * S
NT = T // P
KD = D // P
HEADS, DH = 16, 16
CTX = 128
DI, DS, DC, DR = 256, 16, 4, 8
E, R = 8, 16
XH, XKV, XD = 16, 8, 128
HID = 352
HC = [(0, 128), (128, 128), (256, 96)]
CAP = T // E
EPS = 1e-5
BONUS = 3.0 * (1.0 - min(1 / 625, 1.0))
NEG = -1e30
XSCALE = 1.0 / float(np.float32(np.sqrt(XD)))


_LAST = []


def last():
    return _LAST[-1]


class Signal:

    def __init__(self, ctx, nc, name):
        self.sem, self.n = ctx.enter_context(nc.semaphore(name)), 0

    def inc(self, step=1):
        self.n += step
        _LAST[:] = [(self.sem, self.n)]
        return self.sem, step

    def nth(self, i, step=1):
        return self.sem, (i + 1) * step


class Drained:

    def __init__(self, sem, value):
        self.sem, self.value = sem, value

    def inc(self):
        _LAST[:] = [(self.sem, self.value)]
        return self.sem, 1


class Banks:

    def __init__(self, ctx, nc, name, n):
        self.banks = [ctx.enter_context(nc.psum_tensor(f"{name}{i}", [P, 512], F32)) for i in range(n)]
        self.filled = Signal(ctx, nc, f"{name}_filled")
        self.drained = [Signal(ctx, nc, f"{name}{i}_drained") for i in range(n)]
        self.table, self.used = {}, 0

    def take(self, pe, *use):
        i, k = self.used % len(self.banks), self.used // len(self.banks)
        assert use not in self.table
        self.table[use] = (i, k, self.used)
        self.used += 1
        if k:
            pe.wait_ge(self.drained[i].sem, k)
        return self.banks[i]

    def get(self, eng, *use):
        i, _, n = self.table[use]
        eng.wait_ge(*self.filled.nth(n))
        return self.banks[i]

    def full(self, *use):
        return self.filled.nth(self.table[use][2])

    def drain(self, *use):
        i, k, _ = self.table[use]
        return Drained(self.drained[i].sem, k + 1)

    def empty(self, *use):
        i, k, _ = self.table[use]
        return self.drained[i].sem, k + 1


class Engine:

    def __init__(self, eng):
        self.eng, self.passed = eng, {}

    def wait_ge(self, sem, value):
        if self.passed.get(id(sem), 0) < value:
            self.eng.wait_ge(sem, value)
            self.passed[id(sem)] = value


STEPS = {"ssm_front": 7, "attn0": 8, "ssm": DS + 7, "fold": 8, "moe0": 11, "attn1": 21, "xattn": 2 * (XH + 5) + 2}
PLAN = (
    ("ssm_front", 0, 0, 33),
    ("attn0", 0, 0, 48),
    ("ssm_front", 1, 33, 22),
    ("ssm", 0, 37, 49),
    ("attn0", 1, 50, 33),
    ("ssm_front", 2, 55, 26),
    ("fold", 0, 86, 72),
    ("ssm_front", 3, 89, 18),
    ("attn0", 2, 91, 39),
    ("moe0", 0, 92, 15),
    ("ssm", 1, 94, 88),
    ("attn1", 0, 105, 61),
    ("attn0", 3, 130, 33),
    ("xattn", 0, 168, 112),
    ("moe0", 1, 182, 41),
    ("ssm", 2, 182, 95),
    ("attn1", 1, 222, 57),
    ("ssm", 3, 281, 100),
    ("moe0", 2, 284, 46),
    ("xattn", 1, 286, 103),
    ("attn1", 2, 334, 47),
    ("moe0", 3, 385, 32),
    ("xattn", 2, 389, 117),
    ("attn1", 3, 417, 62),
    ("xattn", 3, 533, 86),
)


def run_layers(**stages):
    running = [stages[name](b) for name, b, _, _ in PLAN]
    steps = sorted((begin + (n + 0.5) * length / STEPS[name], i)
                   for i, (name, _, begin, length) in enumerate(PLAN) for n in range(STEPS[name]))
    for _, i in steps:
        next(running[i])
    assert all(next(stage, None) is None for stage in running)


def decoder(nc, a, out):
    ctx = ExitStack()
    with ctx:
        def sb(name, shape, dt=F32):
            return ctx.enter_context(nc.sbuf_tensor(name, shape, dt))

        def signal(name):
            return Signal(ctx, nc, name)

        x_tok = sb("x_tok", [P, NT, D])
        ctx_t = sb("ctx_t", [CTX, T])
        ident = sb("ident", [P, P])
        ident_bf = sb("ident_bf", [P, P], BF16)
        mask_qk = sb("mask_qk", [P, P], BF16)
        head_of = sb("head_of", [P, 8])
        small = sb("small", [P, 64])
        eid_rev = sb("eid_rev", [P, E])
        delta = sb("delta", [P, 2, B, S])
        u = sb("u", [P, 2, B, S])
        du = sb("du", [P, 2, B, S])
        silu_z = sb("silu_z", [P, 2, D])
        NBC = 4
        bc_all = sb("bc_all", [P, NBC, 2, S])
        y_sum = sb("y_sum", [P, 2, S])
        a_neg = sb("a_neg", [P, 2, DS])
        ln_r = sb("ln_r", [P, 3, 2, D])
        ln_st = sb("ln_st", [P, 3, 2, 6])
        ln_mv = sb("ln_mv", [P, 3, 2, 2])
        ln_var = sb("ln_var", [P, 3, 2])
        ln_rs = sb("ln_rs", [P, 3, 2])
        half_neg = sb("half_neg", [P, 2])
        x_feat = sb("x_feat", [P, KD, S])
        xx_feat = sb("xx_feat", [P, KD, S])
        ssm_p = sb("ssm_p", [P, 2, 4 + 1 + 1 + 1 + DS])
        w_r = sb("w_r", [P, KD, E])
        b_r = sb("b_r", [P, E])
        w_d = sb("w_d", [P, KD, P])
        b_d = sb("b_d", [P, 1])
        w_u = sb("w_u", [P, D])
        b_u = sb("b_u", [E, D])
        spread = sb("spread", [E, P])
        rope = sb("rope", [P, 2, 3, 8])
        g8 = sb("g8", [P, 10, 2, E])
        w_e_t = sb("w_e_t", [E, S])
        h_relu = sb("h_relu", [P, S])
        h_w = sb("h_w", [P, S])

        NB, NSTATE = 2, 3
        decay = sb("decay", [P, NB, 2, S])
        drive = sb("drive", [P, NB, 2, S])
        state = sb("state", [P, NSTATE, 2, S])

        def arena(name, words):
            t = sb(name, [P, words])
            at = [0]

            def reset():
                at[0] = 0

            def view(shape, dt=F32):
                n = int(np.prod(shape))
                w = n if dt != BF16 else n // 2
                v = t[:, at[0]:at[0] + w]
                at[0] += w
                assert at[0] <= words, (name, at[0])
                if dt != F32:
                    v = v.bitcast(dt)
                if len(shape) > 1:
                    names = "abcd"[:len(shape)]
                    v = v.rearrange(f"p ({' '.join(names)}) -> p {' '.join(names)}",
                                    **{c: n for c, n in zip(names, shape)})
                return v
            return view, reset

        one, one_again = arena("arena_one", 13872)
        x0_feat = one([KD, T])
        in_pt = one([DI])
        x_pt = one([2, 2 * DS + DR])
        dt_pt = one([DI])[2 * DS:2 * DS + DR, :]
        w_qkv = one([KD, 3 * D])
        x_pad = one([2, S + DC - 1])
        tmp_a = one([2, S])
        tmp_b = one([2, S])
        bcd = one([T])[0:2 * DS + DR, :]
        one_again()
        w_qk1 = one([KD, 2 * D])
        w_v1 = one([KD, D])
        w_o1 = one([KD, D])
        qk_rot = one([2, 2 * D])
        rot_b = one([2 * D])
        q_feat = one([KD, S])
        k_feat = one([KD, S])
        k_head = one([2, 4, S])
        p_qk = one([2, 12, P])
        p_t0 = one([2, 4, S])
        p_t1 = one([2, 4, P])
        v_aug = one([2, HEADS, 32])
        o_heads, o_norm, o_feat = qk_rot.rearrange("p a (b s) -> p (a b) s", b=2), k_feat, q_feat
        neg_max = one([2, 8])
        o_den = one([2, HEADS])
        one_again()
        w_1 = one([E, KD, HID])
        w_3 = one([E, KD, HID])
        e_gate = one([3 * P])
        e_hid = one([2, 3 * P])
        ws_3 = e_hid.rearrange("p a b -> p (a b)")[:, 0:KD * HID].rearrange("p (k c) -> p k c", k=KD)
        ws_1 = one([KD, HID])
        w_g = one([KD, E])
        tri = one([P], BF16)
        ones = one([P], BF16)
        dump = one([NT])
        ebase = one([E])

        two, two_again = arena("arena_two", 18080)
        m_q = two([XH, KD, XD])
        m_o = two([XH, D])
        wx_k = two([XKV, CTX])
        wx_v = two([XKV, CTX])
        before_xattn = two([7840])
        two_again()
        two([(2 * KD * XH + 2 * XKV) * XD])
        ctx_tok = two([NT, CTX])
        NX = 3
        qx_feat = two([2, S])
        px = two([NX, 2, S])
        px_t = two([2, 2, S])
        ox_feat = two([2, S])
        x_max = two([NX, 2])
        x_nmax = two([NX, 2])
        x_sum = two([NX, 2])
        x_inv = two([NX, 2])
        mask_add = two([B, S], BF16)
        mask_raw = px_t.rearrange("p a b s -> p (a b s)")[:, 0:T // 4].bitcast(U8)
        mask_any = two([B])
        qkv = before_xattn[:, 0:NT * 3 * D].rearrange("p (t c) -> p t c", t=NT)
        before_xattn = before_xattn[:, NT * 3 * D:]
        w_o0 = before_xattn[:, 0:KD * D].rearrange("p (k c) -> p k c", k=KD)
        prod0 = before_xattn[:, KD * D:KD * D + 4 * D].rearrange("p (m c) -> p m c", m=4)
        s0 = before_xattn[:, (KD + 4) * D:(KD + 4) * D + 8 * HEADS].rearrange("p (n h m) -> p n h m", n=2, h=HEADS)
        s0_stat = before_xattn[:, (KD + 4) * D + 8 * HEADS:][:, 0:2 * HEADS].rearrange("p (n h) -> p n h", n=2)
        two_again()
        w_2 = two([E, 3, D])
        ws_2 = two([3, D])
        hs = two([3, 512])
        r8 = two([8, NT, E])
        oh_bf = two([NT, E], BF16)
        r1 = two([8, NT])
        slot_u = two([2, NT]).bitcast(U32)
        og = two([NT, D])
        x5_feat = bc_all[:, :, :, :].rearrange("p a b c -> p (a b c)").rearrange("p (k t) -> p k t", k=KD)
        xd_tok, xd_feat, oe = delta, du, u
        xd_tok = xd_tok[:, :, :, :].rearrange("p a b c -> p (a b c)").rearrange("p (e d) -> p e d", e=E)
        xd_feat = xd_feat[:, :, :, :].rearrange("p a b c -> p (a b c)").rearrange("p (k t) -> p k t", k=KD)
        oe = oe[:, :, :, :].rearrange("p a b c -> p (a b c)").rearrange("p (e d) -> p e d", e=E)

        bc_dram = nc.dram_tensor("bc_dram", (2, DS, B, S), F32).ap()
        xd_dram = nc.dram_tensor("xd_dram", (2 * T, D), F32).ap()
        oe_dram = nc.dram_tensor("oe_dram", (T, D), F32).ap()

        psum = Banks(ctx, nc, "psum", 4)
        x_psum = Banks(ctx, nc, "x_psum", 3)
        o_psum = Banks(ctx, nc, "o_psum", 1)

        names = """ld_attn0 ld_ssm ld_const ld_moe0 ld_x ld_rope ld_attn1 ld_xattn ld_w13 ld_w2 ld_shared ld_route
            ld_ws2
            zeroed xd_scattered xd_loaded oe_stored oe_gathered0 oe_gathered1 oe_gathered2 oe_gathered3
            out_stored act_step dve_step
            pool_step pads_clear final_ready u_ready conv_ready size_ready softplus_ready softplus_t
            softplus_w softplus_ln
            delta_ready a_ready a_exp s0_arg s0_exp o0_ready decay_ready decay_used
            bc_stored0 bc_stored1 bc_stored2 bc_stored3 ld_mask ld_ctx drive_ready seen_even seen_odd y_added
            silu_z_ready
            y_ready x1_ready x2_ready x3_ready x4_ready x5_ready var_ready rstd_ready gate_arg gate_exp
            w_ready qk_ready khead_ready max_ready ones_ready decay_clear smax_ready sexp_ready pn_ready
            ox_used route_arg route_exp oh_ready slots_ready""".split()
        sg = {n: signal(n) for n in names}
        bc_loaded = [signal(f"bc_loaded{i}") for i in range(NBC)]

        def bc_rows(b):
            return bc_dram[:, :, b, :].rearrange("j n s -> (j n) s")

        def bc_here(k):
            return bc_loaded[k % NBC].nth(k // NBC, 16)

        def seen(k):
            return sg["seen_odd" if k % 2 else "seen_even"].nth(k // 2)

        def added(k):
            return sg["y_added"].nth(k // DS * (DS - 1) + max(k % DS - 1, 0))

        block = ctx.enter_context(nc.Block())

        loads = dict(ld_ssm=5, ld_attn0=3, ld_const=4, ld_x=1, ld_moe0=7, ld_xattn=4, ld_mask=1, ld_ctx=1,
                     ld_rope=2, ld_attn1=3, ld_w13=2, ld_w2=1, ld_shared=2, ld_route=5, ld_ws2=1)

        def loaded(name):
            return sg[name].sem, 16 * loads[name]

        qkv0_steps = {0: ((0, 1), (), (), ()), 1: ((2, 3), (4, 5), (6,), (7,)), 2: ((), ) * 4, 3: ((), ) * 4}

        def T2(t, b):
            return t[:, 2 * b:2 * b + 2, :]

        @block.tensor
        def _(eng):
            pe = Engine(eng)
            mm, tr = nc.tensor.matmul, nc.tensor.transpose

            def turn(name, b, tiles, psum=psum):
                ps = psum.take(pe, name, b)
                for k in range(KD):
                    for h in range(2):
                        ins = tr(ps[:, k * S + h * P:k * S + h * P + P], tiles(h, k), ident[:, :])
                ins.then_inc(*psum.filled.inc())

            def project(name, b, feat, w):
                ps = psum.take(pe, name, b)
                for h in range(2):
                    for k in range(KD):
                        ins = mm(ps[:, h * D:(h + 1) * D], feat(h, k), w[:, k, :], start=(k == 0), stop=(k == KD - 1))
                ins.then_inc(*psum.filled.inc())

            def ssm_front(b):
                cols = slice(b * S, (b + 1) * S)
                pe.wait_ge(*loaded("ld_ssm"))
                ps = psum.take(pe, "xin", b)
                for et in range(2):
                    ins = mm(ps[:, et * S:(et + 1) * S], in_pt[:, et * P:(et + 1) * P], ctx_t[:, cols],
                             start=True, stop=True)
                ins.then_inc(*psum.filled.inc())
                yield
                yield
                ps = psum.take(pe, "bc", b)
                for et in range(2):
                    pe.wait_ge(*sg["u_ready"].nth(2 * b + et))
                    ins = mm(ps[0:2 * DS + DR, 0:S], x_pt[:, et, :], u[:, et, b, :], start=(et == 0), stop=(et == 1))
                ins.then_inc(*psum.filled.inc())
                yield
                pe.wait_ge(*psum.empty("bc", b))
                ps = psum.take(pe, "dp", b)
                for et in range(2):
                    ins = mm(ps[:, et * S:(et + 1) * S], dt_pt[:, et * P:(et + 1) * P], bcd[2 * DS:2 * DS + DR, cols],
                             start=True, stop=True)
                ins.then_inc(*psum.filled.inc())
                yield
                yield
                yield
                yield

            def qkv0(t):
                for name, c0, c1 in (("qk0", 0, 512), ("v0", 512, 768)):
                    ps = psum.take(pe, name, t)
                    for k in range(KD):
                        ins = mm(ps[:, 0:c1 - c0], x0_feat[:, k, t * P:(t + 1) * P], w_qkv[:, k, c0:c1],
                                 start=(k == 0), stop=(k == KD - 1))
                    ins.then_inc(*psum.filled.inc())

            def attn0(b):
                pe.wait_ge(*loaded("ld_attn0"))
                for i in range(4):
                    for t in qkv0_steps[b][i]:
                        qkv0(t)
                    yield
                pe.wait_ge(*sg["o0_ready"].nth(b))
                pe.wait_ge(*loaded("ld_const"))
                turn("o0t", b, lambda h, k: qkv[:, 2 * b + h, k * P:(k + 1) * P])
                yield
                yield
                pe.wait_ge(*psum.empty("o0t", b))
                project("proj0", b, lambda h, k: xx_feat[:, k, h * P:(h + 1) * P], w_o0)
                yield
                yield

            def ssm(b):
                for _ in range(DS + 5):
                    yield
                pe.wait_ge(*sg["y_ready"].nth(b))
                ps = psum.take(pe, "yt", b)
                for lt in range(2):
                    for et in range(2):
                        ins = tr(ps[:, lt * DI + et * P:lt * DI + (et + 1) * P], y_sum[:, et, lt * P:(lt + 1) * P],
                                 ident[:, :])
                ins.then_inc(*psum.filled.inc())
                yield
                yield

            def moe0(b):
                pe.wait_ge(*sg["x2_ready"].nth(2 * b + 1))
                pe.wait_ge(*loaded("ld_moe0"))
                turn("x2t", b, lambda h, k: x_tok[:, 2 * b + h, k * P:(k + 1) * P])
                yield
                pe.wait_ge(*psum.empty("x2t", b))
                ps = psum.take(pe, "gate0", b)
                for h in range(2):
                    for k in range(KD):
                        ins = mm(ps[:, h * E:(h + 1) * E], x_feat[:, k, h * P:(h + 1) * P], w_r[:, k, :],
                                 start=(k == 0), stop=(k == KD - 1))
                ins.then_inc(*psum.filled.inc())
                ps = psum.take(pe, "hid0", b)
                for k in range(KD):
                    ins = mm(ps[:, 0:S], w_d[:, k, :], x_feat[:, k, :], start=(k == 0), stop=(k == KD - 1))
                ins.then_inc(*psum.filled.inc())
                yield
                yield
                yield
                yield
                pe.wait_ge(*sg["w_ready"].nth(b))
                ps = psum.take(pe, "wt0", b)
                for h in range(2):
                    ins = tr(ps[0:E, h * P:(h + 1) * P], g8[:, 9, h, :], ident[:, :])
                ins.then_inc(*psum.filled.inc())
                yield
                yield
                pe.wait_ge(*psum.empty("wt0", b))
                ps = psum.take(pe, "spread0", b)
                mm(ps[:, 0:S], spread[:, :], w_e_t[:, :], start=True, stop=True).then_inc(*psum.filled.inc())
                yield
                yield
                pe.wait_ge(*psum.empty("spread0", b))
                ps = psum.take(pe, "out0", b)
                for h in range(2):
                    mm(ps[:, h * D:(h + 1) * D], h_w[:, h * P:(h + 1) * P], w_u[:, :], start=True, stop=False)
                    ins = mm(ps[:, h * D:(h + 1) * D], w_e_t[:, h * P:(h + 1) * P], b_u[:, :], start=False, stop=True)
                ins.then_inc(*psum.filled.inc())
                yield
                yield

            def attn1(b):
                pe.wait_ge(*sg["x3_ready"].nth(2 * b + 1))
                pe.wait_ge(*loaded("ld_attn1"))
                turn("x3t", b, lambda h, k: x_tok[:, 2 * b + h, k * P:(k + 1) * P])
                yield
                pe.wait_ge(*psum.empty("x3t", b))
                for h in range(2):
                    ps = psum.take(pe, "qk1", b, h)
                    for k in range(KD):
                        ins = mm(ps[:, :], x_feat[:, k, h * P:(h + 1) * P], w_qk1[:, k, :],
                                 start=(k == 0), stop=(k == KD - 1))
                    ins.then_inc(*psum.filled.inc())
                project("v1", b, lambda h, k: x_feat[:, k, h * P:(h + 1) * P], w_v1)
                yield
                pe.wait_ge(*sg["qk_ready"].nth(2 * b + 1))
                for name, c0 in (("q1t", 0), ("k1t", D)):
                    ps = psum.take(pe, name, b)
                    for k in range(KD):
                        for h in range(2):
                            ins = tr(ps[:, k * S + h * P:k * S + (h + 1) * P],
                                     qk_rot[:, h, c0 + k * P:c0 + (k + 1) * P], ident[:, :])
                    ins.then_inc(*psum.filled.inc())
                yield
                yield
                yield
                pe.wait_ge(*psum.empty("q1t", b))
                pe.wait_ge(*psum.empty("v1", b))
                pe.wait_ge(*sg["ones_ready"].nth(0))
                causal = mask_qk[:, :].unsqueeze(1)
                for g in range(4 + 2):
                    if 1 <= g < 5:
                        c = g - 1
                        pe.wait_ge(*psum.empty("s1a", b, c))
                        ps = psum.take(pe, "pta", b, c)
                        for j in range(4):
                            ins = tr(ps[:, j * P:(j + 1) * P], p_qk[:, c % 2, j, :], ident[:, :])
                        ins.then_inc(*psum.filled.inc())
                    if g < 4:
                        pe.wait_ge(*sg["khead_ready"].nth(b * HEADS + 4 * g + 3))
                        ps = psum.take(pe, "s1a", b, g)
                        mm(ps[:, :], q_feat[:, g // 2, 0:P], k_head[:, g % 2, :, 0:P], start=True, stop=False)
                        mm(ps[:, :], ident_bf[:, :], causal.broadcast_to([P, 4, P]),
                           start=False, stop=True).then_inc(*psum.filled.inc())
                    yield
                    if 1 <= g < 5:
                        c = g - 1
                        for i in range(2):
                            pe.wait_ge(*psum.empty("s1b", b, 2 * c + 1))
                            ps = psum.take(pe, "ptb", b, c, i)
                            for j in range(4):
                                ins = tr(ps[:, j * P:(j + 1) * P], p_qk[:, c % 2, 4 + 2 * j + i, :], ident[:, :])
                            ins.then_inc(*psum.filled.inc())
                    if g < 4:
                        for i in range(2):
                            ps = psum.take(pe, "s1b", b, 2 * g + i)
                            mm(ps[:, :], q_feat[:, g // 2, P:S], k_head[:, g % 2, 2 * i:2 * i + 2, :],
                               start=True, stop=False)
                            mm(ps[:, :].rearrange("p (h k) -> p h k", h=2)[:, :, P:S], ident_bf[:, :],
                               causal.broadcast_to([P, 2, P]), start=False, stop=True).then_inc(*psum.filled.inc())
                    if g >= 2:
                        c = g - 2
                        pe.wait_ge(*psum.empty("pta", b, c))
                        pe.wait_ge(*psum.empty("ptb", b, c, 0))
                        pe.wait_ge(*psum.empty("ptb", b, c, 1))
                        ps = psum.take(pe, "ov1", b, c)
                        for j in range(4):
                            h = 4 * c + j
                            o = ps[32 * j:32 * j + 32, 0:S]
                            mm(o, v_aug[:, 0, h, :], p_t0[:, c % 2, j, :], start=True, stop=False)
                            ins = mm(o[:, P:S], v_aug[:, 1, h, :], p_t1[:, c % 2, j, :], start=False, stop=True)
                        ins.then_inc(*psum.filled.inc())
                    yield
                for h in range(2):
                    for c in range(4):
                        pe.wait_ge(*psum.empty("ov1", b, c))
                    ps = psum.take(pe, "on1", b, h)
                    for g in range(4):
                        ins = tr(ps[:, g * P:(g + 1) * P], o_heads[:, g, h * P:(h + 1) * P], ident[:, :])
                    ins.then_inc(*psum.filled.inc())
                yield
                pe.wait_ge(*psum.empty("on1", b, 0))
                pe.wait_ge(*psum.empty("on1", b, 1))
                turn("o1t", b, lambda h, k: o_norm[:, h, k * P:(k + 1) * P])
                yield
                pe.wait_ge(*psum.empty("o1t", b))
                project("proj1", b, lambda h, k: o_feat[:, k, h * P:(h + 1) * P], w_o1)
                yield
                yield

            def fold(_):
                pe.wait_ge(*loaded("ld_xattn"))
                for h in range(XH):
                    ps = x_psum.take(pe, "fold", h)
                    for k in range(KD):
                        mm(ps[:, k * XD:(k + 1) * XD], m_q[:, h, k, :], wx_k[:, h // 2, :], start=True, stop=True)
                    mm(ps[:, D:2 * D], wx_v[:, h // 2, :], m_o[:, h, :], start=True, stop=True).then_inc(
                        *x_psum.filled.inc())
                    if h % 2:
                        yield

            def xattn(b):
                pe.wait_ge(*loaded("ld_ctx"))
                pe.wait_ge(*x_psum.empty("fold", XH - 1))
                pe.wait_ge(*sg["x4_ready"].nth(2 * b + 1))
                turn("x4t", b, lambda h, k: x_tok[:, 2 * b + h, k * P:(k + 1) * P], x_psum)
                pe.wait_ge(*x_psum.empty("x4t", b))
                acc = o_psum.take(pe, "ox", b)
                yield
                for i in range(XH + 5):
                    if i >= 5:
                        h = i - 5
                        pe.wait_ge(*x_psum.empty("pvx", b, h))
                        for qt in range(2):
                            ins = mm(acc[:, qt * D:(qt + 1) * D], ox_feat[:, h % 2, qt * P:(qt + 1) * P],
                                     m_o[:, h, :],
                                     start=(h == 0 and qt == 0), stop=(h == XH - 1), skip_group_check=True)
                        ins.then_inc(*(o_psum.filled if h == XH - 1 else sg["ox_used"]).inc())
                    if 4 <= i < XH + 4:
                        h = i - 4
                        pe.wait_ge(*x_psum.empty("pxt", b, h))
                        ps = x_psum.take(pe, "pvx", b, h)
                        for kt in range(2):
                            ins = mm(ps[:, 0:S], ctx_tok[:, 2 * b + kt, :], px_t[:, h % 2, kt, :],
                                     start=(kt == 0), stop=(kt == 1))
                        ins.then_inc(*x_psum.filled.inc())
                    yield
                    if 1 <= i < XH + 1:
                        h = i - 1
                        pe.wait_ge(*x_psum.empty("qx", b, h))
                        ps = x_psum.take(pe, "sx", b, h)
                        for qt in range(2):
                            ins = mm(ps[:, qt * S:(qt + 1) * S], qx_feat[:, h % 2, qt * P:(qt + 1) * P],
                                     ctx_t[:, b * S:(b + 1) * S], start=True, stop=True)
                        ins.then_inc(*x_psum.filled.inc())
                    if 3 <= i < XH + 3:
                        h = i - 3
                        pe.wait_ge(*sg["pn_ready"].nth(2 * (b * XH + h) + 1))
                        ps = x_psum.take(pe, "pxt", b, h)
                        for kt in range(2):
                            for qt in range(2):
                                ins = tr(ps[:, kt * S + qt * P:kt * S + (qt + 1) * P],
                                         px[:, h % NX, qt, kt * P:(kt + 1) * P], ident[:, :])
                        ins.then_inc(*x_psum.filled.inc())
                    if i < XH:
                        ps = x_psum.take(pe, "qx", b, i)
                        for k in range(KD):
                            ins = mm(ps[:, 0:S], m_q[:, i, k, :], xx_feat[:, k, :],
                                     start=(k == 0), stop=(k == KD - 1))
                        ins.then_inc(*x_psum.filled.inc())
                    yield
                yield

            run_layers(ssm_front=ssm_front, attn0=attn0, ssm=ssm, moe0=moe0, attn1=attn1, fold=fold, xattn=xattn)

            def to_features(t):
                pe.wait_ge(*sg["x5_ready"].nth(t + 1))
                pe.wait_ge(*seen(B * DS - 1))
                turn("x5t", t, lambda h, k: x_tok[:, t + h, k * P:(k + 1) * P])

            def route(name, tiles):
                ps = psum.take(pe, name)
                for i, t in enumerate(tiles):
                    pe.wait_ge(*psum.empty("x5t", t // 2 * 2))
                    for k in range(KD):
                        ins = mm(ps[:, i * E:(i + 1) * E], x5_feat[:, k, t * P:(t + 1) * P], w_g[:, k, :],
                                 start=(k == 0), stop=(k == KD - 1))
                ins.then_inc(*psum.filled.inc())

            def shared_hidden(hf, chunks):
                for c in chunks:
                    c0, m = HC[c]
                    for name, w in (("sh1", ws_1), ("sh3", ws_3)):
                        ps = x_psum.take(pe, name, hf, c)
                        for k in range(KD):
                            ins = mm(ps[0:m, :], w[:, k, c0:c0 + m], x5_feat[:, k, hf * 512:(hf + 1) * 512],
                                     start=(k == 0), stop=(k == KD - 1))
                        ins.then_inc(*x_psum.filled.inc())

            def shared_out(hf):
                pe.wait_ge(*loaded("ld_ws2"))
                for c in range(3):
                    pe.wait_ge(*x_psum.empty("sh3", hf, c))
                for t in range(0, 4, 2):
                    ps = psum.take(pe, "sh2", hf, t)
                    for i in range(2):
                        for c, (c0, m) in enumerate(HC):
                            ins = mm(ps[:, i * D:(i + 1) * D], hs[0:m, c, (t + i) * P:(t + i + 1) * P],
                                     ws_2[0:m, c, :],
                                     start=(c == 0), stop=(c == 2))
                    ins.then_inc(*psum.filled.inc())

            pe.wait_ge(*loaded("ld_route"))
            pe.wait_ge(*loaded("ld_shared"))
            for t in range(0, NT - 2, 2):
                to_features(t)
            route("route0", range(NT - 2))
            shared_hidden(0, (0,))
            to_features(NT - 2)
            route("route1", range(NT - 2, NT))
            shared_hidden(0, (1, 2))
            pe.wait_ge(*sg["oh_ready"].nth(0))
            ps = psum.take(pe, "pos")
            for t in range(NT):
                for j in range(t):
                    mm(ps[:, t * E:(t + 1) * E], ones, oh_bf[:, j, :], start=(j == 0), stop=False)
                ins = mm(ps[:, t * E:(t + 1) * E], tri, oh_bf[:, t, :], start=(t == 0), stop=True)
            ins.then_inc(*psum.filled.inc())
            shared_out(0)
            shared_hidden(1, (0, 1, 2))
            shared_out(1)
            pe.wait_ge(*sg["xd_loaded"].nth(0, 16))
            for e in range(0, E, 2):
                turn("xdt", e, lambda h, k: xd_tok[:, e + h, k * P:(k + 1) * P])
            pe.wait_ge(*loaded("ld_w13"))
            pe.wait_ge(*loaded("ld_w2"))
            for e in range(E + 1):
                if e < E:
                    pe.wait_ge(*psum.empty("xdt", e // 2 * 2))
                    for name, w in (("e1", w_1), ("e3", w_3)):
                        ps = psum.take(pe, name, e)
                        for c, (c0, m) in enumerate(HC):
                            for k in range(KD):
                                ins = mm(ps[0:m, c * P:(c + 1) * P], w[:, e, k, c0:c0 + m],
                                         xd_feat[:, k, e * P:(e + 1) * P], start=(k == 0), stop=(k == KD - 1))
                        ins.then_inc(*psum.filled.inc())
                if e:
                    pe.wait_ge(*psum.empty("e3", e - 1))
                    ps = psum.take(pe, "e2", e - 1)
                    for c, (c0, m) in enumerate(HC):
                        ins = mm(ps[:, 0:D], e_hid[0:m, (e - 1) % 2, c * P:(c + 1) * P], w_2[0:m, e - 1, c, :],
                                 start=(c == 0), stop=(c == 2))
                    ins.then_inc(*psum.filled.inc())

        @block.vector
        def _(eng):
            v = Engine(eng)
            V = nc.vector

            def lk(ins, signal=None):
                ins.then_inc(*(signal or sg["dve_step"]).inc())
                v.wait_ge(*last())

            norms = [0, {}]

            def norm_stats(b, get, k=0):
                get(k)
                v.wait_ge(*last())
                for h in range(2):
                    V.bn_stats(ln_st[:, k, h, :], ln_r[:, k, h, :]).then_inc(*sg["dve_step"].inc())
                v.wait_ge(*last())
                for h in range(2):
                    V.bn_aggr(ln_mv[:, k, h, :], ln_st[:, k, h, :]).then_inc(*sg["dve_step"].inc())
                v.wait_ge(*last())
                V.tensor_scalar(ln_var[:, k, :], ln_mv[:, k, :, 1], EPS, None,
                                ALU.add).then_inc(*sg["var_ready"].inc())
                norms[1][k] = norms[0]
                norms[0] += 1

            def norm_scale(b, done, k=0):
                v.wait_ge(*sg["rstd_ready"].nth(norms[1][k]))
                for h in range(2):
                    V.tensor_scalar(x_tok[:, 2 * b + h, :], ln_r[:, k, h, :], ln_mv[:, k, h, 0:1],
                                    ln_rs[:, k, h:h + 1], ALU.subtract, ALU.mult).then_inc(*done.inc())
                v.wait_ge(*last())

            def add_branch(b, name, *use):
                def get(k):
                    ps = psum.get(v, name, *use)
                    V.tensor_tensor(ln_r[:, k, :, :].rearrange("p a b -> p (a b)"), ps[:, :],
                                    T2(x_tok, b).rearrange("p a b -> p (a b)"),
                                    ALU.add).then_inc(*psum.drain(name, *use).inc())
                return get

            v.wait_ge(*loaded("ld_ssm"))
            v.wait_ge(*sg["a_exp"].nth(0))
            V.tensor_scalar(a_neg[:, :, :], ssm_p[:, :, 7:23], -1.0, None, ALU.mult).then_inc(*sg["a_ready"].inc())
            def ssm_front(b):
                yield
                v.wait_ge(*psum.empty("xin", b))
                v.wait_ge(*sg["pads_clear"].nth(0))
                if b:
                    v.wait_ge(*sg["u_ready"].nth(2 * b - 1))
                for j in range(DC):
                    for et in range(2):
                        o, src = tmp_a[:, et, :], x_pad[:, et, j:j + S]
                        if j == 0:
                            V.tensor_scalar(o, src, ssm_p[:, et, 0:1], ssm_p[:, et, 4:5],
                                            ALU.mult, ALU.add).then_inc(*sg["dve_step"].inc())
                        else:
                            V.scalar_tensor_tensor(o, src, ssm_p[:, et, j:j + 1], o, ALU.mult, ALU.add).then_inc(
                                *(sg["conv_ready"] if j == DC - 1 else sg["dve_step"]).inc())
                    v.wait_ge(*last())
                yield
                yield
                xb, d_u = delta[:, :, b, :], du[:, :, b, :]
                ps = psum.get(v, "dp", b)
                v.wait_ge(*sg["size_ready"].nth(2 * b + 1))
                for et in range(2):
                    V.tensor_scalar(xb[:, et, :], ps[:, et * S:(et + 1) * S], ssm_p[:, et, 5:6], 0.0,
                                    ALU.add, ALU.max).then_inc(*(psum.drain("dp", b) if et else sg["dve_step"]).inc())
                v.wait_ge(*last())
                yield
                v.wait_ge(*sg["softplus_t"].nth(b))
                lk(V.tensor_scalar(tmp_a, tmp_b, 1.0, None, ALU.add), sg["softplus_w"])
                yield
                v.wait_ge(*sg["softplus_ln"].nth(b))
                lk(V.scalar_tensor_tensor(tmp_a, tmp_a, -1.0, tmp_b, ALU.add, ALU.subtract))
                lk(V.tensor_tensor(tmp_a, d_u, tmp_a, ALU.subtract))
                lk(V.tensor_tensor(xb, xb, tmp_a, ALU.add), sg["softplus_ready"])
                yield
                yield

            kv = qkv.rearrange("p (m n) c -> p n m c", n=2)

            def attn0(b):
                m = b + 1
                yield
                for t in range(2 * b, 2 * b + 2):
                    v.wait_ge(*psum.empty("qk0", t))
                    v.wait_ge(*psum.empty("v0", t))
                for n in range(2):
                    q = kv[:, n, b, 0:D].unsqueeze(1).broadcast_to([P, m, D])
                    lk(V.tensor_tensor(prod0[:, 0:m, :], q, kv[:, n, 0:m, D:2 * D], ALU.mult))
                    lk(V.tensor_reduce(s0[:, n, :, 0:m].rearrange("p h m -> p m h"),
                                       prod0[:, 0:m, :].rearrange("p m (h d) -> p m h d", h=HEADS), AX.X, ALU.add))
                sm = s0[:, :, :, 0:m]
                wide = s0_stat.unsqueeze(3).broadcast_to([P, 2, HEADS, m])
                lk(V.tensor_reduce(s0_stat, sm, AX.X, ALU.max))
                lk(V.tensor_tensor(sm, sm, wide, ALU.subtract), sg["s0_arg"])
                yield
                v.wait_ge(*sg["s0_exp"].nth(b))
                lk(V.tensor_reduce(s0_stat, sm, AX.X, ALU.add))
                lk(V.reciprocal(s0_stat, s0_stat))
                lk(V.tensor_tensor(sm, sm, wide, ALU.mult))
                yield
                for n in range(2):
                    o = prod0.rearrange("p a b -> p (a b)")[:, 0:D * m].rearrange(
                        "p (h d m) -> p h d m", h=HEADS, m=m)
                    pr = s0[:, n, :, 0:m].unsqueeze(2).broadcast_to([P, HEADS, DH, m])
                    vv = kv[:, n, 0:m, 2 * D:3 * D].rearrange("p m (h d) -> p h d m", h=HEADS)
                    lk(V.tensor_tensor(o, pr, vv, ALU.mult))
                    lk(V.tensor_reduce(kv[:, n, b, 0:D].rearrange("p (h d) -> p h d", h=HEADS), o, AX.X, ALU.add),
                       sg["o0_ready"] if n else None)
                yield
                yield
                yield
                v.wait_ge(*loaded("ld_x"))
                norm_stats(b, add_branch(b, "proj0", b), 1)
                yield
                norm_scale(b, sg["x1_ready"], 1)
                yield

            def ssm(b):
                v.wait_ge(*sg["delta_ready"].nth(b))
                v.wait_ge(*sg["decay_clear"].nth(0))
                scanned = {}
                driven = {}
                for i in range(DS + 2):
                    if i < DS and not b:
                        v.wait_ge(*bc_here(i))
                        if i >= NB:
                            v.wait_ge(*scanned[i - NB])
                        V.tensor_tensor(drive[:, i % NB, :, :], du[:, :, b, :],
                                        bc_all[:, i % NBC, 0, :].unsqueeze(1).broadcast_to([P, 2, S]),
                                        ALU.mult).then_inc(*sg["dve_step"].inc())
                        driven[i] = last()
                    if 1 <= i <= DS:
                        k = b * DS + i - 1
                        v.wait_ge(*sg["decay_ready"].nth(2 * k + 1))
                        v.wait_ge(*(sg["drive_ready"].nth(k - DS) if b else driven[k]))
                        if k >= NSTATE:
                            v.wait_ge(*added(k - NSTATE))
                        V.tensor_tensor_scan(state[:, k % NSTATE, :, :].rearrange("p e s -> p (e s)"),
                                             decay[:, k % NB, :, :].rearrange("p e s -> p (e s)"),
                                             drive[:, k % NB, :, :].rearrange("p e s -> p (e s)"),
                                             0.0, ALU.mult, ALU.add).then_inc(*sg["decay_used"].inc())
                        scanned[k] = last()
                    if i >= 2 and not i % 2:
                        k = b * DS + i - 2
                        v.wait_ge(*bc_here(k))
                        v.wait_ge(*scanned[k])
                        V.tensor_tensor(state[:, k % NSTATE, :, :], state[:, k % NSTATE, :, :],
                                        bc_all[:, k % NBC, 1, :].unsqueeze(1).broadcast_to([P, 2, S]),
                                        ALU.mult).then_inc(*sg["seen_even"].inc())
                    yield
                yield
                v.wait_ge(*sg["y_added"].nth((b + 1) * (DS - 1) - 1))
                for et in range(2):
                    V.scalar_tensor_tensor(y_sum[:, et, :], u[:, et, b, :], ssm_p[:, et, 6:7], y_sum[:, et, :],
                                           ALU.mult, ALU.add).then_inc(*sg["dve_step"].inc())
                v.wait_ge(*last())
                v.wait_ge(*sg["silu_z_ready"].nth(b))
                V.tensor_tensor(y_sum[:, :, :], y_sum[:, :, :], silu_z[:, :, :], ALU.mult).then_inc(
                    *sg["y_ready"].inc())
                yield
                yield
                norm_stats(b, add_branch(b, "yt", b), 2)
                yield
                norm_scale(b, sg["x2_ready"], 2)
                yield

            def first_of_max(g, score, hit, stat, rev, n, signal=None):
                shape = list(g.shape)
                lk(V.tensor_reduce(stat, g, AX.X, ALU.max))
                lk(V.tensor_tensor(hit, g, stat.unsqueeze(2).broadcast_to(shape), ALU.is_equal))
                lk(V.tensor_tensor(score, hit, rev.unsqueeze(1).broadcast_to(shape), ALU.mult))
                lk(V.tensor_reduce(stat, score, AX.X, ALU.max))
                lk(V.tensor_tensor(hit, score, stat.unsqueeze(2).broadcast_to(shape), ALU.is_equal), signal)

            def moe0(b):
                v.wait_ge(*loaded("ld_moe0"))
                v.wait_ge(*loaded("ld_const"))
                G = [g8[:, i, :, :] for i in range(10)]
                stat = small[:, 8:10]
                if b:
                    v.wait_ge(*psum.full("wt0", b - 1))
                yield
                ps = psum.get(v, "gate0", b)
                lk(V.scalar_tensor_tensor(G[0], ps[:, 0:2 * E].rearrange("p (h e) -> p h e", h=2), float(BONUS),
                                          b_r[:, :].unsqueeze(1).broadcast_to([P, 2, E]), ALU.add, ALU.add),
                   psum.drain("gate0", b))
                lk(V.tensor_reduce(stat, G[0], AX.X, ALU.max))
                lk(V.tensor_tensor(G[0], G[0], stat.unsqueeze(2).broadcast_to([P, 2, E]), ALU.subtract),
                   sg["gate_arg"])
                yield
                v.wait_ge(*sg["gate_exp"].nth(b))
                first_of_max(G[1], G[2], G[3], stat, eid_rev[:, :], 2)
                lk(V.scalar_tensor_tensor(G[4], G[3], -4.0, G[1], ALU.mult, ALU.add))
                yield
                first_of_max(G[4], G[5], G[6], stat, eid_rev[:, :], 2)
                lk(V.tensor_tensor(G[7], G[3], G[6], ALU.add))
                lk(V.tensor_tensor(G[8], G[7], G[1], ALU.mult))
                lk(V.tensor_reduce(stat, G[8], AX.X, ALU.add))
                lk(V.reciprocal(stat, stat))
                lk(V.tensor_tensor(G[9], G[8], stat.unsqueeze(2).broadcast_to([P, 2, E]), ALU.mult), sg["w_ready"])
                yield
                yield
                ps = psum.get(v, "wt0", b)
                V.tensor_copy(w_e_t[:, :], ps[0:E, 0:S]).then_inc(*psum.drain("wt0", b).inc())
                yield
                yield
                v.wait_ge(*psum.empty("hid0", b))
                ps = psum.get(v, "spread0", b)
                lk(V.tensor_tensor(h_w[:, :], h_relu[:, :], ps[:, 0:S], ALU.mult), psum.drain("spread0", b))
                yield
                yield
                norm_stats(b, add_branch(b, "out0", b))
                yield
                norm_scale(b, sg["x3_ready"])
                yield

            def attn1(b):
                yield
                v.wait_ge(*loaded("ld_rope"))
                for h in range(2):
                    ps = psum.get(v, "qk1", b, h)[:, :].rearrange("p (g i c) -> p g i c", i=8, c=2)
                    dst = qk_rot[:, h, :].rearrange("p (g i c) -> p g i c", i=8, c=2)
                    tb = rot_b.rearrange("p (g i c) -> p g i c", i=8, c=2)
                    cos, nsin, sin = (rope[:, h, i, :].unsqueeze(1).broadcast_to([P, 32, 8]) for i in range(3))
                    if b and not h:
                        v.wait_ge(*psum.full("k1t", b - 1))
                    V.tensor_tensor(dst[:, :, :, 0], ps[:, :, :, 0], cos, ALU.mult).then_inc(*sg["dve_step"].inc())
                    V.tensor_tensor(dst[:, :, :, 1], ps[:, :, :, 1], cos, ALU.mult).then_inc(*sg["dve_step"].inc())
                    V.tensor_tensor(tb[:, :, :, 0], ps[:, :, :, 1], nsin, ALU.mult).then_inc(*sg["dve_step"].inc())
                    lk(V.tensor_tensor(tb[:, :, :, 1], ps[:, :, :, 0], sin, ALU.mult), psum.drain("qk1", b, h))
                    lk(V.tensor_tensor(qk_rot[:, h, :], qk_rot[:, h, :], rot_b, ALU.add), sg["qk_ready"])
                yield
                yield
                v.wait_ge(*psum.empty("k1t", b))

                def keys(g):
                    for j in range(4):
                        if g >= 2 or b:
                            v.wait_ge(*psum.full("s1b", b if g >= 2 else b - 1, 2 * ((g - 2) % 4) + 1))
                        h = 4 * g + j
                        V.tensor_scalar(k_head[:, g % 2, j, :], k_feat[:, h // 8, :],
                                        head_of[:, h % 8:h % 8 + 1], None,
                                        ALU.mult).then_inc(*sg["khead_ready"].inc())

                keys(0)
                yield
                keys(1)
                yield
                for g in range(4):
                    if g >= 2 or b:
                        v.wait_ge(*psum.empty("s1b", b if g >= 2 else b - 1, 2 * ((g - 2) % 4) + 1))
                    ps = psum.get(v, "s1a", b, g)
                    V.tensor_reduce(neg_max[:, g % 2, 0:4], ps[:, :].rearrange("p (h k) -> p h k", h=4),
                                    AX.X, ALU.max, negate=True).then_inc(*sg["max_ready"].inc())
                    yield
                    for i in range(2):
                        ps = psum.get(v, "s1b", b, 2 * g + i)
                        V.tensor_reduce(neg_max[:, g % 2, 4 + 2 * i:6 + 2 * i],
                                        ps[:, :].rearrange("p (h k) -> p h k", h=2),
                                        AX.X, ALU.max, negate=True).then_inc(*sg["max_ready"].inc())
                    if g < 2:
                        keys(g + 2)
                    yield
                for _ in range(4):
                    yield
                for h in range(2):
                    ps = psum.get(v, "on1", b, h)[:, :].rearrange("p (h c) -> p h c", h=HEADS)
                    if b and not h:
                        v.wait_ge(*psum.full("o1t", b - 1))
                    lk(V.reciprocal(o_den[:, h, :], ps[:, :, DH]))
                    lk(V.tensor_tensor(o_norm[:, h, :].rearrange("p (h d) -> p h d", h=HEADS), ps[:, :, 0:DH],
                                       o_den[:, h, :].unsqueeze(2).broadcast_to([P, HEADS, DH]), ALU.mult),
                       psum.drain("on1", b, h))
                yield
                yield
                norm_stats(b, add_branch(b, "proj1", b))
                yield
                norm_scale(b, sg["x4_ready"])
                yield

            def fold(_):
                for _ in range(STEPS["fold"]):
                    yield

            def xattn(b):
                if not b:
                    v.wait_ge(*loaded("ld_mask"))
                    lk(V.tensor_scalar(mask_add.rearrange("p b s -> p (b s)"), mask_raw, -NEG, NEG,
                                       ALU.mult, ALU.add))
                    lk(V.tensor_reduce(mask_any, mask_raw.rearrange("p (b s) -> p b s", b=B), AX.X, ALU.max))
                yield
                for i in range(XH + 5):
                    if 2 <= i < XH + 2:
                        h = i - 2
                        j = h % NX
                        v.wait_ge(*sg["sexp_ready"].nth(2 * (b * XH + h) + 1))
                        lk(V.reciprocal(x_inv[:, j, :], x_sum[:, j, :]))
                        for qt in range(2):
                            V.tensor_scalar(px[:, j, qt, :], px[:, j, qt, :], x_inv[:, j, qt:qt + 1],
                                            mask_any[:, b:b + 1], ALU.mult, ALU.mult).then_inc(*sg["pn_ready"].inc())
                    yield
                    if 1 <= i < XH + 1:
                        h = i - 1
                        j = h % NX
                        ps = x_psum.get(v, "sx", b, h)
                        if h >= NX:
                            v.wait_ge(*x_psum.full("pxt", b, h - NX))
                        for qt in range(2):
                            V.tensor_tensor_reduce(px[:, j, qt, :], ps[:, qt * S:(qt + 1) * S], mask_add[:, b, :],
                                                   XSCALE, -3e38, ALU.add, ALU.max, x_max[:, j, qt:qt + 1]
                                                   ).then_inc(
                                                       *(x_psum.drain("sx", b, h) if qt else sg["dve_step"]).inc())
                        v.wait_ge(*last())
                        V.tensor_scalar(x_nmax[:, j, :], x_max[:, j, :], -1.0, None,
                                        ALU.mult).then_inc(*sg["smax_ready"].inc())
                    if 3 <= i < XH + 3:
                        h = i - 3
                        ps = x_psum.get(v, "pxt", b, h)
                        if h >= 2:
                            v.wait_ge(*x_psum.full("pvx", b, h - 2))
                        V.tensor_copy(px_t[:, h % 2, :, :].rearrange("p a b -> p (a b)"),
                                      ps[:, :]).then_inc(*x_psum.drain("pxt", b, h).inc())
                    yield

                def get(k):
                    ps = o_psum.get(v, "ox", b)
                    V.tensor_tensor(ln_r[:, k, :, :].rearrange("p a b -> p (a b)"), ps[:, :],
                                    T2(x_tok, b).rearrange("p a b -> p (a b)"),
                                    ALU.add).then_inc(*o_psum.drain("ox", b).inc())
                norm_stats(b, get, 1)
                norm_scale(b, sg["x5_ready"], 1)
                yield

            run_layers(ssm_front=ssm_front, attn0=attn0, ssm=ssm, moe0=moe0, attn1=attn1, fold=fold, xattn=xattn)

            RR = [r8[:, i, :, :] for i in range(8)]
            Q1 = [r1[:, i, :] for i in range(8)]
            v.wait_ge(*loaded("ld_route"))
            v.wait_ge(*o_psum.empty("ox", B - 1))

            def shared(hf, chunks):
                for c in chunks:
                    m = HC[c][1]
                    v.wait_ge(*x_psum.empty("sh1", hf, c))
                    ps = x_psum.get(v, "sh3", hf, c)
                    lk(V.tensor_tensor(hs[0:m, c, :], hs[0:m, c, :], ps[0:m, :], ALU.mult),
                       x_psum.drain("sh3", hf, c))

            for name, t0, t1 in (("route0", 0, NT - 2), ("route1", NT - 2, NT)):
                ps = psum.get(v, name)
                lk(V.tensor_copy(RR[0][:, t0:t1, :], ps[:, 0:(t1 - t0) * E].rearrange("p (t e) -> p t e", e=E)),
                   psum.drain(name))
                if not t0:
                    shared(0, (0,))
            lk(V.tensor_reduce(Q1[0], RR[0], AX.X, ALU.max))
            lk(V.tensor_tensor(RR[0], RR[0], Q1[0].unsqueeze(2).broadcast_to([P, NT, E]), ALU.subtract),
               sg["route_arg"])
            v.wait_ge(*sg["route_exp"].nth(0))
            lk(V.tensor_reduce(Q1[1], RR[1], AX.X, ALU.add))
            lk(V.reciprocal(Q1[1], Q1[1]))
            lk(V.tensor_tensor(RR[1], RR[1], Q1[1].unsqueeze(2).broadcast_to([P, NT, E]), ALU.mult))
            first_of_max(RR[1], RR[2], RR[3], Q1[2], eid_rev[:, :], NT)
            lk(V.tensor_copy(oh_bf[:, :, :], RR[3]), sg["oh_ready"])
            lk(V.tensor_tensor(RR[4], RR[3], RR[1], ALU.mult))
            lk(V.tensor_reduce(Q1[3], RR[4], AX.X, ALU.add))
            shared(0, (1, 2))
            ps = psum.get(v, "pos")
            lk(V.tensor_tensor(RR[5], RR[3], ps[:, 0:NT * E].rearrange("p (t e) -> p t e", t=NT), ALU.mult),
               psum.drain("pos"))
            lk(V.tensor_reduce(Q1[4], RR[5], AX.X, ALU.add))
            lk(V.tensor_tensor(RR[6], RR[3], ebase.unsqueeze(1).broadcast_to([P, NT, E]), ALU.mult))
            lk(V.tensor_reduce(Q1[5], RR[6], AX.X, ALU.add))
            lk(V.tensor_tensor(Q1[5], Q1[5], Q1[4], ALU.add))
            lk(V.tensor_scalar(Q1[6], Q1[4], float(CAP), None, ALU.is_le))
            lk(V.tensor_tensor(Q1[3], Q1[3], Q1[6], ALU.mult))
            lk(V.tensor_tensor(Q1[5], Q1[5], Q1[6], ALU.mult))
            lk(V.tensor_copy(slot_u[:, 1, :], Q1[5]))
            lk(V.tensor_tensor(Q1[7], dump, Q1[6], ALU.mult))
            lk(V.tensor_tensor(Q1[7], dump, Q1[7], ALU.subtract))
            lk(V.tensor_tensor(Q1[7], Q1[7], Q1[5], ALU.add))
            lk(V.tensor_copy(slot_u[:, 0, :], Q1[7]), sg["slots_ready"])

            def shared_add(hf):
                for t in range(0, 4, 2):
                    ps = psum.get(v, "sh2", hf, t)
                    xt = x_tok[:, 4 * hf + t:4 * hf + t + 2, :].rearrange("p a b -> p (a b)")
                    V.tensor_tensor(xt, xt, ps[:, :], ALU.add).then_inc(*psum.drain("sh2", hf, t).inc())

            v.wait_ge(*sg["xd_scattered"].nth(NT - 1, 16))
            shared_add(0)
            shared(1, range(3))
            shared_add(1)
            for e in range(0, E, 2):
                ps = psum.get(v, "xdt", e)
                V.tensor_copy(xd_feat[:, :, e * P:(e + 2) * P], ps[:, :].rearrange("p (k t) -> p k t", k=KD)).then_inc(
                    *psum.drain("xdt", e).inc())
            for e in range(E):
                ps = psum.get(v, "e3", e)
                v.wait_ge(*psum.empty("e1", e))
                if e >= 2:
                    v.wait_ge(*psum.full("e2", e - 2))
                V.tensor_tensor(e_hid[:, e % 2, 0:2 * P], e_gate[:, 0:2 * P], ps[:, 0:2 * P], ALU.mult).then_inc(
                    *sg["dve_step"].inc())
                V.tensor_tensor(e_hid[0:96, e % 2, 2 * P:3 * P], e_gate[0:96, 2 * P:3 * P], ps[0:96, 2 * P:3 * P],
                                     ALU.mult).then_inc(*psum.drain("e3", e).inc())
            for b in range(B + 1):
                if b < B:
                    def get(k):
                        v.wait_ge(*sg[f"oe_gathered{b}"].nth(1, 16))
                        for h in range(2):
                            t = 2 * b + h
                            V.scalar_tensor_tensor(ln_r[:, k, h, :], og[:, t, :], Q1[3][:, t:t + 1], x_tok[:, t, :],
                                                   ALU.mult, ALU.add).then_inc(*sg["dve_step"].inc())
                    norm_stats(b, get, b % 3)
                if b:
                    norm_scale(b - 1, sg["final_ready"], (b - 1) % 3)

        @block.scalar
        def _(eng):
            act = Engine(eng)
            A = nc.scalar.activation

            def copy(dst, src, signal=None):
                return A(dst, src, ACT.Copy).then_inc(*(signal or sg["act_step"]).inc())

            def drain(dst, name, *use, cut=512, ring=psum):
                ps = ring.get(act, name, *use)
                src = ps[:, 0:cut]
                if len(dst.shape) == 3:
                    src = src.rearrange("p (a b) -> p a b", a=dst.shape[1])
                elif len(dst.shape) == 4:
                    src = src.rearrange("p (a b c) -> p a b c", a=dst.shape[1], b=dst.shape[2])
                return copy(dst, src, ring.drain(name, *use))

            act.wait_ge(*loaded("ld_ssm"))
            A(ssm_p[:, :, 7:23], ssm_p[:, :, 7:23], ACT.Exp).then_inc(*sg["a_exp"].inc())
            act.wait_ge(*sg["pads_clear"].nth(0))

            def ssm_front(b):
                if b:
                    act.wait_ge(*sg["conv_ready"].nth(2 * b - 1))
                drain(x_pad[:, :, DC - 1:], "xin", b)
                yield
                for et in range(2):
                    act.wait_ge(*sg["conv_ready"].nth(2 * b + et))
                    A(u[:, et, b, :], tmp_a[:, et, :], ACT.Silu).then_inc(*sg["u_ready"].inc())
                yield
                copy(bcd[:, b * S:(b + 1) * S], psum.get(act, "bc", b)[0:2 * DS + DR, 0:S], psum.drain("bc", b))
                yield
                if b:
                    act.wait_ge(*psum.empty("bc", b))
                    nc.scalar.dma_start(bc_rows(b), bcd[0:2 * DS, b * S:(b + 1) * S]).then_inc(
                        *sg[f"bc_stored{b}"].inc(16))
                ps = psum.get(act, "dp", b)
                for et in range(2):
                    A(tmp_a[:, et, :], ps[:, et * S:(et + 1) * S], ACT.Abs, bias=ssm_p[:, et, 5:6]).then_inc(
                        *sg["size_ready"].inc())
                act.wait_ge(*last())
                A(tmp_b, tmp_a, ACT.Exp, scale=-1.0).then_inc(*sg["softplus_t"].inc())
                yield
                yield
                act.wait_ge(*sg["softplus_w"].nth(b))
                A(du[:, :, b, :], tmp_a, ACT.Ln).then_inc(*sg["softplus_ln"].inc())
                yield
                if b == B - 1:
                    act.wait_ge(*psum.full("v0", NT - 1))
                    act.wait_ge(*sg["delta_ready"].nth(B - 1))
                    for i in range(B):
                        act.wait_ge(*sg[f"bc_stored{i}"].nth(0, 16))
                    for dst, name in ((w_qk1, "w_qk1"), (w_v1, "w_v1"), (w_o1, "w_o1")):
                        nc.scalar.dma_start(dst, a[name]).then_inc(*sg["ld_attn1"].inc(16))
                yield

            def attn0(b):
                for i in range(4):
                    for t in qkv0_steps[b][i]:
                        drain(qkv[:, t, 0:512], "qk0", t)
                        drain(qkv[:, t, 512:768], "v0", t, cut=256)
                    if i == 2:
                        act.wait_ge(*sg["s0_arg"].nth(b))
                        A(s0[:, :, :, 0:b + 1], s0[:, :, :, 0:b + 1], ACT.Exp,
                          scale=float(DH) ** -0.5).then_inc(*sg["s0_exp"].inc())
                    yield
                if b:
                    act.wait_ge(*psum.full("proj0", b - 1))
                drain(xx_feat[:, :, :], "o0t", b)
                for _ in range(4):
                    yield

            def ssm(b):
                act.wait_ge(*sg["a_ready"].nth(0))
                act.wait_ge(*sg["decay_clear"].nth(0))
                act.wait_ge(*sg["delta_ready"].nth(b))
                for n in range(DS + 2):
                    k = b * DS + n
                    if n < DS:
                        if k >= NB:
                            act.wait_ge(*sg["decay_used"].nth(k - NB))
                        for et in range(2):
                            A(decay[:, k % NB, et, 1:], delta[:, et, b, 1:], ACT.Exp,
                              scale=a_neg[:, et, n:n + 1]).then_inc(*sg["decay_ready"].inc())
                    yield
                if b:
                    act.wait_ge(*sg["y_ready"].nth(b - 1))
                act.wait_ge(*sg["x1_ready"].nth(2 * b + 1))
                A(silu_z[:, :, :], T2(x_tok, b), ACT.Silu).then_inc(*sg["silu_z_ready"].inc())
                for _ in range(5):
                    yield

            def moe0(b):
                drain(x_feat[:, :, :], "x2t", b)
                yield
                act.wait_ge(*sg["gate_arg"].nth(b))
                A(g8[:, 1, :, :], g8[:, 0, :, :], ACT.Exp).then_inc(*sg["gate_exp"].inc())
                ps = psum.get(act, "hid0", b)
                A(h_relu[:, :], ps[:, 0:S], ACT.Relu, bias=b_d[:, 0:1]).then_inc(*psum.drain("hid0", b).inc())
                for _ in range(STEPS["moe0"] - 1):
                    yield

            def attn1(b):
                act.wait_ge(*psum.full("hid0", b))
                drain(x_feat[:, :, :], "x3t", b)
                yield
                ps = psum.get(act, "v1", b)
                act.wait_ge(*sg["ones_ready"].nth(0))
                if b:
                    act.wait_ge(*psum.full("ov1", b - 1, 3))
                for h in range(2):
                    A(v_aug[:, h, :, 0:DH], ps[:, h * D:(h + 1) * D].rearrange("p (h d) -> p h d", h=HEADS),
                      ACT.Copy).then_inc(*(psum.drain("v1", b) if h else sg["act_step"]).inc())
                yield
                ps = psum.get(act, "q1t", b)
                A(q_feat, ps[:, :].rearrange("p (k s) -> p k s", k=KD), ACT.Copy,
                  scale=float(DH) ** -0.5).then_inc(*psum.drain("q1t", b).inc())
                drain(k_feat, "k1t", b)
                for _ in range(3):
                    yield
                for g in range(4 + 2):
                    if 1 <= g < 5:
                        c = g - 1
                        if c >= 2:
                            act.wait_ge(*psum.full("ov1", b, c - 2))
                        drain(p_t0[:, c % 2, :, 0:P], "pta", b, c)
                    if g < 4:
                        if g >= 2:
                            act.wait_ge(*psum.full("ptb", b, g - 2, 1))
                        act.wait_ge(*sg["max_ready"].nth(3 * (4 * b + g)))
                        ps = psum.get(act, "s1a", b, g)
                        for j in range(4):
                            ins = A(p_qk[:, g % 2, j, :], ps[:, j * P:(j + 1) * P], ACT.Exp,
                                    bias=neg_max[:, g % 2, j:j + 1])
                            ins.then_inc(*(psum.drain("s1a", b, g) if j == 3 else sg["act_step"]).inc())
                    yield
                    if 1 <= g < 5:
                        drain(p_t0[:, c % 2, :, P:S], "ptb", b, c, 0)
                        drain(p_t1[:, c % 2, :, :], "ptb", b, c, 1)
                    if g < 4:
                        for i in range(2):
                            act.wait_ge(*sg["max_ready"].nth(3 * (4 * b + g) + 1 + i))
                            ps = psum.get(act, "s1b", b, 2 * g + i)
                            for j in range(2):
                                k = 2 * i + j
                                A(p_qk[:, g % 2, 4 + 2 * k:6 + 2 * k, :].rearrange("p a b -> p (a b)"),
                                  ps[:, j * S:(j + 1) * S],
                                  ACT.Exp, bias=neg_max[:, g % 2, 4 + k:5 + k]).then_inc(
                                      *(psum.drain("s1b", b, 2 * g + i) if j else sg["act_step"]).inc())
                    if g >= 2:
                        drain(o_heads[:, g - 2, :], "ov1", b, g - 2, cut=S)
                    yield
                yield
                drain(o_feat, "o1t", b)
                yield
                yield
                yield

            def fold(_):
                for h in range(XH):
                    ps = x_psum.get(act, "fold", h)
                    copy(m_q[:, h, :, :].rearrange("p a b -> p (a b)"), ps[:, 0:D])
                    copy(m_o[:, h, :], ps[:, D:2 * D], x_psum.drain("fold", h))
                    if h % 2:
                        yield

            def xattn(b):
                drain(xx_feat[:, :, :], "x4t", b, ring=x_psum)
                yield
                for i in range(XH + 5):
                    if 4 <= i < XH + 4:
                        h = i - 4
                        if h >= 2:
                            act.wait_ge(*sg["ox_used"].nth(b * (XH - 1) + h - 2))
                        drain(ox_feat[:, h % 2, :], "pvx", b, h, cut=S, ring=x_psum)
                    yield
                    if i < XH:
                        if i >= 2:
                            act.wait_ge(*x_psum.full("sx", b, i - 2))
                        drain(qx_feat[:, i % 2, :], "qx", b, i, cut=S, ring=x_psum)
                    if 1 <= i < XH + 1:
                        h = i - 1
                        j = h % NX
                        act.wait_ge(*sg["smax_ready"].nth(b * XH + h))
                        for qt in range(2):
                            A(px[:, j, qt, :], px[:, j, qt, :], ACT.Exp, bias=x_nmax[:, j, qt:qt + 1],
                              accum_out=x_sum[:, j, qt:qt + 1]).then_inc(*sg["sexp_ready"].inc())
                    yield
                yield

            run_layers(ssm_front=ssm_front, attn0=attn0, ssm=ssm, moe0=moe0, attn1=attn1, fold=fold, xattn=xattn)

            def shared(hf, chunks):
                for c in chunks:
                    m = HC[c][1]
                    ps = x_psum.get(act, "sh1", hf, c)
                    if hf:
                        act.wait_ge(*psum.full("sh2", 0, 2))
                    A(hs[0:m, c, :], ps[0:m, :], ACT.Silu).then_inc(*x_psum.drain("sh1", hf, c).inc())

            def to_features(t):
                drain(x5_feat[:, :, t * P:(t + 2) * P], "x5t", t)

            for t in range(0, NT - 2, 2):
                to_features(t)
            act.wait_ge(*o_psum.empty("ox", B - 1))
            shared(0, (0,))
            to_features(NT - 2)
            act.wait_ge(*sg["route_arg"].nth(0))
            A(r8[:, 1, :, :], r8[:, 0, :, :], ACT.Exp).then_inc(*sg["route_exp"].inc())

            shared(0, (1, 2))
            shared(1, range(3))

            def expert_out(e):
                drain(oe[:, e, :], "e2", e, cut=D)

            for e in range(E):
                ps = psum.get(act, "e1", e)
                if e:
                    act.wait_ge(*psum.empty("e3", e - 1))
                A(e_gate[:, 0:2 * P], ps[:, 0:2 * P], ACT.Silu).then_inc(*sg["act_step"].inc())
                A(e_gate[0:96, 2 * P:3 * P], ps[0:96, 2 * P:3 * P], ACT.Silu).then_inc(*psum.drain("e1", e).inc())
                if e:
                    expert_out(e - 1)
            expert_out(E - 1)

        @block.gpsimd
        def _(eng):
            pool = Engine(eng)
            G = nc.gpsimd
            G.memset(x_pad[:, :, 0:DC - 1], 0.0).then_inc(*sg["pool_step"].inc())
            G.memset(half_neg[:, :], -0.5).then_inc(*sg["pool_step"].inc())
            G.memset(small[:, :], 0.0).then_inc(*sg["pads_clear"].inc())
            pool.wait_ge(*last())

            norms = [0]

            def root(k=0):
                i = norms[0]
                norms[0] += 1
                pool.wait_ge(*sg["var_ready"].nth(i))
                G.tensor_tensor(ln_rs[:, k, :], ln_var[:, k, :], half_neg[:, :], ALU.pow).then_inc(
                    *sg["rstd_ready"].inc())

            G.memset(decay[:, :, :, 0:1], 0.0).then_inc(*sg["decay_clear"].inc())

            def ssm_front(b):
                for _ in range(STEPS["ssm_front"] - 2):
                    yield
                pool.wait_ge(*sg["softplus_ready"].nth(b))
                G.tensor_tensor(du[:, :, b, :], delta[:, :, b, :], u[:, :, b, :], ALU.mult).then_inc(
                    *sg["delta_ready"].inc())
                yield
                yield

            def attn0(b):
                for _ in range(STEPS["attn0"] - 2):
                    yield
                root(1)
                yield
                yield

            def ssm(b):
                pool.wait_ge(*sg["delta_ready"].nth(b))
                for n in range(DS + 3):
                    k = b * DS + n
                    if n < DS and b:
                        pool.wait_ge(*bc_here(k))
                        if k >= NB:
                            pool.wait_ge(*sg["decay_used"].nth(k - NB))
                        G.tensor_tensor(drive[:, k % NB, :, :], du[:, :, b, :],
                                        bc_all[:, k % NBC, 0, :].unsqueeze(1).broadcast_to([P, 2, S]),
                                        ALU.mult).then_inc(*sg["drive_ready"].inc())
                    if n >= 3 and n % 2 and n < DS + 2:
                        j = k - 2
                        pool.wait_ge(*bc_here(j))
                        pool.wait_ge(*sg["decay_used"].nth(j))
                        G.tensor_tensor(state[:, j % NSTATE, :, :], state[:, j % NSTATE, :, :],
                                        bc_all[:, j % NBC, 1, :].unsqueeze(1).broadcast_to([P, 2, S]),
                                        ALU.mult).then_inc(*sg["seen_odd"].inc())
                    if n >= 4:
                        k -= 3
                        pool.wait_ge(*seen(k))
                        if n == 4:
                            pool.wait_ge(*seen(k - 1))
                        if b and n == 4:
                            pool.wait_ge(*psum.full("yt", b - 1))
                        if n > 4:
                            pool.wait_ge(*sg["y_added"].nth(b * (DS - 1) + n - 5))
                        G.tensor_tensor(y_sum[:, :, :],
                                        state[:, (k - 1) % NSTATE, :, :] if n == 4 else y_sum[:, :, :],
                                        state[:, k % NSTATE, :, :], ALU.add).then_inc(*sg["y_added"].inc())
                    yield
                yield
                yield
                root(2)
                yield
                yield

            def moe0(b):
                for _ in range(STEPS["moe0"] - 2):
                    yield
                root()
                yield
                yield

            def attn1(b):
                if not b:
                    pool.wait_ge(*psum.full("v0", NT - 1))
                    pool.wait_ge(*sg["delta_ready"].nth(B - 1))
                    for i in range(B):
                        pool.wait_ge(*sg[f"bc_stored{i}"].nth(0, 16))
                    G.memset(v_aug[:, :, :, DH:], 0.0).then_inc(*sg["pool_step"].inc())
                    pool.wait_ge(*last())
                    G.memset(v_aug[:, :, :, DH:DH + 1], 1.0).then_inc(*sg["ones_ready"].inc())
                for _ in range(STEPS["attn1"] - 2):
                    yield
                root()
                yield
                yield

            def fold(_):
                for _ in range(STEPS["fold"]):
                    yield

            def xattn(b):
                for _ in range(STEPS["xattn"] - 1):
                    yield
                root(1)
                yield

            run_layers(ssm_front=ssm_front, attn0=attn0, ssm=ssm, moe0=moe0, attn1=attn1, fold=fold, xattn=xattn)

            pool.wait_ge(*sg["slots_ready"].nth(0))
            pool.wait_ge(*sg["zeroed"].nth(0, 16))
            for t in range(NT):
                G.indirect_dma_start(
                    xd_dram, bass.IndirectOffsetOnAxis(ap=slot_u[:, 0, t:t + 1], axis=0),
                    x_tok[:, t, :], None).then_inc(
                        *sg["xd_scattered"].inc(16))
            pool.wait_ge(*sg["oe_stored"].nth(E - 1, 16))
            for t in range(NT):
                G.indirect_dma_start(
                    og[:, t, :], None, oe_dram,
                    bass.IndirectOffsetOnAxis(ap=slot_u[:, 1, t:t + 1], axis=0)).then_inc(
                        *sg[f"oe_gathered{t // 2}"].inc(16))
                if t >= 5 and t % 2:
                    root((t - 5) // 2 % 3)
            for b in range(2, B):
                root(b % 3)

        @block.sync
        def _(eng):
            sp = Engine(eng)

            def load(dst, src, name):
                eng.dma_start(dst, src).then_inc(*sg[name].inc(16))

            load(in_pt, a["in_pt"], "ld_ssm")
            load(ctx_t[:, :], a["ctx_t"], "ld_ssm")
            load(ssm_p[:, :, :], a["ssm_p"], "ld_ssm")
            load(x_pt, a["x_pt"], "ld_ssm")
            load(dt_pt, a["dt_pt"], "ld_ssm")
            load(x0_feat, a["x_t"], "ld_attn0")
            load(w_qkv, a["w_qkv"], "ld_attn0")
            load(w_o0, a["w_o0"], "ld_attn0")
            load(ident[:, :], a["ident"], "ld_const")
            load(ident_bf[:, :], a["ident_bf"], "ld_const")
            load(mask_qk[:, :], a["mask_qk"], "ld_const")
            load(eid_rev[:, :], a["eid_rev"], "ld_const")
            load(x_tok[:, :, :], a["x"], "ld_x")
            load(w_r[:, :, :], a["w_r"], "ld_moe0")
            load(b_r[:, :], a["b_r"].partition_broadcast(P), "ld_moe0")
            load(w_d[:, :, :], a["w_d"], "ld_moe0")
            load(b_d[:, :], a["b_d"], "ld_moe0")
            load(w_u[:, :], a["w_u"], "ld_moe0")
            load(b_u[:, :], a["b_u"], "ld_moe0")
            load(spread[:, :], a["spread"], "ld_moe0")
            load(m_q.rearrange("p h k d -> p h (k d)"), a["wx_q"], "ld_xattn")
            load(wx_k, a["wx_k"], "ld_xattn")
            load(wx_v, a["wx_v"], "ld_xattn")
            load(m_o, a["wx_o"], "ld_xattn")
            load(rope[:, :, :, :], a["rope"], "ld_rope")
            load(head_of[:, :], a["head_of"], "ld_rope")
            load(xd_dram[0:T, :], a["zeros"], "zeroed")
            sp.wait_ge(*psum.empty("bc", 0))
            load(bc_rows(0), bcd[0:2 * DS, 0:S], "bc_stored0")

            def load_bc(b):
                sp.wait_ge(*sg[f"bc_stored{b}"].nth(0, 16))
                for n in range(DS):
                    k = b * DS + n
                    if k >= NBC:
                        sp.wait_ge(*seen(k - NBC))
                    eng.dma_start(bc_all[:, k % NBC, :, :], bc_dram[:, n, b, :].partition_broadcast(P)).then_inc(
                        *bc_loaded[k % NBC].inc(16))

            load_bc(0)
            load_bc(1)
            sp.wait_ge(*sg["x1_ready"].nth(NT - 1))
            load(ctx_tok, a["ctx_tok"], "ld_ctx")
            load(mask_raw, a["mask"].partition_broadcast(P), "ld_mask")
            load_bc(2)
            load_bc(3)
            sp.wait_ge(*sg["x4_ready"].nth(2 * B - 1))
            load(w_g, a["w_g"], "ld_route")
            load(tri, a["tri"], "ld_route")
            load(ones, a["ones"], "ld_route")
            load(dump, a["dump"], "ld_route")
            load(ebase, a["ebase"], "ld_route")
            load(ws_1, a["ws_1"], "ld_shared")
            load(ws_3, a["ws_3"], "ld_shared")
            load(w_1, a["w_1"], "ld_w13")
            load(w_3, a["w_3"], "ld_w13")
            sp.wait_ge(*o_psum.empty("ox", B - 1))
            sp.wait_ge(*sg["x5_ready"].nth(2 * B - 1))
            load(ws_2, a["ws_2"], "ld_ws2")
            load(w_2, a["w_2"], "ld_w2")
            sp.wait_ge(*sg["xd_scattered"].nth(NT - 1, 16))
            load(xd_tok, xd_dram[0:T, :].rearrange("(e p) d -> p e d", p=P), "xd_loaded")
            for e in range(E):
                sp.wait_ge(*psum.empty("e2", e))
                load(oe_dram[e * P:(e + 1) * P, :], oe[:, e, :], "oe_stored")
            for t in range(NT):
                sp.wait_ge(*sg["final_ready"].nth(t))
                load(out[t * P:(t + 1) * P, :], x_tok[:, t, :], "out_stored")
            sp.wait_ge(*sg["out_stored"].nth(NT - 1, 16))
            assert all(sg[n].n == 16 * k for n, k in loads.items())


_SHAPE_CONSTANTS = ("ident", "ident_bf", "mask_qk", "eid_rev", "spread", "rope", "head_of",
                    "tri", "ones", "dump", "ebase", "zeros")


def shape_constants():
    bf = mybir.dt.np(BF16)
    i = np.arange(P)
    c = {"ident": np.eye(P, dtype=np.float32), "ident_bf": np.eye(P).astype(bf)}
    c["mask_qk"] = np.where(i[None, :] > i[:, None], NEG, 0.0).astype(bf)
    c["eid_rev"] = np.tile(np.arange(E, 0, -1, dtype=np.float32), (P, 1))
    c["spread"] = (np.arange(P)[None, :] // R == np.arange(E)[:, None]).astype(np.float32)
    freq = (1.0 / 10000.0 ** (np.arange(0, DH, 2, dtype=np.float32) / DH)).astype(np.float32)
    ang = np.outer(np.arange(S, dtype=np.float32), freq).astype(np.float32)
    r = np.stack([np.cos(ang), -np.sin(ang), np.sin(ang)], 1).astype(np.float32)
    c["rope"] = np.ascontiguousarray(r.reshape(2, P, 3, 8).transpose(1, 0, 2, 3))
    c["head_of"] = (i[:, None] // DH == np.arange(8)[None, :]).astype(np.float32)
    c["tri"] = (i[:, None] <= i[None, :]).astype(bf)
    c["ones"] = np.ones((P, P)).astype(bf)
    c["dump"] = (T + np.arange(NT)[None, :] * P + i[:, None]).astype(np.float32)
    c["ebase"] = np.tile(np.arange(E, dtype=np.float32) * CAP - 1, (P, 1))
    c["zeros"] = np.zeros((T, D), np.float32)
    return c


def kernel(**inputs):
    import concourse.bacc as bacc
    from concourse.bass_utils import run_bass_kernel_spmd as run

    w = {k: np.asarray(x) for k, x in inputs.items()}

    def tiles(m, p=P):
        return m.reshape(m.shape[0] // p, p, *m.shape[1:]).swapaxes(0, 1)

    def hid_rows(m):
        pad = np.zeros((*m.shape[:-2], 3 * P - HID, m.shape[-1]), m.dtype)
        m = np.concatenate([m, pad], -2)
        m = m.reshape(*m.shape[:-2], 3, P, m.shape[-1])
        return np.moveaxis(m, -2, 0)

    xp = w["L0_xattn_x_proj_w"]
    x = w["x"].reshape(T, D)
    arrays = dict(
        x=tiles(x), x_t=tiles(x.T), ctx_t=w["ctx_1024"].reshape(T, CTX).T,
        mask=w["mask_BxS2_bf1"].reshape(T).view(np.uint8),
        w_qkv=tiles(w["L0_attn_weight_qkv"].T), w_o0=tiles(w["L0_attn_weight_out"].T),
        in_pt=w["L0_xattn_in_proj_w"].T,
        x_pt=tiles(np.concatenate([xp[DR:], xp[:DR]], 0).T),
        dt_pt=w["L0_xattn_dt_proj_w"].T,
        ssm_p=tiles(np.concatenate([w["L0_xattn_conv_w"], w["L0_xattn_conv_b"][:, None],
                                    w["L0_xattn_dt_proj_b"][:, None], w["L0_xattn_D"][:, None],
                                    w["L0_xattn_A_log"]], 1)),
        w_r=tiles(w["L0_ffn_Wr"]), b_r=w["L0_ffn_br"],
        w_d=tiles(w["L0_ffn_Wd"].transpose(1, 0, 2).reshape(D, E * R)),
        b_d=w["L0_ffn_bd"].reshape(P, 1), w_u=w["L0_ffn_Wu"].reshape(E * R, D), b_u=w["L0_ffn_bu"],
        w_qk1=tiles(np.concatenate([w["L1_attn_Wq"].T, w["L1_attn_Wk"].T], 1)),
        w_v1=tiles(w["L1_attn_Wv"].T), w_o1=tiles(w["L1_attn_Wo"].T),
        ctx_tok=tiles(w["ctx_1024"].reshape(T, CTX)),
        wx_q=tiles(w["L1_xattn_Wq"].T), wx_k=tiles(w["L1_xattn_Wk"].T), wx_v=tiles(w["L1_xattn_Wv"].T),
        wx_o=tiles(w["L1_xattn_Wo"]),
        w_g=tiles(w["L1_ffn_Wg"]),
        w_1=w["L1_ffn_W1"].reshape(E, KD, P, HID).transpose(2, 0, 1, 3),
        w_3=w["L1_ffn_W3"].reshape(E, KD, P, HID).transpose(2, 0, 1, 3),
        w_2=hid_rows(w["L1_ffn_W2"]), ws_1=tiles(w["L1_ffn_sw1"]), ws_3=tiles(w["L1_ffn_sw3"]),
        ws_2=hid_rows(w["L1_ffn_sw2"]),
    )
    arrays.update(shape_constants())
    arrays = {f"in_{k}": np.ascontiguousarray(v) for k, v in arrays.items()}
    nc = bacc.Bacc("TRN2", target_bir_lowering=False, num_devices=1)
    aps = {k[3:]: nc.dram_tensor(k, v.shape, mybir.dt.from_np(v.dtype), kind="ExternalInput").ap()
           for k, v in arrays.items()}
    out = nc.dram_tensor("out", (T, D), F32, kind="ExternalOutput").ap()
    decoder(nc, aps, out)
    r = run(nc, [arrays], core_ids=[0])
    return r.results[0]["out"].reshape(B, S, D)
```
